# Optimizing a Trainium2 kernel written in Bass

```python
import numpy as np
import jax
import jax.numpy as jnp

def _softmax(x, axis=-1):
    return jax.nn.softmax(x, axis=axis)

def _gelu(x):
    return jax.nn.gelu(x, approximate=True)

def _silu(x):
    return jax.nn.silu(x)

def _sigmoid(x):
    return jax.nn.sigmoid(x)

def _layernorm(x, axis=-1, eps=1e-05):
    m = jnp.mean(x, axis=axis, keepdims=True)
    v = jnp.var(x, axis=axis, keepdims=True)
    return (x - m) / jnp.sqrt(v + eps)

def _scatter_add(tgt, idx, src, axis=0):
    return tgt.at[idx].add(src)

def _segment_sum(src, seg, n):
    return jax.ops.segment_sum(src, seg, n)
kernel_name = 'mk_prb_d2_jaxref_r4_60d1b3'

def setup_inputs(seed: int=0):
    np.random.seed(seed)
    _w = jnp.asarray

    def _L0_attn_setup():
        import jax, jax.numpy as jnp
        import numpy as np
        import math
        E, N, K, R = (256, 16, 4, 64)
        B, L = (2, 512)
        key = jax.random.key(seed)
        ks = jax.random.split(key, 8)
        gn = lambda k, sh, sc: jax.random.normal(k, sh, dtype=jnp.float32) * sc
        W_z = gn(ks[0], (E, E), E ** (-0.5))
        W_params = gn(ks[1], (R + 2 * N, E), E ** (-0.5))
        conv_w = gn(ks[2], (E, 1, K), 0.5)
        dt_std = R ** (-0.5) * 0.1
        W_dt = jax.random.uniform(ks[3], (E, R), jnp.float32, -dt_std, dt_std)
        b_dt = jnp.full((E,), math.log(math.expm1(0.001)), dtype=jnp.float32)
        A_log = jnp.tile(jnp.log(jnp.arange(1, N + 1, dtype=jnp.float32))[None, :], (E, 1))
        D = jnp.ones((E,), dtype=jnp.float32)
        W_out = gn(ks[4], (E, E), E ** (-0.5))
        x = jax.random.normal(ks[5], (B, L, E), dtype=jnp.float32)
        return dict(x=x, W_z=W_z, W_params=W_params, conv_w=conv_w, W_dt=W_dt, b_dt=b_dt, A_log=A_log, D=D, W_out=W_out)
    _L0_attn_in = _L0_attn_setup()

    def _L0_ffn_setup():
        import jax, jax.numpy as jnp
        import numpy as np
        DM, NE, ES, ESZ = (256, 16, 4, 64)
        BATCH, SEQ = (8, 512)
        key = jax.random.key(seed)
        k = jax.random.split(key, 5)
        scale = 0.02
        return {'x': jax.random.normal(k[0], (BATCH, SEQ, DM), dtype=jnp.float32), 'controller': jax.random.normal(k[1], (DM, NE, ES), dtype=jnp.float32) * scale, 'f1': jax.random.normal(k[2], (DM, NE, ES, ESZ), dtype=jnp.float32) * scale, 'f2': jax.random.normal(k[3], (NE, ES, ESZ, DM), dtype=jnp.float32) * scale, 'bias': jax.random.normal(k[4], (NE, ES, ESZ), dtype=jnp.float32) * scale}
    _L0_ffn_in = _L0_ffn_setup()

    def _L1_attn_setup():
        import jax, jax.numpy as jnp
        import numpy as np
        from jax import lax
        B, L, D_MODEL = (2, 512, 256)
        EXPAND = 2
        D_INNER = D_MODEL * EXPAND
        D_STATE = 16
        D_CONV = 4
        DT_RANK = (D_MODEL + 15) // 16
        EPS = 1e-05

        def _mamba_params(key, pfx, scale=0.02):
            ks = jax.random.split(key, 6)
            return {pfx + '_Win': jax.random.normal(ks[0], (D_MODEL, 2 * D_INNER), jnp.float32) * scale, pfx + '_convw': jax.random.normal(ks[1], (D_INNER, D_CONV), jnp.float32) * scale, pfx + '_convb': jnp.zeros((D_INNER,), jnp.float32), pfx + '_Wx': jax.random.normal(ks[2], (D_INNER, DT_RANK + 2 * D_STATE), jnp.float32) * scale, pfx + '_Wdt': jax.random.normal(ks[3], (DT_RANK, D_INNER), jnp.float32) * scale, pfx + '_bdt': jax.random.uniform(ks[4], (D_INNER,), jnp.float32, -4.0, -2.0), pfx + '_Alog': jnp.log(jnp.broadcast_to(jnp.arange(1, D_STATE + 1, dtype=jnp.float32), (D_INNER, D_STATE))).copy(), pfx + '_D': jnp.ones((D_INNER,), jnp.float32), pfx + '_Wout': jax.random.normal(ks[5], (D_INNER, D_MODEL), jnp.float32) * scale}

        def _layernorm(x, w, b):
            mu = x.mean(-1, keepdims=True)
            xc = x - mu
            v = (xc * xc).mean(-1, keepdims=True)
            return xc * lax.rsqrt(v + EPS) * w + b

        def _causal_dwconv(x, w, b):
            xc = x.transpose(0, 2, 1)
            out = lax.conv_general_dilated(xc, w[:, None, :], window_strides=(1,), padding=[(D_CONV - 1, 0)], feature_group_count=D_INNER, dimension_numbers=('NCH', 'OIH', 'NCH'))
            return (out + b[None, :, None]).transpose(0, 2, 1)

        def _selective_scan(u, dt, A, Bm, Cm, Dp):
            h0 = jnp.zeros((u.shape[0], D_INNER, D_STATE), u.dtype)

            def step(h, inp):
                u_t, dt_t, B_t, C_t = inp
                dA = jnp.exp(dt_t[:, :, None] * A)
                h = dA * h + (dt_t * u_t)[:, :, None] * B_t[:, None, :]
                y = jnp.einsum('bds,bs->bd', h, C_t)
                return (h, y)
            _, ys = lax.scan(step, h0, (u.transpose(1, 0, 2), dt.transpose(1, 0, 2), Bm.transpose(1, 0, 2), Cm.transpose(1, 0, 2)))
            return ys.transpose(1, 0, 2) + u * Dp

        def _mamba(x, Win, convw, convb, Wx, Wdt, bdt, Alog, Dp, Wout):
            xz = x @ Win
            xi, z = jnp.split(xz, 2, axis=-1)
            xi = jax.nn.silu(_causal_dwconv(xi, convw, convb))
            xdbc = xi @ Wx
            dt_in = xdbc[..., :DT_RANK]
            Bm = xdbc[..., DT_RANK:DT_RANK + D_STATE]
            Cm = xdbc[..., DT_RANK + D_STATE:]
            dt = jax.nn.softplus(dt_in @ Wdt + bdt)
            A = -jnp.exp(Alog)
            y = _selective_scan(xi, dt, A, Bm, Cm, Dp)
            return y * jax.nn.silu(z) @ Wout
        key = jax.random.key(seed)
        k = jax.random.split(key, 6)
        inp = {'x': jax.random.normal(k[0], (B, L, D_MODEL), jnp.float32)}
        inp.update(_mamba_params(k[1], 'fw'))
        inp.update(_mamba_params(k[2], 'bw'))
        inp.update({'fwn_w': jnp.ones((D_MODEL,), jnp.float32), 'fwn_b': jnp.zeros((D_MODEL,), jnp.float32), 'fin_w': jnp.ones((D_MODEL,), jnp.float32), 'fin_b': jnp.zeros((D_MODEL,), jnp.float32), 'ff_W1': jax.random.normal(k[3], (D_MODEL, D_MODEL * EXPAND), jnp.float32) * 0.02, 'ff_b1': jnp.zeros((D_MODEL * EXPAND,), jnp.float32), 'ff_W2': jax.random.normal(k[4], (D_MODEL * EXPAND, D_MODEL), jnp.float32) * 0.02, 'ff_b2': jnp.zeros((D_MODEL,), jnp.float32)})
        return inp
    _L1_attn_in = _L1_attn_setup()

    def _L1_ffn_setup():
        import jax, jax.numpy as jnp
        import numpy as np
        D_MODEL = 256
        EXPANSION = 4
        D_HIDDEN = D_MODEL * EXPANSION
        NUM_STAGES = int(np.log2(D_HIDDEN))

        def butterfly(y, weights, dim):
            lead = y.shape[:-1]
            for stage in range(weights.shape[0]):
                s = 2 ** stage
                nb = dim // (2 * s)
                yr = y.reshape(*lead, nb, 2, s)
                a = yr[..., 0, :]
                b = yr[..., 1, :]
                w = weights[stage].reshape(nb, s, 2, 2)
                na = w[..., 0, 0] * a + w[..., 0, 1] * b
                nb2 = w[..., 1, 0] * a + w[..., 1, 1] * b
                y = jnp.stack([na, nb2], axis=-2).reshape(*lead, dim)
            return y
        key = jax.random.key(seed)
        ks = jax.random.split(key, 6)
        B, S = (4, 512)
        x = jax.random.normal(ks[0], (B, S, D_MODEL), jnp.float32)
        W_exp = jax.random.normal(ks[1], (D_MODEL, D_HIDDEN), jnp.float32) * 0.02
        b_exp = jnp.zeros((D_HIDDEN,), jnp.float32)
        up_weights = jax.random.normal(ks[2], (NUM_STAGES, D_HIDDEN // 2, 2, 2), jnp.float32) * 0.02
        up_bias = jnp.zeros((D_HIDDEN,), jnp.float32)
        down_weights = jax.random.normal(ks[3], (NUM_STAGES, D_HIDDEN // 2, 2, 2), jnp.float32) * 0.02
        W_con = jax.random.normal(ks[4], (D_HIDDEN, D_MODEL), jnp.float32) * 0.02
        b_con = jnp.zeros((D_MODEL,), jnp.float32)
        down_bias = jnp.zeros((D_MODEL,), jnp.float32)
        return dict(x=x, W_exp=W_exp, b_exp=b_exp, up_weights=up_weights, up_bias=up_bias, down_weights=down_weights, W_con=W_con, b_con=b_con, down_bias=down_bias)
    _L1_ffn_in = _L1_ffn_setup()
    _d = {'L0_attn_x': _L0_attn_in['x'], 'L0_attn_W_z': _L0_attn_in['W_z'], 'L0_attn_W_params': _L0_attn_in['W_params'], 'L0_attn_conv_w': _L0_attn_in['conv_w'], 'L0_attn_W_dt': _L0_attn_in['W_dt'], 'L0_attn_b_dt': _L0_attn_in['b_dt'], 'L0_attn_A_log': _L0_attn_in['A_log'], 'L0_attn_D': _L0_attn_in['D'], 'L0_attn_W_out': _L0_attn_in['W_out'], 'L0_ffn_controller': _L0_ffn_in['controller'], 'L0_ffn_f1': _L0_ffn_in['f1'], 'L0_ffn_f2': _L0_ffn_in['f2'], 'L0_ffn_bias': _L0_ffn_in['bias'], 'L1_attn_fw_Win': _L1_attn_in['fw_Win'], 'L1_attn_fw_convw': _L1_attn_in['fw_convw'], 'L1_attn_fw_convb': _L1_attn_in['fw_convb'], 'L1_attn_fw_Wx': _L1_attn_in['fw_Wx'], 'L1_attn_fw_Wdt': _L1_attn_in['fw_Wdt'], 'L1_attn_fw_bdt': _L1_attn_in['fw_bdt'], 'L1_attn_fw_Alog': _L1_attn_in['fw_Alog'], 'L1_attn_fw_D': _L1_attn_in['fw_D'], 'L1_attn_fw_Wout': _L1_attn_in['fw_Wout'], 'L1_attn_bw_Win': _L1_attn_in['bw_Win'], 'L1_attn_bw_convw': _L1_attn_in['bw_convw'], 'L1_attn_bw_convb': _L1_attn_in['bw_convb'], 'L1_attn_bw_Wx': _L1_attn_in['bw_Wx'], 'L1_attn_bw_Wdt': _L1_attn_in['bw_Wdt'], 'L1_attn_bw_bdt': _L1_attn_in['bw_bdt'], 'L1_attn_bw_Alog': _L1_attn_in['bw_Alog'], 'L1_attn_bw_D': _L1_attn_in['bw_D'], 'L1_attn_bw_Wout': _L1_attn_in['bw_Wout'], 'L1_attn_fwn_w': _L1_attn_in['fwn_w'], 'L1_attn_fwn_b': _L1_attn_in['fwn_b'], 'L1_attn_fin_w': _L1_attn_in['fin_w'], 'L1_attn_fin_b': _L1_attn_in['fin_b'], 'L1_attn_ff_W1': _L1_attn_in['ff_W1'], 'L1_attn_ff_b1': _L1_attn_in['ff_b1'], 'L1_attn_ff_W2': _L1_attn_in['ff_W2'], 'L1_attn_ff_b2': _L1_attn_in['ff_b2'], 'L1_ffn_W_exp': _L1_ffn_in['W_exp'], 'L1_ffn_b_exp': _L1_ffn_in['b_exp'], 'L1_ffn_up_weights': _L1_ffn_in['up_weights'], 'L1_ffn_up_bias': _L1_ffn_in['up_bias'], 'L1_ffn_down_weights': _L1_ffn_in['down_weights'], 'L1_ffn_W_con': _L1_ffn_in['W_con'], 'L1_ffn_b_con': _L1_ffn_in['b_con'], 'L1_ffn_down_bias': _L1_ffn_in['down_bias']}
    _x0 = _d['L0_attn_x']
    _d['L0_attn_x'] = jax.random.normal(jax.random.fold_in(jax.random.key(seed), 1), (2, 2048, 256), dtype=_x0.dtype)
    del _x0
    return _d

def reference(L0_attn_x, L0_attn_W_z, L0_attn_W_params, L0_attn_conv_w, L0_attn_W_dt, L0_attn_b_dt, L0_attn_A_log, L0_attn_D, L0_attn_W_out, L0_ffn_controller, L0_ffn_f1, L0_ffn_f2, L0_ffn_bias, L1_attn_fw_Win, L1_attn_fw_convw, L1_attn_fw_convb, L1_attn_fw_Wx, L1_attn_fw_Wdt, L1_attn_fw_bdt, L1_attn_fw_Alog, L1_attn_fw_D, L1_attn_fw_Wout, L1_attn_bw_Win, L1_attn_bw_convw, L1_attn_bw_convb, L1_attn_bw_Wx, L1_attn_bw_Wdt, L1_attn_bw_bdt, L1_attn_bw_Alog, L1_attn_bw_D, L1_attn_bw_Wout, L1_attn_fwn_w, L1_attn_fwn_b, L1_attn_fin_w, L1_attn_fin_b, L1_attn_ff_W1, L1_attn_ff_b1, L1_attn_ff_W2, L1_attn_ff_b2, L1_ffn_W_exp, L1_ffn_b_exp, L1_ffn_up_weights, L1_ffn_up_bias, L1_ffn_down_weights, L1_ffn_W_con, L1_ffn_b_con, L1_ffn_down_bias):

    def _L0_attn_ref(x, W_z, W_params, conv_w, W_dt, b_dt, A_log, D, W_out):
        import jax, jax.numpy as jnp
        import numpy as np
        import math
        E, N, K, R = (256, 16, 4, 64)
        B, L = (2, 512)
        b, l, e = x.shape
        n = A_log.shape[1]
        r = W_dt.shape[1]
        k = conv_w.shape[-1]
        z = x @ W_z.T
        params = x @ W_params.T
        dt_unproj = params[..., :r]
        C_proj = params[..., r + n:]
        dt = jax.nn.softplus(dt_unproj @ W_dt.T + b_dt)
        xc = jax.lax.conv_general_dilated(x.transpose(0, 2, 1), conv_w, (1,), [(k - 1, 0)], dimension_numbers=('NCH', 'OIH', 'NCH'), feature_group_count=e)
        u = jax.nn.silu(xc.transpose(0, 2, 1))
        A = -jnp.exp(A_log)
        A_tilde = jnp.exp(dt[..., None] * A[None, None])
        B_tilde = jnp.where(jnp.abs(A)[None, None] < 1e-05, dt[..., None], (A_tilde - 1.0) / (A[None, None] + 1e-10))
        h0 = B_tilde[:, 0] * u[:, 0, :, None]

        def step(h, inp):
            a, bt, uu = inp
            h_new = a * h + bt * uu[..., None]
            return (h_new, h_new)
        xs = (A_tilde[:, :-1].transpose(1, 0, 2, 3), B_tilde[:, :-1].transpose(1, 0, 2, 3), u[:, :-1].transpose(1, 0, 2))
        _, hs = jax.lax.scan(step, h0, xs)
        h = jnp.concatenate([h0[None], hs], axis=0).transpose(1, 0, 2, 3)
        y = jnp.einsum('bln,blen->ble', C_proj, h)
        y_ssm = y + u * D
        y_gated = y_ssm * jax.nn.silu(z)
        return y_gated @ W_out.T

    def _L0_ffn_ref(x, controller, f1, f2, bias):
        import jax, jax.numpy as jnp
        import numpy as np
        DM, NE, ES, ESZ = (256, 16, 4, 64)
        BATCH, SEQ = (8, 512)
        ne = controller.shape[1]
        d = x.shape[-1]
        grouped = x.reshape(x.shape[:-2] + (-1, ne, d))
        logits = jnp.einsum('...btd,des->...btes', grouped, controller)
        tie = jnp.linspace(0.0, 1e-06, ne, dtype=logits.dtype).reshape(ne, 1, 1)
        logits = logits + tie
        perm = (logits == jnp.max(logits, axis=-3, keepdims=True)).astype(x.dtype)
        sel = jnp.einsum('...btd,...btes->...besd', grouped, perm)
        inner = jax.nn.relu(jnp.einsum('...besd,desf->...besf', sel, f1) + bias)
        inter = jnp.einsum('...besf,esfd->...besd', inner, f2)
        out = jnp.einsum('...besd,...btes->...btd', inter, perm)
        return out.reshape(x.shape)

    def _L1_attn_ref(x, fw_Win, fw_convw, fw_convb, fw_Wx, fw_Wdt, fw_bdt, fw_Alog, fw_D, fw_Wout, bw_Win, bw_convw, bw_convb, bw_Wx, bw_Wdt, bw_bdt, bw_Alog, bw_D, bw_Wout, fwn_w, fwn_b, fin_w, fin_b, ff_W1, ff_b1, ff_W2, ff_b2):
        import jax, jax.numpy as jnp
        import numpy as np
        from jax import lax
        B, L, D_MODEL = (2, 512, 256)
        EXPAND = 2
        D_INNER = D_MODEL * EXPAND
        D_STATE = 16
        D_CONV = 4
        DT_RANK = (D_MODEL + 15) // 16
        EPS = 1e-05

        def _mamba_params(key, pfx, scale=0.02):
            ks = jax.random.split(key, 6)
            return {pfx + '_Win': jax.random.normal(ks[0], (D_MODEL, 2 * D_INNER), jnp.float32) * scale, pfx + '_convw': jax.random.normal(ks[1], (D_INNER, D_CONV), jnp.float32) * scale, pfx + '_convb': jnp.zeros((D_INNER,), jnp.float32), pfx + '_Wx': jax.random.normal(ks[2], (D_INNER, DT_RANK + 2 * D_STATE), jnp.float32) * scale, pfx + '_Wdt': jax.random.normal(ks[3], (DT_RANK, D_INNER), jnp.float32) * scale, pfx + '_bdt': jax.random.uniform(ks[4], (D_INNER,), jnp.float32, -4.0, -2.0), pfx + '_Alog': jnp.log(jnp.broadcast_to(jnp.arange(1, D_STATE + 1, dtype=jnp.float32), (D_INNER, D_STATE))).copy(), pfx + '_D': jnp.ones((D_INNER,), jnp.float32), pfx + '_Wout': jax.random.normal(ks[5], (D_INNER, D_MODEL), jnp.float32) * scale}

        def _layernorm(x, w, b):
            mu = x.mean(-1, keepdims=True)
            xc = x - mu
            v = (xc * xc).mean(-1, keepdims=True)
            return xc * lax.rsqrt(v + EPS) * w + b

        def _causal_dwconv(x, w, b):
            xc = x.transpose(0, 2, 1)
            out = lax.conv_general_dilated(xc, w[:, None, :], window_strides=(1,), padding=[(D_CONV - 1, 0)], feature_group_count=D_INNER, dimension_numbers=('NCH', 'OIH', 'NCH'))
            return (out + b[None, :, None]).transpose(0, 2, 1)

        def _selective_scan(u, dt, A, Bm, Cm, Dp):
            h0 = jnp.zeros((u.shape[0], D_INNER, D_STATE), u.dtype)

            def step(h, inp):
                u_t, dt_t, B_t, C_t = inp
                dA = jnp.exp(dt_t[:, :, None] * A)
                h = dA * h + (dt_t * u_t)[:, :, None] * B_t[:, None, :]
                y = jnp.einsum('bds,bs->bd', h, C_t)
                return (h, y)
            _, ys = lax.scan(step, h0, (u.transpose(1, 0, 2), dt.transpose(1, 0, 2), Bm.transpose(1, 0, 2), Cm.transpose(1, 0, 2)))
            return ys.transpose(1, 0, 2) + u * Dp

        def _mamba(x, Win, convw, convb, Wx, Wdt, bdt, Alog, Dp, Wout):
            xz = x @ Win
            xi, z = jnp.split(xz, 2, axis=-1)
            xi = jax.nn.silu(_causal_dwconv(xi, convw, convb))
            xdbc = xi @ Wx
            dt_in = xdbc[..., :DT_RANK]
            Bm = xdbc[..., DT_RANK:DT_RANK + D_STATE]
            Cm = xdbc[..., DT_RANK + D_STATE:]
            dt = jax.nn.softplus(dt_in @ Wdt + bdt)
            A = -jnp.exp(Alog)
            y = _selective_scan(xi, dt, A, Bm, Cm, Dp)
            return y * jax.nn.silu(z) @ Wout
        yf = _mamba(x, fw_Win, fw_convw, fw_convb, fw_Wx, fw_Wdt, fw_bdt, fw_Alog, fw_D, fw_Wout)
        yf = _layernorm(yf + x, fwn_w, fwn_b)
        yb = _mamba(jnp.flip(x, 1), bw_Win, bw_convw, bw_convb, bw_Wx, bw_Wdt, bw_bdt, bw_Alog, bw_D, bw_Wout)
        yb = _layernorm(jnp.flip(yb, 1) + x, fwn_w, fwn_b)
        y = yf + yb
        ff = jax.nn.relu(y @ ff_W1 + ff_b1) @ ff_W2 + ff_b2
        return _layernorm(ff + y, fin_w, fin_b)

    def _L1_ffn_ref(x, W_exp, b_exp, up_weights, up_bias, down_weights, W_con, b_con, down_bias):
        import jax, jax.numpy as jnp
        import numpy as np
        D_MODEL = 256
        EXPANSION = 4
        D_HIDDEN = D_MODEL * EXPANSION
        NUM_STAGES = int(np.log2(D_HIDDEN))

        def butterfly(y, weights, dim):
            lead = y.shape[:-1]
            for stage in range(weights.shape[0]):
                s = 2 ** stage
                nb = dim // (2 * s)
                yr = y.reshape(*lead, nb, 2, s)
                a = yr[..., 0, :]
                b = yr[..., 1, :]
                w = weights[stage].reshape(nb, s, 2, 2)
                na = w[..., 0, 0] * a + w[..., 0, 1] * b
                nb2 = w[..., 1, 0] * a + w[..., 1, 1] * b
                y = jnp.stack([na, nb2], axis=-2).reshape(*lead, dim)
            return y
        h = jnp.einsum('bsd,dh->bsh', x, W_exp) + b_exp
        h = butterfly(h, up_weights, D_HIDDEN)
        h = jax.nn.gelu(h + up_bias, approximate=False)
        h = butterfly(h, down_weights, D_HIDDEN)
        y = jnp.einsum('bsh,hd->bsd', h, W_con) + b_con
        return y + down_bias
    x = L0_attn_x
    xn = _layernorm(x, axis=-1)
    x = x + _L0_attn_ref(xn, L0_attn_W_z, L0_attn_W_params, L0_attn_conv_w, L0_attn_W_dt, L0_attn_b_dt, L0_attn_A_log, L0_attn_D, L0_attn_W_out) + _L0_ffn_ref(xn, L0_ffn_controller, L0_ffn_f1, L0_ffn_f2, L0_ffn_bias)
    xn = _layernorm(x, axis=-1)
    x = x + _L1_attn_ref(xn, L1_attn_fw_Win, L1_attn_fw_convw, L1_attn_fw_convb, L1_attn_fw_Wx, L1_attn_fw_Wdt, L1_attn_fw_bdt, L1_attn_fw_Alog, L1_attn_fw_D, L1_attn_fw_Wout, L1_attn_bw_Win, L1_attn_bw_convw, L1_attn_bw_convb, L1_attn_bw_Wx, L1_attn_bw_Wdt, L1_attn_bw_bdt, L1_attn_bw_Alog, L1_attn_bw_D, L1_attn_bw_Wout, L1_attn_fwn_w, L1_attn_fwn_b, L1_attn_fin_w, L1_attn_fin_b, L1_attn_ff_W1, L1_attn_ff_b1, L1_attn_ff_W2, L1_attn_ff_b2) + _L1_ffn_ref(xn, L1_ffn_W_exp, L1_ffn_b_exp, L1_ffn_up_weights, L1_ffn_up_bias, L1_ffn_down_weights, L1_ffn_W_con, L1_ffn_b_con, L1_ffn_down_bias)
    return x

_drawn_inputs = setup_inputs


def setup_inputs(seed=0):
    import zlib

    import numpy as np

    out = dict(_drawn_inputs(seed))
    spreads = {'L0_attn_b_dt': (-6.907255172729492, 0.2),
     'L0_attn_D': (1.0, 0.2),
     'L1_attn_fw_convb': (0.0, 0.8),
     'L1_attn_fw_D': (1.0, 0.6),
     'L1_attn_bw_convb': (0.0, 0.8),
     'L1_attn_bw_D': (1.0, 0.6),
     'L1_attn_fwn_w': (1.0, 0.2),
     'L1_attn_fwn_b': (0.0, 0.1),
     'L1_attn_fin_w': (1.0, 0.2),
     'L1_attn_fin_b': (0.0, 0.1),
     'L1_attn_ff_b1': (0.0, 0.8),
     'L1_attn_ff_b2': (0.0, 0.315),
     'L1_ffn_b_exp': (0.0, 0.1),
     'L1_ffn_up_bias': (0.0, 0.1),
     'L1_ffn_b_con': (0.0, 0.1),
     'L1_ffn_down_bias': (0.0, 0.1)}
    factors = {'L0_attn_W_dt': 8.0,
     'L0_ffn_bias': 8.0,
     'L1_attn_fw_Win': 8.0,
     'L1_attn_fw_convw': 8.0,
     'L1_attn_fw_Wx': 8.0,
     'L1_attn_fw_Wdt': 8.0,
     'L1_attn_fw_bdt': 8.0,
     'L1_attn_fw_Alog': 8.0,
     'L1_attn_fw_Wout': 8.0,
     'L1_attn_bw_Win': 8.0,
     'L1_attn_bw_convw': 8.0,
     'L1_attn_bw_Wx': 8.0,
     'L1_attn_bw_Wdt': 8.0,
     'L1_attn_bw_bdt': 8.0,
     'L1_attn_bw_Alog': 8.0,
     'L1_attn_bw_Wout': 8.0}
    for name, (base, spread) in spreads.items():
        noise = np.random.default_rng([zlib.crc32(name.encode()), seed]).standard_normal(out[name].shape)
        drawn = base * np.exp(spread * noise) if base else spread * noise
        out[name] = jnp.asarray(drawn.astype(out[name].dtype))
    for name, factor in factors.items():
        out[name] = (out[name] * factor).astype(out[name].dtype)
    return out
```

```python
from contextlib import ExitStack

import concourse.bass as bass
from concourse import mybir

ALU = mybir.AluOpType
ACT = mybir.ActivationFunctionType
F32 = mybir.dt.float32
BF16 = mybir.dt.bfloat16
AX = mybir.AxisListType

P = 128
E = 256
C = E // P
B = 2
L = 2048
T = B * L
TT = 512
TC = 1024
NS = 16
KC = 4
PAD = KC - 1
LP = L + 2 * PAD
GROUPS = 4
UNITS = GROUPS * NS
CREDIT = 2
EPS = 1e-5
ds = bass.ds


class Mem:

    used = []

    def __init__(self, nc, ctx, tag):
        self.nc, self.ctx, self.tag = nc, ctx, tag

    def sb(self, name, shape, dt=F32):
        return self.ctx.enter_context(self.nc.sbuf_tensor(f"{self.tag}_{name}", shape, dt))

    def ps(self, name, shape, dt=F32):
        return self.ctx.enter_context(self.nc.psum_tensor(f"{self.tag}_{name}", shape, dt))

    def sem(self, name):
        Mem.used.append(self.nc.alloc_semaphore(name=f"{self.tag}_{name}"))
        return Mem.used[-1]


def clear_semaphores(nc):
    nc.clear_and_free_semaphores(Mem.used)
    nc.all_engine_barrier()
    Mem.used = []


def constants(nc, k):
    with ExitStack() as ctx:
        m = Mem(nc, ctx, "const")
        zeroed, step = m.sem("zeroed"), m.sem("step")
        block = ctx.enter_context(nc.Block())

        @block.vector
        def _(dve):
            dve.memset(k.mean[:], 1.0 / E)
            dve.memset(k.xn[:, :, :, 0:PAD], 0.0)
            dve.memset(k.xn[:, :, :, PAD + L:LP], 0.0).then_inc(zeroed, 1)

        @block.gpsimd
        def _(pool):
            pool.memset(k.ident[:], 0.0).then_inc(step, 1)
            pool.memset(k.sel[:], 0.0).then_inc(step, 1)
            pool.wait_ge(step, 2)
            pool.affine_select(out=k.ident[:], in_=k.ident[:], compare_op=ALU.not_equal, fill=1.0,
                               base=0, pattern=[[-1, P]], channel_multiplier=1).then_inc(step, 1)
            for part in range(3):
                pool.wait_ge(step, 3 + part)
                pool.affine_select(out=k.sel[:], in_=k.sel[:], compare_op=ALU.not_equal, fill=1.0,
                                   base=-32 * part, pattern=[[-1, 32], [0, P]],
                                   channel_multiplier=1).then_inc(step, 1)


def layernorm(nc, k, src, load=None, save=None):
    with ExitStack() as ctx:
        m = Mem(nc, ctx, "ln" if load is not None else "ln1")
        stat = m.ps("mean", [P, TT])
        var = m.ps("var", [P, TT])
        sq = m.sb("sq", [P, C, TT])
        logv = m.sb("logv", [P, TT])
        r0 = m.sb("r0", [P, TT])
        ra, rb, rstd = m.sb("ra", [P, TT]), m.sb("rb", [P, TT]), m.sb("rstd", [P, TT])
        epst = m.sb("eps", [P, 1])
        eps_set = m.sem("eps_set")
        loaded, mean_ready, centred = m.sem("loaded"), m.sem("mean_ready"), m.sem("centred")
        squared, var_ready, root_ready = m.sem("squared"), m.sem("var_ready"), m.sem("root_ready")
        logged, newton, normed = m.sem("logged"), m.sem("newton"), m.sem("normed")
        PB = L // TT
        block = ctx.enter_context(nc.Block())

        @block.sync
        def _(sp):
            if load is not None:
                for b in range(B):
                    for q in range(PB):
                        sp.dma_start(src[:, :, b * L + q * TT:b * L + (q + 1) * TT],
                                     load[:, b * L + q * TT:b * L + (q + 1) * TT]
                                     .rearrange("(c p) t -> p c t", p=P)).then_inc(loaded, 16)
                sp.wait_ge(loaded, 16 * B * PB)
            if save is not None:
                sp.dma_start(save.rearrange("(c p) t -> p c t", p=P), src[:]).then_inc(loaded, 16)
                sp.wait_ge(loaded, 16)

        @block.tensor
        def _(pe):
            if load is not None:
                pe.wait_ge(loaded, 16 * B * PB)
            with pe.Fori(0, B) as b, pe.Fori(0, PB) as q:
                i = b * PB + q
                pe.wait_ge(normed, i + 1)
                for c in range(C):
                    mm = pe.matmul(stat[:], k.mean[:], src[:, c, ds(b * L + q * TT, TT)],
                                   start=c == 0, stop=c == C - 1)
                mm.then_inc(mean_ready, 1)
                pe.wait_ge(squared, i + 1)
                for c in range(C):
                    mm = pe.matmul(var[:], k.mean[:], sq[:, c, :], start=c == 0, stop=c == C - 1)
                mm.then_inc(var_ready, 1)

        @block.scalar
        def _(act):
            act.preload_act_table_set("natural_log_exp_and_others")
            act.wait_ge(eps_set, 1)
            with act.Fori(0, B) as b, act.Fori(0, PB) as q:
                i = b * PB + q
                act.wait_ge(centred, i + 1)
                act.activation(sq[:], k.xn[:, :, b, ds(PAD + q * TT, TT)], ACT.Square).then_inc(squared, 1)
                act.wait_ge(var_ready, i + 1)
                act.activation(logv[:], var[:], ACT.Ln, bias=epst[:, 0:1]).then_inc(logged, 1)
                act.wait_ge(logged, i + 1)
                act.activation(r0[:], logv[:], ACT.Exp, scale=-0.5).then_inc(root_ready, 1)

        @block.vector
        def _(dve):
            dve.memset(epst[:], EPS).then_inc(eps_set, 1)
            dve.memset(ra[:], 0.0).then_inc(normed, 1)
            dve.wait_ge(normed, 1)
            with dve.Fori(0, B) as b, dve.Fori(0, PB) as q:
                i = b * PB + q
                dve.wait_ge(mean_ready, i + 1)
                for c in range(C):
                    ins = dve.tensor_tensor(k.xn[:, c, b, ds(PAD + q * TT, TT)],
                                            src[:, c, ds(b * L + q * TT, TT)], stat[:], ALU.subtract)
                ins.then_inc(centred, 1)
                dve.wait_ge(root_ready, i + 1)
                dve.scalar_tensor_tensor(out=ra[:], in0=var[:], scalar=EPS, in1=r0[:], op0=ALU.add,
                                         op1=ALU.mult).then_inc(newton, 1)
                dve.wait_ge(newton, i * 3 + 1)
                dve.scalar_tensor_tensor(out=rb[:], in0=ra[:], scalar=-0.5, in1=r0[:], op0=ALU.mult,
                                         op1=ALU.mult).then_inc(newton, 1)
                dve.wait_ge(newton, i * 3 + 2)
                dve.scalar_tensor_tensor(out=rstd[:], in0=rb[:], scalar=1.5, in1=r0[:], op0=ALU.add,
                                         op1=ALU.mult).then_inc(newton, 1)
                dve.wait_ge(newton, i * 3 + 3)
                for c in range(C):
                    xs = k.xn[:, c, b, ds(PAD + q * TT, TT)]
                    ins = dve.tensor_tensor(xs, xs, rstd[:], ALU.mult)
                ins.then_inc(normed, 1)


def scan_counts(it, g):
    return it * UNITS + g * NS


class ScanRing:

    def __init__(self, m):
        banks = m.ps("banks", [P, 8, TT])
        self.banks = banks
        self.decay = [banks[:, 2 * j:2 * j + 2, :] for j in range(2)]
        self.chat = banks[:, 4:6, :]
        self.y = banks[:, 6:8, :]
        self.drive = m.sb("drive", [P, 2, TC])
        self.h = m.sb("h", [P, 2, TC])
        self.prod = m.sb("prod", [P, 2, TC])
        self.decay_ready = m.sem("decay_ready")
        self.drive_ready = m.sem("drive_ready")
        self.scan_done = m.sem("scan_done")
        self.prod_ready = m.sem("prod_ready")
        self.chat_ready = m.sem("chat_ready")
        self.sum_done = m.sem("sum_done")


def flat(ap):
    return ap.rearrange("p a t -> p (a t)")


def dve_credits(dve, r):
    dve.memset(r.h[:], 0.0).then_inc(r.scan_done, CREDIT)
    dve.memset(r.prod[:], 0.0).then_inc(r.prod_ready, CREDIT)


def dve_scans(dve, r, it, g, state, col, reverse=False, state_set=None):
    step = slice(None, None, -1) if reverse else slice(None)
    with dve.Fori(0, NS // 2) as n2:
        for j in range(2):
            u = scan_counts(it, g) + n2 * 2 + j
            if state_set is not None and j == 0:
                dve.wait_ge(state_set, it + 1)
            dve.wait_ge(r.decay_ready, u + 1)
            dve.wait_ge(r.drive_ready, u + 1)
            dve.wait_ge(r.prod_ready, CREDIT + u - 1)
            dve.tensor_tensor_scan(r.h[:, j, step], flat(r.decay[j])[:, step], r.drive[:, j, step],
                                   state[:, ds(col + n2 * 2 + j, 1)], ALU.mult,
                                   ALU.add).then_inc(r.scan_done, 1)
            dve.wait_ge(r.scan_done, CREDIT + u + 1)
            dve.wait_ge(r.chat_ready, u + 1)
            dve.wait_ge(r.sum_done, CREDIT + u - 1)
            dve.tensor_tensor(r.prod[:, j, :], flat(r.chat), r.h[:, j, :],
                              ALU.mult).then_inc(r.prod_ready, 1)


def pe_sums(pe, r, it, g, weight, selector, parts):

    def spread(u, n):
        for q in range(2):
            mm = pe.matmul(r.chat[:, q, :], selector(n), parts[:, q * TT:(q + 1) * TT],
                           start=True, stop=True)
        mm.then_inc(r.chat_ready, 1)

    def add(j):
        for q in range(2):
            mm = pe.matmul(r.y[:, q, :], weight(j), r.prod[:, j, q * TT:(q + 1) * TT],
                           start=False, stop=True, skip_group_check=True)
        mm.then_inc(r.sum_done, 1)

    base = scan_counts(it, g)
    pe.wait_ge(r.prod_ready, CREDIT + base)
    spread(base, 0)
    with pe.Fori(0, NS // 2 - 1) as n2:
        for j in range(2):
            u = base + n2 * 2 + j
            pe.wait_ge(r.prod_ready, CREDIT + u + 1)
            spread(u + 1, n2 * 2 + (j + 1))
            add(j)
    pe.wait_ge(r.prod_ready, CREDIT + base + NS - 1)
    spread(base + NS - 1, NS - 1)
    add(0)
    pe.wait_ge(r.prod_ready, CREDIT + base + NS)
    add(1)


def softplus_act(act, s, ps, bias, i, credit):
    act.wait_ge(s.soft_done, credit + i)
    act.activation(s.lin, ps, ACT.Identity, bias=bias)
    act.activation(s.ex, ps, ACT.Abs, bias=bias).then_inc(s.abs_done, 1)
    act.wait_ge(s.abs_done, i + 1)
    act.activation(s.ex, s.ex, ACT.Exp, scale=-1.0).then_inc(s.exp_done, 1)
    act.wait_ge(s.exp_done, i + 1)
    act.activation(s.lg, s.ex, ACT.Ln, bias=s.one).then_inc(s.log_done, 1)


def softplus_dve(dve, s, out, i):
    dve.wait_ge(s.log_done, i + 1)
    dve.tensor_scalar(s.off, s.ex, 1.0, -1.0, ALU.add, ALU.add).then_inc(s.soft_step, 1)
    dve.wait_ge(s.soft_step, i * 3 + 1)
    dve.scalar_tensor_tensor(out=s.off, in0=s.off, scalar=-1.0, in1=s.ex, op0=ALU.mult,
                             op1=ALU.add).then_inc(s.soft_step, 1)
    dve.wait_ge(s.soft_step, i * 3 + 2)
    dve.tensor_tensor(s.lg, s.lg, s.off, ALU.add).then_inc(s.soft_step, 1)
    dve.wait_ge(s.soft_step, i * 3 + 3)
    dve.scalar_tensor_tensor(out=out, in0=s.lin, scalar=0.0, in1=s.lg, op0=ALU.max,
                             op1=ALU.add).then_inc(s.soft_done, 1)


class SoftPlus:

    def __init__(self, m, lin, ex, lg, off, one):
        self.lin, self.ex, self.lg, self.off, self.one = lin, ex, lg, off, one
        self.abs_done, self.exp_done, self.log_done = m.sem("abs_done"), m.sem("exp_done"), m.sem("log_done")
        self.soft_step, self.soft_done = m.sem("soft_step"), m.sem("soft_done")


def split_rows(dve, step, i, rows, parts, half, mid, rest):
    dve.tensor_copy(parts[0:32, :], rows).then_inc(step, 1)
    dve.wait_ge(step, i * 5 + 1)
    dve.tensor_tensor(rest, rows, parts[0:32, :], ALU.subtract).then_inc(step, 1)
    dve.wait_ge(step, i * 5 + 2)
    dve.tensor_copy(mid, rest).then_inc(step, 1)
    dve.wait_ge(step, i * 5 + 3)
    dve.tensor_copy(parts[32:64, :], mid)
    dve.tensor_tensor(rest, rest, mid, ALU.subtract).then_inc(step, 1)
    dve.wait_ge(step, i * 5 + 4)
    dve.tensor_copy(parts[64:96, :], rest).then_inc(step, 1)


def mixer0(nc, k, acc):
    R = 64
    a = k.a
    H2 = L // TC
    with ExitStack() as ctx:
        m = Mem(nc, ctx, "mix0")
        wz, wout = m.sb("wz", [P, C, E]), m.sb("wout", [P, C, E])
        wpar = m.sb("wpar", [P, C, P])
        wdt = m.sb("wdt", [R, E])
        taps, bdt, alog, dcol = m.sb("taps", [P, C, KC]), m.sb("bdt", [P, C]), m.sb("alog", [P, C, NS]), m.sb("dcol", [P, C])
        ea, neg_a, mask, keep = (m.sb(n, [P, C * NS]) for n in ("ea", "neg_a", "mask", "keep"))
        den, rec, reff, rsum = (m.sb(n, [P, C * NS]) for n in ("den", "rec", "reff", "rsum"))
        rsum_t = m.sb("rsum_t", [NS, C, P])
        diag_d = m.sb("diag_d", [P, C, P])
        diag_r = m.sb("diag_r", [P, 2, P])
        one = m.sb("one", [P, 1])
        u = m.sb("u", [P, C, L + 1])
        dt = m.sb("dt", [P, C, L + 1])
        du = m.sb("du", [P, C, L])
        dd = m.sb("dd", [P, C, L])
        rows, dtin = m.sb("rows", [32, L]), m.sb("dtin", [R, L])
        parts = m.sb("parts", [96, L], BF16)
        state = m.sb("state", [P, C * (NS + 1)])
        r = ScanRing(m)
        mid = r.prod[0:32, 0, :].bitcast(BF16)
        rest = r.h[0:32, :, :].rearrange("p a t -> p (a t)")
        s = SoftPlus(m, r.drive[:, 0, :], r.drive[:, 1, :], r.h[:, 0, :], r.h[:, 1, :], one[:, 0:1])

        loaded, cleared = m.sem("loaded"), m.sem("cleared")
        ea_ready, setup, rs_turned, rs_kept = m.sem("ea_ready"), m.sem("setup"), m.sem("rs_turned"), m.sem("rs_kept")
        batch_done = m.sem("batch_done")
        tap_done, u_ready = m.sem("tap_done"), m.sem("u_ready")
        par_ready, par_kept, split = m.sem("par_ready"), m.sem("par_kept"), m.sem("split")
        dt_ready = m.sem("dt_ready")
        shaped, step_ready = m.sem("shaped"), m.sem("step_ready")
        mask_ready, saved = m.sem("mask_ready"), m.sem("saved")
        rs_ready, y_step, y_ready = m.sem("rs_ready"), m.sem("y_step"), m.sem("y_ready")
        z_ready, gate_ready, gated = m.sem("z_ready"), m.sem("gate_ready"), m.sem("gated")
        out_ready, added = m.sem("out_ready"), m.sem("added")
        SETUP = 9
        block = ctx.enter_context(nc.Block())

        @block.sync
        def _(sp):
            sp.wait_ge(cleared, 1)
            for dst, src in (
                (wz[:], a["W_z"].rearrange("(c p) m -> p c m", p=P)),
                (wout[:], a["W_out"].rearrange("(c p) m -> p c m", p=P)),
                (wpar[:, :, 0:NS], a["W_par"][:, R + NS:R + 2 * NS].rearrange("(c p) m -> p c m", p=P)),
                (wpar[:, :, 64:64 + R], a["W_par"][:, 0:R].rearrange("(c p) m -> p c m", p=P)),
                (wdt[:], a["W_dt"]),
                (taps[:], a["conv_w"].rearrange("(c p) k -> p c k", p=P)),
                (bdt[:], a["b_dt"]),
                (alog[:], a["A_log"].rearrange("(c p) n -> p c n", p=P)),
                (dcol[:], a["D"]),
            ):
                sp.dma_start(dst, src).then_inc(loaded, 16)

        LOADS = 9 * 16

        @block.gpsimd
        def _(pool):
            with pool.Fori(0, B) as b:
                for c in range(C):
                    for hf in range(H2):
                        g = c * H2 + hf
                        with pool.Fori(0, NS // 2) as n2:
                            for j in range(2):
                                un = scan_counts(b, g) + n2 * 2 + j
                                pool.wait_ge(mask_ready, un + 1)
                                pool.tensor_tensor(r.drive[:, j, :], r.drive[:, j, :],
                                                   du[:, c, hf * TC:(hf + 1) * TC],
                                                   ALU.add).then_inc(r.drive_ready, 1)

        @block.scalar
        def _(act):
            act.preload_act_table_set("natural_log_exp_and_others")
            act.wait_ge(loaded, LOADS)
            act.activation(ea[:], alog[:].rearrange("p c n -> p (c n)"), ACT.Exp).then_inc(ea_ready, 1)
            act.wait_ge(rs_turned, 1)
            act.activation(rsum_t[:], r.banks[0:NS, 0, 0:C * P].rearrange("n (c p) -> n c p", c=C),
                           ACT.Copy).then_inc(rs_kept, 1)
            with act.Fori(0, B) as b:
                for c in range(C):
                    act.wait_ge(tap_done, b * 8 + 4 * (c + 1))
                    act.activation(u[:, c, 1:L + 1], u[:, c, 1:L + 1], ACT.Silu).then_inc(u_ready, 1)
                act.preload_act_table_set("natural_log_exp_and_others")
                act.wait_ge(par_ready, b + 1)
                act.activation(rows[:], r.banks[0:32, 0:4, :].rearrange("p a t -> p (a t)"),
                               ACT.Copy).then_inc(par_kept, 1)
                act.activation(dtin[:], r.banks[64:128, 0:4, :].rearrange("p a t -> p (a t)"),
                               ACT.Copy).then_inc(par_kept, 1)
                act.wait_ge(split, b * 5 + 5)
                for c in range(C):
                    for hf in range(H2):
                        i = b * 4 + (c * H2 + hf)
                        act.wait_ge(dt_ready, i + 1)
                        softplus_act(act, s, flat(r.decay[hf]), bdt[:, c:c + 1], i, 1)
                act.wait_ge(step_ready, b + 1)
                for c in range(C):
                    for hf in range(H2):
                        g = c * H2 + hf
                        if g:
                            act.wait_ge(saved, b * 4 + g)
                        with act.Fori(0, NS // 2) as n2:
                            for j in range(2):
                                un = scan_counts(b, g) + n2 * 2 + j
                                at = n2 * 2 + (c * NS + j)
                                act.wait_ge(r.scan_done, CREDIT + un - 1)
                                act.activation(r.drive[:, j, :], dd[:, c, hf * TC:(hf + 1) * TC], ACT.Copy,
                                               scale=mask[:, ds(at, 1)]).then_inc(mask_ready, 1)
                                act.wait_ge(r.sum_done, CREDIT + un - 1)
                                act.activation(diag_r[:, j, :], k.ident[:], ACT.Copy, scale=reff[:, ds(at, 1)])
                                act.activation(flat(r.decay[j]), dt[:, c, hf * TC:(hf + 1) * TC], ACT.Exp,
                                               scale=neg_a[:, ds(at, 1)]).then_inc(r.decay_ready, 1)
                                act.wait_ge(r.scan_done, CREDIT + un)
                                act.activation(state[:, ds(at + c, 1)], r.h[:, 1 - j, TC - 1:TC], ACT.Copy)
                        act.wait_ge(r.scan_done, CREDIT + scan_counts(b, g) + NS)
                        act.activation(state[:, c * (NS + 1) + NS:(c + 1) * (NS + 1)], r.h[:, 1, TC - 1:TC],
                                       ACT.Copy).then_inc(saved, 1)
                for c in range(C):
                    for hf in range(H2):
                        g = c * H2 + hf
                        act.wait_ge(z_ready, b * 4 + g + 1)
                        act.activation(dd[:, c, hf * TC:(hf + 1) * TC], flat(r.decay[hf]),
                                       ACT.Silu).then_inc(gate_ready, 1)

        @block.vector
        def _(dve):
            dve.memset(wpar[:], 0.0).then_inc(cleared, 1)
            dve.memset(one[:], 1.0).then_inc(batch_done, 1)
            dve_credits(dve, r)
            dve.wait_ge(r.scan_done, CREDIT)
            dve.wait_ge(r.prod_ready, CREDIT)
            dve.memset(s.off, 0.0).then_inc(s.soft_done, 1)
            dve.wait_ge(loaded, LOADS)
            for c in range(C):
                dve.tensor_scalar(diag_d[:, c, :], k.ident[:], dcol[:, c:c + 1], None, ALU.mult)
            dve.wait_ge(ea_ready, 1)
            dve.tensor_scalar(neg_a[:], ea[:], -1.0, None, ALU.mult).then_inc(setup, 1)
            dve.tensor_scalar(mask[:], ea[:], 1e-5, None, ALU.is_lt).then_inc(setup, 1)
            dve.wait_ge(setup, 2)
            dve.tensor_scalar(keep[:], mask[:], -1.0, 1.0, ALU.mult, ALU.add).then_inc(setup, 1)
            dve.tensor_scalar(den[:], neg_a[:], 1e-10, None, ALU.add).then_inc(setup, 1)
            dve.wait_ge(setup, 4)
            dve.tensor_tensor(den[:], den[:], mask[:], ALU.subtract).then_inc(setup, 1)
            dve.wait_ge(setup, 5)
            dve.reciprocal(rec[:], den[:]).then_inc(setup, 1)
            dve.wait_ge(setup, 6)
            dve.tensor_tensor(rsum[:], rec[:], keep[:], ALU.mult).then_inc(setup, 1)
            dve.wait_ge(setup, 7)
            dve.tensor_tensor(reff[:], rsum[:], mask[:], ALU.add).then_inc(setup, 1)
            dve.memset(state[:], 0.0).then_inc(setup, 1)
            dve.wait_ge(setup, SETUP)
            with dve.Fori(0, B) as b:
                for c in range(C):
                    uc = u[:, c, 1:L + 1]
                    dve.tensor_scalar(uc, k.xn[:, c, ds(b, 1), 0:L], taps[:, c, 0:1], None,
                                      ALU.mult).then_inc(tap_done, 1)
                    for t in range(1, KC):
                        dve.wait_ge(tap_done, b * 8 + (4 * c + t))
                        dve.scalar_tensor_tensor(out=uc, in0=k.xn[:, c, b, t:t + L], scalar=taps[:, c, t:t + 1],
                                                 in1=uc, op0=ALU.mult, op1=ALU.add).then_inc(tap_done, 1)
                dve.wait_ge(par_kept, b * 2 + 1)
                split_rows(dve, split, b, rows[:], parts, None, mid, rest)
                dve.wait_ge(split, b * 5 + 5)
                for c in range(C):
                    for hf in range(H2):
                        softplus_dve(dve, s, dt[:, c, 1 + hf * TC:1 + (hf + 1) * TC], b * 4 + (c * H2 + hf))
                dve.wait_ge(u_ready, b * 2 + 2)
                dve.wait_ge(s.soft_done, 1 + b * 4 + 4)
                for c in range(C):
                    dve.tensor_copy(u[:, c, 0:1], u[:, c, 1:2])
                    dve.tensor_copy(dt[:, c, 0:1], dt[:, c, 1:2]).then_inc(shaped, 1)
                dve.wait_ge(shaped, b * 6 + 2)
                for c in range(C):
                    dve.tensor_tensor(du[:, c, :], u[:, c, 1:L + 1], u[:, c, 0:L], ALU.subtract)
                    dve.tensor_tensor(dd[:, c, :], u[:, c, 0:L], dt[:, c, 0:L], ALU.mult).then_inc(shaped, 1)
                    dve.tensor_scalar(state[:, 1 + c * (NS + 1):(c + 1) * (NS + 1)], keep[:, c * NS:(c + 1) * NS],
                                      u[:, c, 0:1], None, ALU.mult).then_inc(shaped, 1)
                dve.wait_ge(shaped, b * 6 + 6)
                for c in range(C):
                    ins = dve.tensor_tensor(dd[:, c, :], dd[:, c, :], du[:, c, :], ALU.subtract)
                ins.then_inc(step_ready, 1)
                for c in range(C):
                    for hf in range(H2):
                        g = c * H2 + hf
                        dve_scans(dve, r, b, g, state, 1 + c * (NS + 1))
                        dve.wait_ge(rs_ready, b * 4 + g + 1)
                        dve.wait_ge(r.prod_ready, CREDIT + scan_counts(b, g) + NS)
                        dve.tensor_tensor(r.prod[:, 0, :], flat(r.chat), u[:, c, 1 + hf * TC:1 + (hf + 1) * TC],
                                          ALU.mult).then_inc(y_step, 1)
                        dve.wait_ge(y_step, b * 4 + g + 1)
                        dve.tensor_tensor(du[:, c, hf * TC:(hf + 1) * TC], flat(r.y), r.prod[:, 0, :],
                                          ALU.subtract).then_inc(y_ready, 1)
                for c in range(C):
                    for hf in range(H2):
                        g = c * H2 + hf
                        yc = du[:, c, hf * TC:(hf + 1) * TC]
                        dve.wait_ge(gate_ready, b * 4 + g + 1)
                        dve.wait_ge(y_ready, b * 4 + g + 1)
                        dve.tensor_tensor(yc, yc, dd[:, c, hf * TC:(hf + 1) * TC], ALU.mult).then_inc(gated, 1)
                for c in range(C):
                    for hf in range(H2):
                        g = c * H2 + hf
                        dve.wait_ge(out_ready, b * 4 + g + 1)
                        ac = acc[:, c, ds(b * L + hf * TC, TC)]
                        ins = dve.tensor_tensor(ac, flat(r.decay[hf]), ac, ALU.add).then_inc(added, 1)
                dve.wait_ge(added, b * 4 + 4)
                dve.memset(one[:], 1.0).then_inc(batch_done, 1)

        @block.tensor
        def _(pe):
            pe.sem_inc(r.sum_done, CREDIT)
            pe.wait_ge(loaded, LOADS)
            pe.wait_ge(setup, SETUP)
            for c in range(C):
                mm = pe.transpose(r.banks[0:NS, 0, c * P:(c + 1) * P], rsum[:, c * NS:(c + 1) * NS], k.ident[:])
            mm.then_inc(rs_turned, 1)
            pe.wait_ge(rs_kept, 1)
            with pe.Fori(0, B) as b:
                pe.wait_ge(batch_done, b + 1)
                for q in range(4):
                    for c in range(C):
                        mm = pe.matmul(r.banks[:, q, :], wpar[:, c, :],
                                       k.xn[:, c, b, PAD + q * TT:PAD + (q + 1) * TT],
                                       start=c == 0, stop=c == C - 1)
                mm.then_inc(par_ready, 1)
                pe.wait_ge(par_kept, b * 2 + 2)
                for c in range(C):
                    for hf in range(H2):
                        i = b * 4 + (c * H2 + hf)
                        if c:
                            pe.wait_ge(s.log_done, i - 1)
                        for q in range(2):
                            mm = pe.matmul(r.decay[hf][:, q, :], wdt[:, c * P:(c + 1) * P],
                                           dtin[:, hf * TC + q * TT:hf * TC + (q + 1) * TT],
                                           start=True, stop=True)
                        mm.then_inc(dt_ready, 1)
                for c in range(C):
                    for hf in range(H2):
                        g = c * H2 + hf
                        if g == 0:
                            pe.wait_ge(step_ready, b + 1)
                            pe.wait_ge(split, b * 5 + 5)
                        else:
                            pe.wait_ge(y_ready, b * 4 + g)
                        for q in range(2):
                            o = 1 + hf * TC + q * TT
                            pe.matmul(r.y[:, q, :], diag_d[:, c, :], u[:, c, o:o + TT], start=True, stop=True,
                                      skip_group_check=True)
                        pe_sums(pe, r, b, g, lambda j: diag_r[:, j, :],
                                lambda n: k.sel[:, n, :] if isinstance(n, int) else k.sel[:, ds(n, 1), :],
                                parts[:, hf * TC:(hf + 1) * TC])
                        for q in range(2):
                            o = hf * TC + q * TT
                            mm = pe.matmul(r.chat[:, q, :], rsum_t[:, c, :], rows[0:NS, o:o + TT],
                                           start=True, stop=True)
                        mm.then_inc(rs_ready, 1)
                for c in range(C):
                    for hf in range(H2):
                        g = c * H2 + hf
                        if g == 0:
                            pe.wait_ge(saved, b * 4 + 4)
                        if c:
                            pe.wait_ge(gate_ready, b * 4 + g - 1)
                        for q in range(2):
                            o = PAD + hf * TC + q * TT
                            for kk in range(C):
                                mm = pe.matmul(r.decay[hf][:, q, :], wz[:, kk, c * P:(c + 1) * P],
                                               k.xn[:, kk, b, o:o + TT], start=kk == 0, stop=kk == C - 1)
                        mm.then_inc(z_ready, 1)
                pe.wait_ge(gated, b * 4 + 4)
                for c in range(C):
                    for hf in range(H2):
                        g = c * H2 + hf
                        if c:
                            pe.wait_ge(added, b * 4 + g - 1)
                        for q in range(2):
                            o = hf * TC + q * TT
                            for kk in range(C):
                                mm = pe.matmul(r.decay[hf][:, q, :], wout[:, kk, c * P:(c + 1) * P],
                                               du[:, kk, o:o + TT], start=kk == 0, stop=kk == C - 1)
                        mm.then_inc(out_ready, 1)


def experts0(nc, k, acc):
    GS, SL, F = 16, 64, 64
    NG = L // GS
    QG = TT // GS
    NQ = L // TT
    EG = 8
    NE = SL // EG
    a = k.a
    z = nc.dram_tensor("slot_outputs", (B, NG, SL, E), F32, kind="Internal").ap()
    with ExitStack() as keep:
        perm_t = Mem(nc, keep, "exp").sb("perm_t", [P, T])
        with ExitStack() as ctx:
            m = Mem(nc, ctx, "exa")
            ctrl, bias = m.sb("ctrl", [P, C, P]), m.sb("bias", [F, SL])
            tie, parity = m.sb("tie", [P, QG, GS]), m.sb("parity", [P, QG, GS])
            pair_of = m.sb("pair_of", [P, 4])
            lt, pq = m.sb("lt", [P, TT]), m.sb("pq", [P, TT])
            top = m.sb("top", [P, QG])
            work = m.sb("work", [P, 2, EG * P])
            xs = work[:, 0, :].rearrange("p (c t) -> p c t", c=C)
            xtok = work[:, 1, :].rearrange("p (t e) -> p t e", t=4)
            inner = work[0:F, :, :].rearrange("p j (s g) -> p j s g", s=EG)
            pex = m.sb("pex", [P, 2, 4, P])
            sel_t = m.sb("sel_t", [P, C, SL, NG])
            f1 = m.sb("f1", [P, 2, C, EG, F])
            f2 = m.sb("f2", [F, 2, EG, E])
            inter = m.sb("inter", [P, 2, 4, E])
            banks = m.ps("banks", [P, 8, TT])
            loaded, built = m.sem("loaded"), m.sem("built")
            lg_ready, pstep, perm_ready = m.sem("lg_ready"), m.sem("pstep"), m.sem("perm_ready")
            xs_ready, turned, xtok_ready, pex_ready = m.sem("xs_ready"), m.sem("turned"), m.sem("xtok_ready"), m.sem("pex_ready")
            sel_ready, sel_kept = m.sem("sel_ready"), m.sem("sel_kept")
            w_loaded = [m.sem(f"w_loaded{j}") for j in range(2)]
            stored = [m.sem(f"stored{j}") for j in range(2)]
            slot_free = [m.sem(f"slot_free{j}") for j in range(2)]
            biased = m.sem("biased")
            in_ready, inner_ready = m.sem("in_ready"), m.sem("inner_ready")
            fill_ready, act_kept, dve_kept = m.sem("fill_ready"), m.sem("act_kept"), m.sem("dve_kept")
            block = ctx.enter_context(nc.Block())

            @block.sync
            def _(sp):
                ctl = a["controller"].rearrange("(c p) m -> p c m", p=P)
                for dst, src in ((ctrl[:, :, 0:SL], ctl), (ctrl[:, :, SL:P], ctl), (bias[:], a["bias"]),
                                 (tie[:], a["tie"])):
                    sp.dma_start(dst, src).then_inc(loaded, 16)
                with sp.Fori(0, B) as b, sp.Fori(0, NE // 2) as e2:
                    for j in range(2):
                        e = b * NE + e2 * 2 + j
                        sp.wait_ge(fill_ready, 8 + e * 4 - 4)
                        sp.dma_start(f1[:, j], a["f1"].rearrange("(c p) (e s) f -> p c e s f", p=P, s=EG)[
                            :, :, ds(e2 * 2 + j, 1)].rearrange("p c e s f -> p c (e s f)")).then_inc(w_loaded[j], 16)
                        sp.dma_start(f2[:, j], a["f2"].rearrange("(e s) f d -> f e s d", e=NE)[
                            :, ds(e2 * 2 + j, 1)].rearrange("p e s d -> p (e s) d")).then_inc(w_loaded[j], 16)

            @block.gpsimd
            def _(pool):
                for j in range(2):
                    pool.sem_inc(slot_free[j], 1)
                with pool.Fori(0, B) as b, pool.Fori(0, NE) as e:
                    i = b * NE + e
                    for j in range(2):
                        pool.wait_ge(act_kept, 1 + i * 2 + (j + 1))
                        pool.wait_ge(dve_kept, 1 + i * 2 + (j + 1))
                        pool.dma_start(z[ds(b, 1), :, ds(e * EG + j * 4, 4), :].rearrange("b g s d -> (b g) (s d)"),
                                       inter[:, j].rearrange("p s d -> p (s d)")).then_inc(stored[j], 16)
                    for j in range(2):
                        pool.wait_ge(stored[j], i * 16 + 16)
                        pool.sem_inc(slot_free[j], 1)

            @block.scalar
            def _(act):
                act.wait_ge(loaded, 16 * 4)
                act.sem_inc(act_kept, 1)
                with act.Fori(0, B) as b:
                    with act.Fori(0, NQ) as q:
                        i = b * NQ + q
                        act.wait_ge(sel_ready, 1 + i * 8)
                        act.activation(xs, k.xn[:, :, b, ds(PAD + q * TT, TT)], ACT.Copy).then_inc(xs_ready, 1)
                        act.wait_ge(perm_ready, 1 + (i + 1))
                        act.activation(perm_t[:, ds(b * L + q * TT, TT)], pq[:], ACT.Copy)
                        act.wait_ge(turned, i + 1)
                        act.activation(work[:, 1, :],
                                       banks[:, 1:3, :].rearrange("p a t -> p (a t)"), ACT.Copy).then_inc(xtok_ready, 1)
                        for t in range(4):
                            for c in range(C):
                                n = i * 8 + (t * C + c)
                                act.wait_ge(sel_ready, 1 + (n + 1))
                                act.activation(
                                    sel_t[:, c, :, ds(q * QG + t * 8, 8)].rearrange("p s g -> p g s"),
                                    banks[:, 4 + c, :].rearrange("p (g s) -> p g s", s=SL),
                                    ACT.Copy).then_inc(sel_kept, 1)
                    with act.Fori(0, NE // 2) as e2:
                        for j in range(2):
                            e = b * NE + e2 * 2 + j
                            for h in range(2):
                                act.wait_ge(fill_ready, 8 + e * 4 + (2 * h + 1))
                                act.wait_ge(slot_free[h], e + 1)
                                act.activation(inter[:, h, 0:2, :].rearrange("p s d -> p (s d)"), banks[:, 7, :],
                                               ACT.Copy).then_inc(act_kept, 1)

            @block.vector
            def _(dve):
                dve.memset(parity[0:64, 0:QG:2], 1.0)
                dve.memset(parity[0:64, 1:QG:2], 0.0)
                dve.memset(parity[64:128, 0:QG:2], 0.0)
                dve.memset(parity[64:128, 1:QG:2], 1.0).then_inc(built, 1)
                for i in range(4):
                    for v in range(4):
                        ins = dve.memset(pair_of[32 * v:32 * v + 32, i:i + 1], 1.0 if i == v else 0.0)
                ins.then_inc(built, 1)
                dve.memset(lt[:], 0.0).then_inc(perm_ready, 1)
                dve.memset(pex[:], 0.0).then_inc(dve_kept, 1)
                dve.wait_ge(perm_ready, 1)
                dve.wait_ge(dve_kept, 1)
                dve.wait_ge(loaded, 16 * 4)
                dve.wait_ge(built, 2)
                with dve.Fori(0, B) as b:
                    with dve.Fori(0, NQ) as q:
                        i = b * NQ + q
                        lg = banks[:, 0, :].rearrange("p (g t) -> p g t", t=GS)
                        ltg = lt[:].rearrange("p (g t) -> p g t", t=GS)
                        dve.wait_ge(lg_ready, i + 1)
                        dve.tensor_tensor(ltg, lg, tie[:], ALU.add).then_inc(pstep, 1)
                        dve.wait_ge(pstep, i * 3 + 1)
                        dve.tensor_reduce(top[:], ltg, AX.X, ALU.max).then_inc(pstep, 1)
                        dve.wait_ge(pstep, i * 3 + 2)
                        dve.tensor_tensor(ltg, ltg, top[:].unsqueeze(2).broadcast_to([P, QG, GS]),
                                          ALU.is_equal).then_inc(pstep, 1)
                        dve.wait_ge(pstep, i * 3 + 3)
                        dve.tensor_tensor(pq[:].rearrange("p (g t) -> p g t", t=GS), ltg, parity[:],
                                          ALU.mult).then_inc(perm_ready, 1)
                        dve.wait_ge(turned, i + 1)
                        for t in range(4):
                            dve.wait_ge(sel_ready, 1 + i * 8 + 2 * (t - 1) if t > 1 else 1 + i * 8)
                            dve.tensor_tensor(pex[:, t % 2], banks[:, 3, t * P:(t + 1) * P].unsqueeze(1)
                                              .broadcast_to([P, 4, P]),
                                              pair_of[:].unsqueeze(2).broadcast_to([P, 4, P]),
                                              ALU.mult).then_inc(pex_ready, 1)
                    with dve.Fori(0, NE // 2) as e2:
                        for j in range(2):
                            ex = b * NE + e2 * 2 + j
                            dve.wait_ge(in_ready, ex + 1)
                            dve.wait_ge(fill_ready, 8 + ex * 4 - 4)
                            dve.tensor_tensor(inner[:, j], banks[0:F, 5:7, :].rearrange("p a (s g) -> p (a s) g", g=P),
                                              bias[:, ds((e2 * 2 + j) * EG, EG)].unsqueeze(2).broadcast_to([F, EG, P]),
                                              ALU.add).then_inc(biased, 1)
                            dve.wait_ge(biased, ex + 1)
                            dve.tensor_scalar(inner[:, j], inner[:, j], 0.0, None, ALU.max).then_inc(inner_ready, 1)
                            for h in range(2):
                                dve.wait_ge(fill_ready, 8 + ex * 4 + (2 * h + 2))
                                dve.wait_ge(slot_free[h], ex + 1)
                                dve.tensor_copy(inter[:, h, 2:4, :].rearrange("p s d -> p (s d)"),
                                                banks[:, 0, :]).then_inc(dve_kept, 1)

            @block.tensor
            def _(pe):
                pe.sem_inc(fill_ready, 8)
                pe.sem_inc(sel_ready, 1)
                pe.wait_ge(loaded, 16 * 4)
                with pe.Fori(0, B) as b:
                    with pe.Fori(0, NQ) as q:
                        i = b * NQ + q
                        pe.wait_ge(perm_ready, 1 + i)
                        pe.wait_ge(dve_kept, 1 + b * 2 * NE)
                        for c in range(C):
                            mm = pe.matmul(banks[:, 0, :], ctrl[:, c, :], k.xn[:, c, b, ds(PAD + q * TT, TT)],
                                           start=c == 0, stop=c == C - 1)
                        mm.then_inc(lg_ready, 1)
                        pe.wait_ge(xs_ready, i + 1)
                        for t in range(4):
                            for c in range(C):
                                o = (t * C + c) * P
                                pe.transpose(banks[:, 1 + o // TT, o % TT:o % TT + P], xs[:, c, t * P:(t + 1) * P],
                                             k.ident[:])
                        pe.wait_ge(perm_ready, 1 + (i + 1))
                        for t in range(4):
                            mm = pe.transpose(banks[:, 3, t * P:(t + 1) * P], pq[:, t * P:(t + 1) * P], k.ident[:])
                        mm.then_inc(turned, 1)
                        pe.wait_ge(xtok_ready, i + 1)
                        for t in range(4):
                            pe.wait_ge(pex_ready, i * 4 + (t + 1))
                            for c in range(C):
                                n = i * 8 + (t * C + c)
                                if t:
                                    pe.wait_ge(sel_kept, n - 1)
                                mm = pe.matmul(banks[:, 4 + c, :], xtok[:, t, c * P:(c + 1) * P],
                                               pex[:, t % 2].rearrange("p a n -> p (a n)"), start=True, stop=True)
                                mm.then_inc(sel_ready, 1)
                    with pe.Fori(0, NE // 2) as e2:
                        for j in range(2):
                            e = b * NE + e2 * 2 + j
                            pe.wait_ge(w_loaded[j], (b * (NE // 2) + e2 + 1) * 32)
                            pe.wait_ge(sel_kept, (b + 1) * NQ * 8)
                            for s in range(EG):
                                for c in range(C):
                                    mm = pe.matmul(banks[0:F, 5 + s // 4, s % 4 * P:(s % 4 + 1) * P],
                                                   f1[:, j, c, s, :],
                                                   sel_t[:, c, ds((e2 * 2 + j) * EG + s, 1), :],
                                                   start=c == 0, stop=c == C - 1)
                            mm.then_inc(in_ready, 1)
                            pe.wait_ge(inner_ready, e + 1)
                            for f in range(4):
                                kept = act_kept if f % 2 == 0 else dve_kept
                                bank = 7 if f % 2 == 0 else 0
                                pe.wait_ge(kept, 1 + e * 2 + f // 2)
                                for h in range(2):
                                    mm = pe.matmul(banks[:, bank, h * E:(h + 1) * E], inner[:, j, 2 * f + h, :],
                                                   f2[:, j, 2 * f + h, :], start=True, stop=True)
                                mm.then_inc(fill_ready, 1)

        with ExitStack() as ctx:
            m = Mem(nc, ctx, "exb")
            zp = m.sb("zp", [P, 2, TT // 32, E])
            out = m.ps("out", [P, 2, C, TT])
            z_loaded = [m.sem(f"z_loaded{j}") for j in range(2)]
            out_ready, added = m.sem("out_ready"), m.sem("added")
            block = ctx.enter_context(nc.Block())

            @block.sync
            def _(sp):
                zr = z.rearrange("b (q r h) s d -> (h s) (b q) r d", h=2, r=TT // 32)
                with sp.Fori(0, B * NQ // 2) as i2:
                    for j in range(2):
                        sp.wait_ge(out_ready, i2 * 2 + (j + 1))
                        sp.dma_start(zp[:, j], zr[:, ds(i2 * 2 + j, 1)].rearrange("p q r d -> p (q r) d")
                                     ).then_inc(z_loaded[j], 16)

            @block.tensor
            def _(pe):
                pe.sem_inc(out_ready, 2)
                with pe.Fori(0, B * NQ // 2) as i2:
                    for j in range(2):
                        i = i2 * 2 + j
                        pe.wait_ge(z_loaded[j], i2 * 16 + 16)
                        pe.wait_ge(added, i + 1)
                        for t in range(TT // 32):
                            for c in range(C):
                                mm = pe.matmul(out[:, j, c, t * 32:(t + 1) * 32], zp[:, j, t, c * P:(c + 1) * P],
                                               perm_t[:, ds(i * TT + t * 32, 32)], start=True, stop=True)
                        mm.then_inc(out_ready, 1)

            @block.vector
            def _(dve):
                dve.sem_inc(added, 2)
                with dve.Fori(0, B * NQ // 2) as i2:
                    for j in range(2):
                        i = i2 * 2 + j
                        dve.wait_ge(out_ready, 2 + (i + 1))
                        ac = acc[:, :, ds(i * TT, TT)]
                        dve.tensor_tensor(ac, out[:, j], ac, ALU.add).then_inc(added, 1)


def mixer1(nc, k, way, y_dram):
    D2, R, MB = 512, 16, 4
    a = k.a
    bw = way == "bw"
    NC = L // TC
    with ExitStack() as ctx:
        m = Mem(nc, ctx, way)
        win, wout = m.sb("win", [P, C, 2 * D2]), m.sb("wout", [P, MB, E])
        wx, wdt = m.sb("wx", [P, MB, 64 + R]), m.sb("wdt", [R, D2])
        taps, small = m.sb("taps", [P, MB, KC]), m.sb("small", [P, 3, MB])
        convb, bdt, dcol = small[:, 0, :], small[:, 1, :], small[:, 2, :]
        norm = m.sb("norm", [P, 2, C])
        alog, neg_a = m.sb("alog", [P, MB * NS]), m.sb("neg_a", [P, MB * NS])
        diag_d = m.sb("diag_d", [P, MB, P])
        consts = m.sb("consts", [P, 4])
        one, eps, carry = consts[:, 0:1], consts[:, 1:2], consts[:, 2:4]
        u, dt, dtu = m.sb("u", [P, MB, TC]), m.sb("dt", [P, MB, TC]), m.sb("dtu", [P, MB, TC])
        rows, dtin = m.sb("rows", [32, TC]), m.sb("dtin", [R, TC])
        parts = m.sb("parts", [96, TC], BF16)
        brep = m.sb("brep", [P, NS, TC])
        state = m.sb("state", [P, MB * (NS + 1)])
        r = ScanRing(m)
        flatb = r.banks[:].rearrange("p a t -> p (a t)")
        mid = r.prod[0:32, 0, 0:TC // 2].bitcast(BF16)
        rest = r.prod[0:32, 1, :]
        s = SoftPlus(m, r.drive[:, 0, :], r.drive[:, 1, :], r.h[:, 0, :], r.h[:, 1, :], one)
        res, sq, logv, r0, ra, rb, rstd, yf = (brep[:, 0:2], brep[:, 2:4], brep[:, 4], brep[:, 5], brep[:, 6],
                                               brep[:, 7], brep[:, 8], brep[:, 9:11])
        (loaded, cleared, ea_ready, setup, xi_ready, tap0, tap_done, u_ready, par_ready, par_kept, split, dt_ready,
         dtu_ready, b_spread, b_act, b_dve, b_free, started, y_done, saved, z_ready, gate_ready, gated, out_ready,
         summed, mean_ready, centred, squared, var_ready, logged, root_ready, newton, scaled, y_out, stored,
         yf_loaded) = (m.sem(n) for n in (
             "loaded cleared ea_ready setup xi_ready tap0 tap_done u_ready par_ready par_kept split dt_ready "
             "dtu_ready b_spread b_act b_dve b_free started y_done saved z_ready gate_ready gated out_ready "
             "summed mean_ready centred squared var_ready logged root_ready newton scaled y_out stored "
             "yf_loaded").split())
        LOADS = 11 * 16
        block = ctx.enter_context(nc.Block())

        def passes(eng):
            both = ExitStack()
            b = both.enter_context(eng.Fori(0, B))
            tc = both.enter_context(eng.Fori(0, NC))
            return both, b, b * NC + tc, tc, ((tc * -TC) + (L - TC)) if bw else tc * TC

        @block.sync
        def _(sp):
            sp.wait_ge(cleared, 1)
            wxa = a[way + "_Wx"].rearrange("(c p) m -> p c m", p=P)
            for dst, src in ((win[:], a[way + "_Win"].rearrange("(c p) m -> p c m", p=P)),
                             (wout[:], a[way + "_Wout"].rearrange("(c p) m -> p c m", p=P)),
                             (wx[:, :, 0:2 * NS], wxa[:, :, R:R + 2 * NS]),
                             (wx[:, :, 64:64 + R], wxa[:, :, 0:R]),
                             (wdt[:], a[way + "_Wdt"]),
                             (taps[:], a[way + "_convw"].rearrange("(c p) k -> p c k", p=P)),
                             (convb, a[way + "_convb"]), (bdt, a[way + "_bdt"]), (dcol, a[way + "_D"]),
                             (alog[:].rearrange("p (c n) -> p c n", n=NS), a[way + "_Alog"].rearrange("(c p) n -> p c n", p=P)),
                             (norm[:], a["fwn"])):
                sp.dma_start(dst, src).then_inc(loaded, 16)
            sp.sem_inc(b_free, 1)
            yd = y_dram.rearrange("(c p) t -> p c t", p=P)
            both, b, it, tc, t0 = passes(sp)
            with both:
                here = yd[:, :, ds(b * L + t0, TC)]
                if bw:
                    sp.wait_ge(gated, it * MB + MB)
                    sp.dma_start(yf, here).then_inc(yf_loaded, 16)
                sp.wait_ge(y_out, 1 + (it + 1))
                sp.dma_start(here, res).then_inc(stored, 16)
                sp.wait_ge(stored, it * 16 + 16)
                sp.sem_inc(b_free, 1)

        @block.gpsimd
        def _(pool):
            both, b, it, tc, t0 = passes(pool)
            with both:
                for g in range(MB):
                    with pool.Fori(0, NS // 2) as n2:
                        for j in range(2):
                            un = scan_counts(it, g) + n2 * 2 + j
                            if g == 0:
                                pool.wait_ge(b_act, it * 8 + n2 + 1)
                                pool.wait_ge(b_dve, it * 8 + n2 + 1)
                            pool.wait_ge(dtu_ready, it * MB + (g + 1))
                            pool.wait_ge(r.scan_done, CREDIT + un - 1)
                            pool.tensor_tensor(r.drive[:, j, :], brep[:, ds(n2 * 2 + j, 1), :].rearrange("p n t -> p (n t)"),
                                               dtu[:, g, :], ALU.mult).then_inc(r.drive_ready, 1)

        @block.scalar
        def _(act):
            act.preload_act_table_set("natural_log_exp_and_others")
            act.wait_ge(loaded, LOADS)
            act.activation(alog[:], alog[:], ACT.Exp).then_inc(ea_ready, 1)
            both, b, it, tc, t0 = passes(act)
            with both:
                for g in range(MB):
                    x0 = g % 2 * 4 * TT + (PAD if bw else 0)
                    act.wait_ge(xi_ready, it * MB + (g + 1))
                    act.activation(u[:, g, :], flatb[:, x0:x0 + TC], ACT.Identity, bias=convb[:, g:g + 1],
                                   scale=taps[:, g, 0:1]).then_inc(tap0, 1)
                for g in range(MB):
                    act.wait_ge(tap_done, it * 12 + 3 * (g + 1))
                    act.activation(u[:, g, :], u[:, g, :], ACT.Silu).then_inc(u_ready, 1)
                act.preload_act_table_set("natural_log_exp_and_others")
                act.wait_ge(par_ready, it + 1)
                act.activation(rows[:], flatb[0:32, 0:TC], ACT.Copy).then_inc(par_kept, 1)
                act.activation(dtin[:], flatb[64:64 + R, 0:TC], ACT.Copy).then_inc(par_kept, 1)
                for g in range(MB):
                    act.wait_ge(dt_ready, it * MB + (g + 1))
                    softplus_act(act, s, flat(r.decay[g % 2]), bdt[:, g:g + 1], it * MB + g, 1)
                act.wait_ge(b_free, it + 1)
                for n in range(0, NS, 2):
                    act.wait_ge(b_spread, it * NS + n + 1)
                    act.activation(brep[:, n, :], flatb[:, 4 * TT:6 * TT], ACT.Copy).then_inc(b_act, 1)
                act.wait_ge(dtu_ready, it * MB + MB)
                act.wait_ge(started, it + 1)

                def pair(g, n2):
                    for j in range(2):
                        un = scan_counts(it, g) + n2 * 2 + j
                        at = n2 * 2 + (g * NS + j)
                        act.wait_ge(r.scan_done, CREDIT + un - 1)
                        act.activation(flat(r.decay[j]), dt[:, g, :], ACT.Exp,
                                       scale=neg_a[:, ds(at, 1)] if not isinstance(at, int)
                                       else neg_a[:, at:at + 1]).then_inc(r.decay_ready, 1)
                        act.wait_ge(r.scan_done, CREDIT + un)
                        if isinstance(at, int) and n2 * 2 + j == 0:
                            continue
                        act.activation(state[:, ds(at + g, 1)] if not isinstance(at, int)
                                       else state[:, at + g:at + g + 1],
                                       r.h[:, 1 - j, 0:1] if bw else r.h[:, 1 - j, TC - 1:TC], ACT.Copy)

                def keep_y(g):
                    act.wait_ge(r.sum_done, CREDIT + scan_counts(it, g) + NS)
                    act.activation(u[:, g, :], flat(r.y), ACT.Copy).then_inc(y_done, 1)

                for g in range(MB):
                    pair(g, 0)
                    if g:
                        keep_y(g - 1)
                    with act.Fori(1, NS // 2) as n2:
                        pair(g, n2)
                    act.wait_ge(r.scan_done, CREDIT + scan_counts(it, g) + NS)
                    last = g * (NS + 1) + NS
                    act.activation(state[:, last:last + 1], r.h[:, 1, 0:1] if bw else r.h[:, 1, TC - 1:TC],
                                   ACT.Copy).then_inc(saved, 1)
                keep_y(MB - 1)
                for g in range(MB):
                    act.wait_ge(z_ready, it * MB + (g + 1))
                    act.activation(dtu[:, g, :], flat(r.decay[g % 2]), ACT.Silu).then_inc(gate_ready, 1)
                act.preload_act_table_set("natural_log_exp_and_others")
                act.wait_ge(centred, it + 1)
                act.activation(sq, res, ACT.Square).then_inc(squared, 1)
                act.wait_ge(var_ready, it + 1)
                act.activation(logv, flat(r.y), ACT.Ln, bias=eps).then_inc(logged, 1)
                act.wait_ge(logged, it + 1)
                act.activation(r0, logv, ACT.Exp, scale=-0.5).then_inc(root_ready, 1)

        @block.vector
        def _(dve):
            dve.memset(wx[:], 0.0).then_inc(cleared, 1)
            dve.memset(one, 1.0)
            dve.memset(eps, EPS)
            dve.memset(carry[:, 0:1], 0.0)
            dve.memset(carry[:, 1:2], 1.0)
            dve.memset(state[:], 0.0).then_inc(y_out, 1)
            dve_credits(dve, r)
            dve.wait_ge(r.scan_done, CREDIT)
            dve.wait_ge(r.prod_ready, CREDIT)
            dve.wait_ge(y_out, 1)
            dve.memset(s.off, 0.0).then_inc(s.soft_done, 1)
            dve.wait_ge(loaded, LOADS)
            dve.wait_ge(ea_ready, 1)
            for g in range(MB):
                dve.tensor_scalar(diag_d[:, g, :], k.ident[:], dcol[:, g:g + 1], None, ALU.mult)
            dve.tensor_scalar(neg_a[:], alog[:], -1.0, None, ALU.mult).then_inc(setup, 1)
            both, b, it, tc, t0 = passes(dve)
            with both:
                for g in range(MB):
                    for t in range(1, KC):
                        if t == 1:
                            dve.wait_ge(tap0, it * MB + (g + 1))
                        else:
                            dve.wait_ge(tap_done, it * 12 + (3 * g + t - 1))
                        x0 = g % 2 * 4 * TT + (PAD - t if bw else t)
                        dve.scalar_tensor_tensor(out=u[:, g, :], in0=flatb[:, x0:x0 + TC], scalar=taps[:, g, t:t + 1],
                                                 in1=u[:, g, :], op0=ALU.mult, op1=ALU.add).then_inc(tap_done, 1)
                dve.wait_ge(par_kept, it * 2 + 1)
                split_rows(dve, split, it, rows[:], parts, None, mid, rest)
                dve.wait_ge(u_ready, it * MB + MB)
                for g in range(MB):
                    softplus_dve(dve, s, dt[:, g, :], it * MB + g)
                    dve.wait_ge(s.soft_done, 1 + it * MB + (g + 1))
                    dve.tensor_tensor(dtu[:, g, :], dt[:, g, :], u[:, g, :], ALU.mult).then_inc(dtu_ready, 1)
                dve.wait_ge(b_free, it + 1)
                for n in range(1, NS, 2):
                    dve.wait_ge(b_spread, it * NS + n + 1)
                    dve.tensor_copy(brep[:, n, :], flatb[:, 6 * TT:8 * TT]).then_inc(b_dve, 1)
                dve.wait_ge(y_out, it + 1)
                dve.tensor_scalar(state[:], state[:], carry[:, ds(tc, 1)], None, ALU.mult).then_inc(started, 1)
                for g in range(MB):
                    dve_scans(dve, r, it, g, state, 1 + g * (NS + 1), reverse=bw, state_set=None if g else started)
                for g in range(MB):
                    dve.wait_ge(gate_ready, it * MB + (g + 1))
                    dve.wait_ge(y_done, it * MB + (g + 1))
                    dve.tensor_tensor(u[:, g, :], u[:, g, :], dtu[:, g, :], ALU.mult).then_inc(gated, 1)
                dve.wait_ge(out_ready, it + 1)
                xnow = k.xn[:, :, b, ds(t0 + PAD, TC)]
                dve.tensor_tensor(res, r.banks[:, 0:4, :].rearrange("p (c q) t -> p c (q t)", c=C), xnow,
                                  ALU.add).then_inc(summed, 1)
                dve.wait_ge(summed, it + 1)
                dve.wait_ge(mean_ready, it + 1)
                for c in range(C):
                    ins = dve.tensor_tensor(res[:, c, :], res[:, c, :], flat(r.chat), ALU.subtract)
                ins.then_inc(centred, 1)
                dve.wait_ge(root_ready, it + 1)
                dve.scalar_tensor_tensor(out=ra, in0=flat(r.y), scalar=EPS, in1=r0, op0=ALU.add,
                                         op1=ALU.mult).then_inc(newton, 1)
                dve.wait_ge(newton, it * 3 + 1)
                dve.scalar_tensor_tensor(out=rb, in0=ra, scalar=-0.5, in1=r0, op0=ALU.mult,
                                         op1=ALU.mult).then_inc(newton, 1)
                dve.wait_ge(newton, it * 3 + 2)
                dve.scalar_tensor_tensor(out=rstd, in0=rb, scalar=1.5, in1=r0, op0=ALU.add,
                                         op1=ALU.mult).then_inc(newton, 1)
                dve.wait_ge(newton, it * 3 + 3)
                for c in range(C):
                    dve.tensor_tensor(res[:, c, :], res[:, c, :], rstd, ALU.mult).then_inc(scaled, 1)
                n_scaled = 6 if bw else 4
                for c in range(C):
                    dve.wait_ge(scaled, it * n_scaled + (c + 1))
                    dve.tensor_scalar(res[:, c, :], res[:, c, :], norm[:, 0, c:c + 1], norm[:, 1, c:c + 1],
                                      ALU.mult, ALU.add).then_inc(scaled, 1)
                dve.wait_ge(scaled, it * n_scaled + 4)
                if bw:
                    dve.wait_ge(yf_loaded, it * 16 + 16)
                    for c in range(C):
                        dve.tensor_tensor(res[:, c, :], res[:, c, :], yf[:, c, :], ALU.add).then_inc(scaled, 1)
                    dve.wait_ge(scaled, it * n_scaled + 6)
                dve.memset(consts[:, 0:1], 1.0).then_inc(y_out, 1)

        @block.tensor
        def _(pe):
            pe.sem_inc(r.sum_done, CREDIT)
            pe.wait_ge(loaded, LOADS)
            pe.wait_ge(setup, 1)
            both, b, it, tc, t0 = passes(pe)
            with both:
                pe.wait_ge(y_out, it + 1)
                for g in range(MB):
                    bank = g % 2 * 4
                    if g > 1:
                        pe.wait_ge(tap_done, it * 12 + 3 * (g - 1))
                    for q, n in ((0, TT), (1, TT), (2, PAD)):
                        for c in range(C):
                            mm = pe.matmul(r.banks[:, bank + q, 0:n], win[:, c, g * P:(g + 1) * P],
                                           k.xn[:, c, b, ds(t0 + ((PAD if bw else 0) + q * TT), n)],
                                           start=c == 0, stop=c == C - 1)
                    mm.then_inc(xi_ready, 1)
                pe.wait_ge(u_ready, it * MB + MB)
                for q in range(2):
                    for g in range(MB):
                        mm = pe.matmul(r.banks[0:64 + R, q, :], wx[:, g, :], u[:, g, q * TT:(q + 1) * TT],
                                       start=g == 0, stop=g == MB - 1)
                mm.then_inc(par_ready, 1)
                pe.wait_ge(par_kept, it * 2 + 2)
                for g in range(MB):
                    if g > 1:
                        pe.wait_ge(s.log_done, it * MB + (g - 1))
                    for q in range(2):
                        mm = pe.matmul(r.decay[g % 2][:, q, :], wdt[:, g * P:(g + 1) * P],
                                       dtin[:, q * TT:(q + 1) * TT], start=True, stop=True)
                    mm.then_inc(dt_ready, 1)
                pe.wait_ge(split, it * 5 + 5)
                for n in range(NS):
                    if n > 1:
                        pe.wait_ge(b_act if n % 2 == 0 else b_dve, it * 8 + n // 2)
                    for q in range(2):
                        mm = pe.matmul(r.banks[:, 4 + n % 2 * 2 + q, :], k.sel[:, n, :],
                                       parts[:, q * TT:(q + 1) * TT], start=True, stop=True)
                    mm.then_inc(b_spread, 1)
                pe.wait_ge(b_act, it * 8 + 8)
                pe.wait_ge(b_dve, it * 8 + 8)
                for g in range(MB):
                    if g:
                        pe.wait_ge(y_done, it * MB + g)
                    for q in range(2):
                        pe.matmul(r.y[:, q, :], diag_d[:, g, :], u[:, g, q * TT:(q + 1) * TT], start=True, stop=True,
                                  skip_group_check=True)
                    pe_sums(pe, r, it, g, lambda j: k.ident[:],
                            lambda n: k.sel[:, NS + n, :] if isinstance(n, int) else k.sel[:, ds(n + NS, 1), :],
                            parts)
                for g in range(MB):
                    if g > 1:
                        pe.wait_ge(gate_ready, it * MB + (g - 1))
                    for q in range(2):
                        for c in range(C):
                            mm = pe.matmul(r.decay[g % 2][:, q, :], win[:, c, D2 + g * P:D2 + (g + 1) * P],
                                           k.xn[:, c, b, ds(t0 + (PAD + q * TT), TT)], start=c == 0, stop=c == C - 1)
                    mm.then_inc(z_ready, 1)
                pe.wait_ge(gated, it * MB + MB)
                for c in range(C):
                    for q in range(2):
                        for g in range(MB):
                            mm = pe.matmul(r.banks[:, 2 * c + q, :], wout[:, g, c * P:(c + 1) * P],
                                           u[:, g, q * TT:(q + 1) * TT], start=g == 0, stop=g == MB - 1)
                mm.then_inc(out_ready, 1)
                pe.wait_ge(summed, it + 1)
                for q in range(2):
                    for c in range(C):
                        mm = pe.matmul(r.chat[:, q, :], k.mean[:], res[:, c, q * TT:(q + 1) * TT],
                                       start=c == 0, stop=c == C - 1)
                mm.then_inc(mean_ready, 1)
                pe.wait_ge(squared, it + 1)
                for q in range(2):
                    for c in range(C):
                        mm = pe.matmul(r.y[:, q, :], k.mean[:], sq[:, c, q * TT:(q + 1) * TT],
                                       start=c == 0, stop=c == C - 1)
                mm.then_inc(var_ready, 1)


H = 1024
HB = H // P
LANE = 7
ACROSS = 3


def butterfly(nc, k, tag, x, spare, width, own, cross, upward):
    with ExitStack() as ctx:
        m = Mem(nc, ctx, tag)
        swap, mat = m.sb("swap", [P, LANE, P]), m.sb("mat", [P, 2, P])
        banks = m.ps("banks", [P, 2, TT])
        swapped, half, mat_ready = m.sem("swapped"), m.sem("half"), m.sem("mat_ready")
        turned, kept, scaled, crossed, ready = m.sem("turned"), m.sem("kept"), m.sem("scaled"), m.sem("crossed"), m.sem("ready")
        first = 0 if upward else ACROSS
        start_across = LANE if upward else 0
        block = ctx.enter_context(nc.Block())

        def across(dve):
            a, b = x, spare
            for n in range(ACROSS):
                st = start_across + n
                stride = 1 << (n if upward else ACROSS - 1 - n)
                if n:
                    dve.wait_ge(crossed, n * HB)
                for j in range(HB):
                    dve.tensor_scalar(b[:, j, 0:width], a[:, j, 0:width], own[:, st, j:j + 1], None, ALU.mult).then_inc(scaled, 1)
                for j in range(HB):
                    dve.wait_ge(scaled, n * HB + j + 1)
                    dve.scalar_tensor_tensor(out=b[:, j, 0:width], in0=a[:, j ^ stride, 0:width], scalar=cross[:, st, j:j + 1],
                                             in1=b[:, j, 0:width], op0=ALU.mult, op1=ALU.add).then_inc(crossed, 1)
                a, b = b, a
            dve.wait_ge(crossed, ACROSS * HB)
            dve.tensor_copy(x[:], spare[:]).then_inc(ready, 1)

        @block.vector
        def _(dve):
            for n in range(LANE):
                s = 1 << (n if upward else LANE - 1 - n)
                for side in range(2):
                    ins = dve.tensor_copy(swap[:, n, :].rearrange("p (a two s) -> p a two s", two=2, s=s)[:, :, side, :],
                                          k.ident[:].rearrange("p (a two s) -> p a two s", two=2, s=s)[:, :, 1 - side, :])
            ins.then_inc(swapped, 1)
            if not upward:
                across(dve)
            dve.wait_ge(swapped, 1)
            with dve.Fori(0, LANE) as n:
                for j in range(HB):
                    i = n * HB + j
                    dve.wait_ge(turned, i + 1)
                    dve.tensor_scalar(mat[:, j % 2, :], k.ident[:], own[:, ds(n + first, 1), j], None,
                                      ALU.mult).then_inc(half, 1)
                    dve.wait_ge(half, i + 1)
                    dve.scalar_tensor_tensor(out=mat[:, j % 2, :], in0=swap[:, ds(n, 1), :].rearrange("p n q -> p (n q)"),
                                             scalar=cross[:, ds(n + first, 1), j], in1=mat[:, j % 2, :], op0=ALU.mult,
                                             op1=ALU.add).then_inc(mat_ready, 1)
            if upward:
                dve.wait_ge(kept, 2 + LANE * HB)
                across(dve)

        @block.tensor
        def _(pe):
            pe.sem_inc(turned, 2)
            if not upward:
                pe.wait_ge(ready, 1)
            with pe.Fori(0, LANE) as n:
                for j in range(HB):
                    i = n * HB + j
                    pe.wait_ge(mat_ready, i + 1)
                    pe.wait_ge(kept, i + 1)
                    pe.matmul(banks[:, j % 2, 0:width], mat[:, j % 2, :], x[:, j, 0:width], start=True,
                              stop=True).then_inc(turned, 1)

        @block.scalar
        def _(act):
            act.sem_inc(kept, 2)
            with act.Fori(0, LANE) as n:
                for j in range(HB):
                    i = n * HB + j
                    act.wait_ge(turned, 2 + (i + 1))
                    act.activation(x[:, j, 0:width], banks[:, j % 2, 0:width], ACT.Copy).then_inc(kept, 1)


def last(nc, k, out):
    FF = 512
    FB = FF // P
    a = k.a
    W = E + 1
    with ExitStack() as keep:
        mk = Mem(nc, keep, "fin")
        up, down = mk.sb("up", [P, HB, W]), mk.sb("down", [P, HB, W])
        up_b, w_up = mk.sb("up_b", [P, HB]), mk.sb("w_up", [P, C, H])
        w1, w2, b1 = mk.sb("w1", [P, C, FF]), mk.sb("w2", [P, FB, E]), mk.sb("b1", [P, FB])
        vec = mk.sb("vec", [P, 5, C])
        add_b = mk.sb("add_b", [P, C])
        with ExitStack() as ctx:
            m = Mem(nc, ctx, "fina")
            spare = m.sb("spare", [P, HB, W])
            fac = m.sb("fac", [P, 4, LANE + ACROSS, HB])
            with ExitStack() as ctx2:
                loaded = Mem(nc, ctx2, "finl").sem("loaded")
                filled = Mem(nc, ctx2, "finl").sem("filled")
                block = ctx2.enter_context(nc.Block())

                @block.sync
                def _(sp):
                    sp.wait_ge(filled, 1)
                    n = 0
                    for dst, src in ((up[:], a["exp"].rearrange("(j p) e -> p j e", p=P)), (down[:, :, 0:E], a["W_con"].rearrange("(j p) e -> p j e", p=P)),
                                     (fac[:], a["factors"]), (up_b[:], a["up_bias"]),
                                     (w1[:], a["W1"].rearrange("(c p) m -> p c m", p=P)),
                                     (w2[:], a["W2"].rearrange("(c p) m -> p c m", p=P)), (b1[:], a["b1"]),
                                     (vec[:], a["vec"])):
                        sp.dma_start(dst, src).then_inc(loaded, 16)
                        n += 16
                    sp.wait_ge(loaded, n)

                @block.vector
                def _(dve):
                    dve.memset(down[:, :, E:W], 0.0)
                    dve.memset(spare[:, :, E:W], 0.0).then_inc(filled, 1)
            butterfly(nc, k, "bup", up, spare, W, fac[:, 0], fac[:, 1], True)
            butterfly(nc, k, "bdn", down, spare, E, fac[:, 2], fac[:, 3], False)

        with ExitStack() as ctx:
            m = Mem(nc, ctx, "finb")
            y, x1 = m.sb("y", [P, 2, C, TT]), m.sb("x1", [P, 2, C, TT])
            f, g = m.sb("f", [P, FB, TT]), m.sb("g", [P, HB, TT])
            res, sq, o = m.sb("res", [P, C, TT]), m.sb("sq", [P, C, TT]), m.sb("o", [P, 2, C, TT])
            logv, r0, ra, rb, rstd = (m.sb(n, [P, TT]) for n in ("logv", "r0", "ra", "rb", "rstd"))
            eps = m.sb("eps", [P, 1])
            banks = m.ps("banks", [P, 8, TT])
            (turned, w_ready, f_ready, f_kept, ff_ready, summed, up_ready, g_ready, mean_ready, centred, squared, var_ready,
             logged, root_ready, newton, step, down_ready, o_ready) = (m.sem(n) for n in (
                 "turned w_ready f_ready f_kept ff_ready summed up_ready g_ready mean_ready centred squared var_ready "
                 "logged root_ready newton step down_ready o_ready").split())
            loaded = [m.sem(f"loaded{j}") for j in range(2)]
            stored = [m.sem(f"stored{j}") for j in range(2)]
            slot_free = m.sem("slot_free")
            NT = T // TT
            STEPS = 8
            block = ctx.enter_context(nc.Block())

            @block.sync
            def _(sp):
                yd, xd, od = (v.rearrange("(c p) t -> p c t", p=P) for v in (k.y, k.x1, out))
                with sp.Fori(0, NT // 2) as i2:
                    for j in range(2):
                        i = i2 * 2 + j
                        sp.wait_ge(o_ready, i + 1)
                        sp.dma_start(y[:, j], yd[:, :, ds(i * TT, TT)]).then_inc(loaded[j], 16)
                        sp.dma_start(x1[:, j], xd[:, :, ds(i * TT, TT)]).then_inc(loaded[j], 16)

            @block.gpsimd
            def _(pool):
                od = out.rearrange("(c p) t -> p c t", p=P)
                pool.sem_inc(slot_free, 1)
                with pool.Fori(0, NT // 2) as i2:
                    for j in range(2):
                        i = i2 * 2 + j
                        pool.wait_ge(o_ready, 2 + (i + 1))
                        pool.dma_start(od[:, :, ds(i * TT, TT)], o[:, j]).then_inc(stored[j], 16)
                        pool.wait_ge(stored[j], i2 * 16 + 16)
                        pool.sem_inc(slot_free, 1)

            @block.tensor
            def _(pe):
                for j in range(HB):
                    for c in range(C):
                        n = j * C + c
                        if n >= 4:
                            pe.wait_ge(w_ready, n - 3)
                        pe.transpose(banks[:, n % 4, 0:P], up[:, j, c * P:(c + 1) * P], k.ident[:]).then_inc(turned, 1)
                pe.wait_ge(w_ready, HB * C)
                with pe.Fori(0, NT // 2) as i2:
                    for j in range(2):
                        i = i2 * 2 + j
                        pe.wait_ge(loaded[j], i2 * 32 + 32)
                        pe.wait_ge(o_ready, 2 + i)
                        for h in range(FB):
                            for c in range(C):
                                mm = pe.matmul(banks[:, h, :], w1[:, c, h * P:(h + 1) * P], y[:, j, c, :],
                                               start=c == 0, stop=c == C - 1)
                            mm.then_inc(f_ready, 1)
                        for h in range(FB):
                            pe.wait_ge(f_kept, i * FB + (h + 1))
                        for c in range(C):
                            for h in range(FB):
                                mm = pe.matmul(banks[:, 6 + c, :], w2[:, h, c * P:(c + 1) * P], f[:, h, :],
                                               start=h == 0, stop=h == FB - 1)
                        mm.then_inc(ff_ready, 1)

                        def up_block(h):
                            if h >= 4:
                                pe.wait_ge(g_ready, i * HB + (h - 3))
                            for c in range(C):
                                mm = pe.matmul(banks[:, h % 4, :], w_up[:, c, h * P:(h + 1) * P],
                                               xnow(c, i2, j), start=c == 0, stop=c == C - 1)
                            mm.then_inc(up_ready, 1)

                        def xnow(c, i2, j):
                            return k.xn[:, c, :, :].rearrange("p b t -> p (b t)")[
                                :, ds(i2 * (2 * TT) + (i2 // 2) * (2 * PAD) + (j * TT + PAD), TT)]

                        for h in range(4):
                            up_block(h)
                        pe.wait_ge(summed, i + 1)
                        for c in range(C):
                            mm = pe.matmul(banks[:, 6, :], k.mean[:], res[:, c, :], start=c == 0, stop=c == C - 1)
                        mm.then_inc(mean_ready, 1)
                        for h in range(4, HB):
                            up_block(h)
                        pe.wait_ge(squared, i + 1)
                        for c in range(C):
                            mm = pe.matmul(banks[:, 7, :], k.mean[:], sq[:, c, :], start=c == 0, stop=c == C - 1)
                        mm.then_inc(var_ready, 1)
                        for h in range(HB):
                            pe.wait_ge(g_ready, i * HB + (h + 1))
                            for c in range(C):
                                mm = pe.matmul(banks[:, 4 + c, :], down[:, h, c * P:(c + 1) * P], g[:, h, :],
                                               start=h == 0, stop=h == HB - 1)
                        mm.then_inc(down_ready, 1)

            @block.scalar
            def _(act):
                act.wait_ge(w_ready, HB * C)
                with act.Fori(0, NT) as i:
                    for h in range(FB):
                        act.wait_ge(f_ready, i * FB + (h + 1))
                        act.activation(f[:, h, :], banks[:, h, :], ACT.Relu, bias=b1[:, h:h + 1]).then_inc(f_kept, 1)

                    def gelu(h):
                        act.wait_ge(up_ready, i * HB + (h + 1))
                        act.activation(g[:, h, :], banks[:, h % 4, :], ACT.Gelu, bias=up_b[:, h:h + 1]).then_inc(g_ready, 1)

                    for h in range(4):
                        gelu(h)
                    act.wait_ge(centred, i + 1)
                    act.activation(sq[:], res[:], ACT.Square).then_inc(squared, 1)
                    for h in range(4, HB):
                        gelu(h)
                    act.preload_act_table_set("natural_log_exp_and_others")
                    act.wait_ge(var_ready, i + 1)
                    act.activation(logv[:], banks[:, 7, :], ACT.Ln, bias=eps[:, 0:1]).then_inc(logged, 1)
                    act.wait_ge(logged, i + 1)
                    act.activation(r0[:], logv[:], ACT.Exp, scale=-0.5).then_inc(root_ready, 1)

            @block.vector
            def _(dve):
                dve.memset(eps[:], EPS)
                for j in range(HB):
                    for c in range(C):
                        n = j * C + c
                        dve.wait_ge(turned, n + 1)
                        dve.tensor_copy(w_up[:, c, j * P:(j + 1) * P], banks[:, n % 4, 0:P]).then_inc(w_ready, 1)
                dve.tensor_tensor(up_b[:], up_b[:], up[:, :, E:W].rearrange("p j o -> p (j o)"), ALU.add)
                dve.tensor_tensor(add_b[:], vec[:, 3, :], vec[:, 4, :], ALU.add).then_inc(o_ready, 2)
                dve.wait_ge(o_ready, 2)
                with dve.Fori(0, NT // 2) as i2:
                    for j in range(2):
                        i = i2 * 2 + j
                        dve.wait_ge(ff_ready, i + 1)
                        dve.wait_ge(loaded[j], i2 * 32 + 32)
                        for c in range(C):
                            ins = dve.scalar_tensor_tensor(out=res[:, c, :], in0=banks[:, 6 + c, :], scalar=vec[:, 0, c:c + 1],
                                                           in1=y[:, j, c, :], op0=ALU.add, op1=ALU.add)
                        ins.then_inc(summed, 1)
                        dve.wait_ge(summed, i + 1)
                        dve.wait_ge(mean_ready, i + 1)
                        for c in range(C):
                            ins = dve.tensor_tensor(res[:, c, :], res[:, c, :], banks[:, 6, :], ALU.subtract)
                        ins.then_inc(centred, 1)
                        dve.wait_ge(root_ready, i + 1)
                        dve.scalar_tensor_tensor(out=ra[:], in0=banks[:, 7, :], scalar=EPS, in1=r0[:], op0=ALU.add,
                                                 op1=ALU.mult).then_inc(newton, 1)
                        dve.wait_ge(newton, i * 3 + 1)
                        dve.scalar_tensor_tensor(out=rb[:], in0=ra[:], scalar=-0.5, in1=r0[:], op0=ALU.mult,
                                                 op1=ALU.mult).then_inc(newton, 1)
                        dve.wait_ge(newton, i * 3 + 2)
                        dve.scalar_tensor_tensor(out=rstd[:], in0=rb[:], scalar=1.5, in1=r0[:], op0=ALU.add,
                                                 op1=ALU.mult).then_inc(newton, 1)
                        dve.wait_ge(newton, i * 3 + 3)
                        for c in range(C):
                            dve.tensor_tensor(res[:, c, :], res[:, c, :], rstd[:], ALU.mult).then_inc(step, 1)
                        for c in range(C):
                            dve.wait_ge(step, i * STEPS + (c + 1))
                            dve.tensor_scalar(res[:, c, :], res[:, c, :], vec[:, 1, c:c + 1], vec[:, 2, c:c + 1],
                                              ALU.mult, ALU.add).then_inc(step, 1)
                        for c in range(C):
                            dve.wait_ge(step, i * STEPS + (3 + c))
                            dve.tensor_tensor(res[:, c, :], res[:, c, :], x1[:, j, c, :], ALU.add).then_inc(step, 1)
                        dve.wait_ge(down_ready, i + 1)
                        dve.wait_ge(slot_free, i + 1)
                        for c in range(C):
                            dve.wait_ge(step, i * STEPS + (5 + c))
                            ins = dve.scalar_tensor_tensor(out=o[:, j, c, :], in0=banks[:, 4 + c, :], scalar=add_b[:, c:c + 1],
                                                           in1=res[:, c, :], op0=ALU.add, op1=ALU.add)
                            ins.then_inc(step, 1)
                        dve.wait_ge(step, i * STEPS + 8)
                        dve.memset(eps[:], EPS).then_inc(o_ready, 1)


class Kept:
    pass


def program(nc, a, out):
    Mem.used = []
    with ExitStack() as ctx:
        m = Mem(nc, ctx, "kept")
        k = Kept()
        k.ident = m.sb("ident", [P, P])
        k.mean = m.sb("mean", [P, P])
        k.sel = m.sb("sel", [96, 32, P], BF16)
        k.xn = m.sb("xn", [P, C, B, LP])
        k.a = a
        k.x1 = nc.dram_tensor("x1_scratch", (E, T), F32, kind="Internal").ap()
        k.y = nc.dram_tensor("mixer_scratch", (E, T), F32, kind="Internal").ap()
        constants(nc, k)
        with ExitStack() as first:
            acc = Mem(nc, first, "first").sb("acc", [P, C, T])
            layernorm(nc, k, acc, a["xT"])
            mixer0(nc, k, acc)
            experts0(nc, k, acc)
            layernorm(nc, k, acc, save=k.x1)
        clear_semaphores(nc)
        mixer1(nc, k, "fw", k.y)
        mixer1(nc, k, "bw", k.y)
        last(nc, k, out)


def _factors(w, upward):
    import numpy as np

    i = np.arange(H)
    own, cross = [], []
    for stage in range(LANE + ACROSS):
        s = 1 << stage
        bit, pair = i // s % 2, i // (2 * s) * s + i % s
        own.append(w[stage, pair, bit, bit])
        leaves = w[stage, pair, 1 - bit, bit]
        arrives = w[stage, pair, bit, 1 - bit]
        cross.append(leaves if (stage < LANE) == upward else arrives)
    order = list(range(LANE + ACROSS)) if upward else list(range(LANE + ACROSS))[::-1]
    return [np.stack([v[n].reshape(HB, P).T for n in order], axis=1) for v in (own, cross)]


def _laid_out(i):
    import numpy as np

    def arr(name):
        return np.asarray(i[name])

    def cols(name):
        return arr(name).reshape(-1, P).T

    a = {"xT": arr("L0_attn_x").transpose(2, 0, 1).reshape(E, T),
         "W_z": arr("L0_attn_W_z").T, "W_out": arr("L0_attn_W_out").T, "W_par": arr("L0_attn_W_params").T,
         "W_dt": arr("L0_attn_W_dt").T, "conv_w": arr("L0_attn_conv_w")[:, 0], "b_dt": cols("L0_attn_b_dt"),
         "A_log": arr("L0_attn_A_log"), "D": cols("L0_attn_D"),
         "controller": arr("L0_ffn_controller").reshape(E, -1), "f1": arr("L0_ffn_f1").reshape(E, 64, 64),
         "f2": arr("L0_ffn_f2").reshape(64, 64, E), "bias": arr("L0_ffn_bias").reshape(64, 64).T,
         "tie": np.broadcast_to(np.linspace(0.0, 1e-6, 16, dtype=np.float32), (P, 32, 16))}
    for way in ("fw", "bw"):
        for w in ("Win", "Wout", "Wx", "Wdt", "convw", "Alog"):
            a[f"{way}_{w}"] = arr(f"L1_attn_{way}_{w}")
        for w in ("convb", "bdt", "D"):
            a[f"{way}_{w}"] = cols(f"L1_attn_{way}_{w}")
    for w in ("fwn", "fin"):
        a[w] = np.stack([cols(f"L1_attn_{w}_w"), cols(f"L1_attn_{w}_b")], axis=1)
    a["W1"], a["W2"] = arr("L1_attn_ff_W1"), arr("L1_attn_ff_W2")
    a["b1"] = cols("L1_attn_ff_b1")
    a["vec"] = np.stack([cols(n) for n in ("L1_attn_ff_b2", "L1_attn_fin_w", "L1_attn_fin_b", "L1_ffn_b_con",
                                           "L1_ffn_down_bias")], axis=1)
    a["exp"] = np.concatenate([arr("L1_ffn_W_exp").T, arr("L1_ffn_b_exp")[:, None]], axis=1)
    a["W_con"], a["up_bias"] = arr("L1_ffn_W_con"), cols("L1_ffn_up_bias")
    a["factors"] = np.stack(_factors(arr("L1_ffn_up_weights"), True) + _factors(arr("L1_ffn_down_weights"), False),
                            axis=1)
    return {n: np.ascontiguousarray(v) for n, v in a.items()}


def kernel(**inputs):
    import concourse.bacc as _bacc
    from concourse.bass_utils import run_bass_kernel_spmd as _run

    nc = _bacc.Bacc("TRN2", target_bir_lowering=False, num_devices=1)
    arrays = _laid_out(inputs)
    args = {n: nc.dram_tensor(n, v.shape, mybir.dt.from_np(v.dtype), kind="ExternalInput").ap()
            for n, v in arrays.items()}
    out = nc.dram_tensor("out", (E, T), F32, kind="ExternalOutput").ap()
    program(nc, args, out)
    r = _run(nc, [arrays], core_ids=[0])
    return r.results[0]["out"].reshape(E, B, L).transpose(1, 2, 0)
```

```python
from contextlib import ExitStack

import concourse.bass as bass
from concourse import mybir

ALU = mybir.AluOpType
ACT = mybir.ActivationFunctionType
F32 = mybir.dt.float32
BF16 = mybir.dt.bfloat16
AX = mybir.AxisListType

P = 128
E = 256
C = E // P
B = 2
L = 2048
T = B * L
TT = 512
TC = 1024
NS = 16
KC = 4
PAD = KC - 1
LP = L + 2 * PAD
GROUPS = 4
UNITS = GROUPS * NS
CREDIT = 2
EPS = 1e-5
ds = bass.ds


class Mem:

    used = []

    def __init__(self, nc, ctx, tag):
        self.nc, self.ctx, self.tag = nc, ctx, tag

    def sb(self, name, shape, dt=F32):
        return self.ctx.enter_context(self.nc.sbuf_tensor(f"{self.tag}_{name}", shape, dt))

    def ps(self, name, shape, dt=F32):
        return self.ctx.enter_context(self.nc.psum_tensor(f"{self.tag}_{name}", shape, dt))

    def sem(self, name):
        Mem.used.append(self.nc.alloc_semaphore(name=f"{self.tag}_{name}"))
        return Mem.used[-1]


def clear_semaphores(nc):
    nc.clear_and_free_semaphores(Mem.used)
    nc.all_engine_barrier()
    Mem.used = []


def constants(nc, k):
    with ExitStack() as ctx:
        m = Mem(nc, ctx, "const")
        zeroed, step = m.sem("zeroed"), m.sem("step")
        block = ctx.enter_context(nc.Block())

        @block.vector
        def _(dve):
            dve.memset(k.mean[:], 1.0 / E)
            dve.memset(k.xn[:, :, :, 0:PAD], 0.0)
            dve.memset(k.xn[:, :, :, PAD + L:LP], 0.0).then_inc(zeroed, 1)

        @block.gpsimd
        def _(pool):
            pool.memset(k.ident[:], 0.0).then_inc(step, 1)
            pool.memset(k.sel[:], 0.0).then_inc(step, 1)
            pool.wait_ge(step, 2)
            pool.affine_select(out=k.ident[:], in_=k.ident[:], compare_op=ALU.not_equal, fill=1.0,
                               base=0, pattern=[[-1, P]], channel_multiplier=1).then_inc(step, 1)
            for part in range(3):
                pool.wait_ge(step, 3 + part)
                pool.affine_select(out=k.sel[:], in_=k.sel[:], compare_op=ALU.not_equal, fill=1.0,
                                   base=-32 * part, pattern=[[-1, 32], [0, P]],
                                   channel_multiplier=1).then_inc(step, 1)


def layernorm(nc, k, src, load=None, save=None):
    with ExitStack() as ctx:
        m = Mem(nc, ctx, "ln" if load is not None else "ln1")
        stat = m.ps("mean", [P, TT])
        var = m.ps("var", [P, TT])
        sq = m.sb("sq", [P, C, TT])
        logv = m.sb("logv", [P, TT])
        r0 = m.sb("r0", [P, TT])
        ra, rb, rstd = m.sb("ra", [P, TT]), m.sb("rb", [P, TT]), m.sb("rstd", [P, TT])
        epst = m.sb("eps", [P, 1])
        eps_set = m.sem("eps_set")
        loaded, mean_ready, centred = m.sem("loaded"), m.sem("mean_ready"), m.sem("centred")
        squared, var_ready, root_ready = m.sem("squared"), m.sem("var_ready"), m.sem("root_ready")
        logged, newton, normed = m.sem("logged"), m.sem("newton"), m.sem("normed")
        PB = L // TT
        block = ctx.enter_context(nc.Block())

        @block.sync
        def _(sp):
            if load is not None:
                for b in range(B):
                    for q in range(PB):
                        sp.dma_start(src[:, :, b * L + q * TT:b * L + (q + 1) * TT],
                                     load[:, b * L + q * TT:b * L + (q + 1) * TT]
                                     .rearrange("(c p) t -> p c t", p=P)).then_inc(loaded, 16)
                sp.wait_ge(loaded, 16 * B * PB)
            if save is not None:
                sp.dma_start(save.rearrange("(c p) t -> p c t", p=P), src[:]).then_inc(loaded, 16)
                sp.wait_ge(loaded, 16)

        @block.tensor
        def _(pe):
            if load is not None:
                pe.wait_ge(loaded, 16 * B * PB)
            with pe.Fori(0, B) as b, pe.Fori(0, PB) as q:
                i = b * PB + q
                pe.wait_ge(normed, i + 1)
                for c in range(C):
                    mm = pe.matmul(stat[:], k.mean[:], src[:, c, ds(b * L + q * TT, TT)],
                                   start=c == 0, stop=c == C - 1)
                mm.then_inc(mean_ready, 1)
                pe.wait_ge(squared, i + 1)
                for c in range(C):
                    mm = pe.matmul(var[:], k.mean[:], sq[:, c, :], start=c == 0, stop=c == C - 1)
                mm.then_inc(var_ready, 1)

        @block.scalar
        def _(act):
            act.preload_act_table_set("natural_log_exp_and_others")
            act.wait_ge(eps_set, 1)
            with act.Fori(0, B) as b, act.Fori(0, PB) as q:
                i = b * PB + q
                act.wait_ge(centred, i + 1)
                act.activation(sq[:], k.xn[:, :, b, ds(PAD + q * TT, TT)], ACT.Square).then_inc(squared, 1)
                act.wait_ge(var_ready, i + 1)
                act.activation(logv[:], var[:], ACT.Ln, bias=epst[:, 0:1]).then_inc(logged, 1)
                act.wait_ge(logged, i + 1)
                act.activation(r0[:], logv[:], ACT.Exp, scale=-0.5).then_inc(root_ready, 1)

        @block.vector
        def _(dve):
            dve.memset(epst[:], EPS).then_inc(eps_set, 1)
            dve.memset(ra[:], 0.0).then_inc(normed, 1)
            dve.wait_ge(normed, 1)
            with dve.Fori(0, B) as b, dve.Fori(0, PB) as q:
                i = b * PB + q
                dve.wait_ge(mean_ready, i + 1)
                for c in range(C):
                    ins = dve.tensor_tensor(k.xn[:, c, b, ds(PAD + q * TT, TT)],
                                            src[:, c, ds(b * L + q * TT, TT)], stat[:], ALU.subtract)
                ins.then_inc(centred, 1)
                dve.wait_ge(root_ready, i + 1)
                dve.scalar_tensor_tensor(out=ra[:], in0=var[:], scalar=EPS, in1=r0[:], op0=ALU.add,
                                         op1=ALU.mult).then_inc(newton, 1)
                dve.wait_ge(newton, i * 3 + 1)
                dve.scalar_tensor_tensor(out=rb[:], in0=ra[:], scalar=-0.5, in1=r0[:], op0=ALU.mult,
                                         op1=ALU.mult).then_inc(newton, 1)
                dve.wait_ge(newton, i * 3 + 2)
                dve.scalar_tensor_tensor(out=rstd[:], in0=rb[:], scalar=1.5, in1=r0[:], op0=ALU.add,
                                         op1=ALU.mult).then_inc(newton, 1)
                dve.wait_ge(newton, i * 3 + 3)
                for c in range(C):
                    xs = k.xn[:, c, b, ds(PAD + q * TT, TT)]
                    ins = dve.tensor_tensor(xs, xs, rstd[:], ALU.mult)
                ins.then_inc(normed, 1)


def scan_counts(it, g):
    return it * UNITS + g * NS


class ScanRing:

    def __init__(self, m):
        banks = m.ps("banks", [P, 8, TT])
        self.banks = banks
        self.decay = [banks[:, 2 * j:2 * j + 2, :] for j in range(2)]
        self.chat = banks[:, 4:6, :]
        self.y = banks[:, 6:8, :]
        self.drive = m.sb("drive", [P, 2, TC])
        self.h = m.sb("h", [P, 2, TC])
        self.prod = m.sb("prod", [P, 2, TC])
        self.decay_ready = m.sem("decay_ready")
        self.drive_ready = m.sem("drive_ready")
        self.scan_done = m.sem("scan_done")
        self.prod_ready = m.sem("prod_ready")
        self.chat_ready = m.sem("chat_ready")
        self.sum_done = m.sem("sum_done")


def flat(ap):
    return ap.rearrange("p a t -> p (a t)")


def dve_credits(dve, r):
    dve.memset(r.h[:], 0.0).then_inc(r.scan_done, CREDIT)
    dve.memset(r.prod[:], 0.0).then_inc(r.prod_ready, CREDIT)


def dve_scans(dve, r, it, g, state, col, reverse=False, state_set=None):
    step = slice(None, None, -1) if reverse else slice(None)
    with dve.Fori(0, NS // 2) as n2:
        for j in range(2):
            u = scan_counts(it, g) + n2 * 2 + j
            if state_set is not None and j == 0:
                dve.wait_ge(state_set, it + 1)
            dve.wait_ge(r.decay_ready, u + 1)
            dve.wait_ge(r.drive_ready, u + 1)
            dve.wait_ge(r.prod_ready, CREDIT + u - 1)
            dve.tensor_tensor_scan(r.h[:, j, step], flat(r.decay[j])[:, step], r.drive[:, j, step],
                                   state[:, ds(col + n2 * 2 + j, 1)], ALU.mult,
                                   ALU.add).then_inc(r.scan_done, 1)
            dve.wait_ge(r.scan_done, CREDIT + u + 1)
            dve.wait_ge(r.chat_ready, u + 1)
            dve.wait_ge(r.sum_done, CREDIT + u - 1)
            dve.tensor_tensor(r.prod[:, j, :], flat(r.chat), r.h[:, j, :],
                              ALU.mult).then_inc(r.prod_ready, 1)


def pe_sums(pe, r, it, g, weight, selector, parts):

    def spread(u, n):
        for q in range(2):
            mm = pe.matmul(r.chat[:, q, :], selector(n), parts[:, q * TT:(q + 1) * TT],
                           start=True, stop=True)
        mm.then_inc(r.chat_ready, 1)

    def add(j):
        for q in range(2):
            mm = pe.matmul(r.y[:, q, :], weight(j), r.prod[:, j, q * TT:(q + 1) * TT],
                           start=False, stop=True, skip_group_check=True)
        mm.then_inc(r.sum_done, 1)

    base = scan_counts(it, g)
    pe.wait_ge(r.prod_ready, CREDIT + base)
    spread(base, 0)
    with pe.Fori(0, NS // 2 - 1) as n2:
        for j in range(2):
            u = base + n2 * 2 + j
            pe.wait_ge(r.prod_ready, CREDIT + u + 1)
            spread(u + 1, n2 * 2 + (j + 1))
            add(j)
    pe.wait_ge(r.prod_ready, CREDIT + base + NS - 1)
    spread(base + NS - 1, NS - 1)
    add(0)
    pe.wait_ge(r.prod_ready, CREDIT + base + NS)
    add(1)


def softplus_act(act, s, ps, bias, i, credit):
    act.wait_ge(s.soft_done, credit + i)
    act.activation(s.lin, ps, ACT.Identity, bias=bias)
    act.activation(s.ex, ps, ACT.Abs, bias=bias).then_inc(s.abs_done, 1)
    act.wait_ge(s.abs_done, i + 1)
    act.activation(s.ex, s.ex, ACT.Exp, scale=-1.0).then_inc(s.exp_done, 1)
    act.wait_ge(s.exp_done, i + 1)
    act.activation(s.lg, s.ex, ACT.Ln, bias=s.one).then_inc(s.log_done, 1)


def softplus_dve(dve, s, out, i):
    dve.wait_ge(s.log_done, i + 1)
    dve.tensor_scalar(s.off, s.ex, 1.0, -1.0, ALU.add, ALU.add).then_inc(s.soft_step, 1)
    dve.wait_ge(s.soft_step, i * 3 + 1)
    dve.scalar_tensor_tensor(out=s.off, in0=s.off, scalar=-1.0, in1=s.ex, op0=ALU.mult,
                             op1=ALU.add).then_inc(s.soft_step, 1)
    dve.wait_ge(s.soft_step, i * 3 + 2)
    dve.tensor_tensor(s.lg, s.lg, s.off, ALU.add).then_inc(s.soft_step, 1)
    dve.wait_ge(s.soft_step, i * 3 + 3)
    dve.scalar_tensor_tensor(out=out, in0=s.lin, scalar=0.0, in1=s.lg, op0=ALU.max,
                             op1=ALU.add).then_inc(s.soft_done, 1)


class SoftPlus:

    def __init__(self, m, lin, ex, lg, off, one):
        self.lin, self.ex, self.lg, self.off, self.one = lin, ex, lg, off, one
        self.abs_done, self.exp_done, self.log_done = m.sem("abs_done"), m.sem("exp_done"), m.sem("log_done")
        self.soft_step, self.soft_done = m.sem("soft_step"), m.sem("soft_done")


def split_rows(dve, step, i, rows, parts, half, mid, rest):
    dve.tensor_copy(parts[0:32, :], rows).then_inc(step, 1)
    dve.wait_ge(step, i * 5 + 1)
    dve.tensor_tensor(rest, rows, parts[0:32, :], ALU.subtract).then_inc(step, 1)
    dve.wait_ge(step, i * 5 + 2)
    dve.tensor_copy(mid, rest).then_inc(step, 1)
    dve.wait_ge(step, i * 5 + 3)
    dve.tensor_copy(parts[32:64, :], mid)
    dve.tensor_tensor(rest, rest, mid, ALU.subtract).then_inc(step, 1)
    dve.wait_ge(step, i * 5 + 4)
    dve.tensor_copy(parts[64:96, :], rest).then_inc(step, 1)


def mixer0(nc, k, acc):
    R = 64
    a = k.a
    H2 = L // TC
    with ExitStack() as ctx:
        m = Mem(nc, ctx, "mix0")
        wz, wout = m.sb("wz", [P, C, E]), m.sb("wout", [P, C, E])
        wpar = m.sb("wpar", [P, C, P])
        wdt = m.sb("wdt", [R, E])
        taps, bdt, alog, dcol = m.sb("taps", [P, C, KC]), m.sb("bdt", [P, C]), m.sb("alog", [P, C, NS]), m.sb("dcol", [P, C])
        ea, neg_a, mask, keep = (m.sb(n, [P, C * NS]) for n in ("ea", "neg_a", "mask", "keep"))
        den, rec, reff, rsum = (m.sb(n, [P, C * NS]) for n in ("den", "rec", "reff", "rsum"))
        rsum_t = m.sb("rsum_t", [NS, C, P])
        diag_d = m.sb("diag_d", [P, C, P])
        diag_r = m.sb("diag_r", [P, 2, P])
        one = m.sb("one", [P, 1])
        u = m.sb("u", [P, C, L + 1])
        dt = m.sb("dt", [P, C, L + 1])
        du = m.sb("du", [P, C, L])
        dd = m.sb("dd", [P, C, L])
        rows, dtin = m.sb("rows", [32, L]), m.sb("dtin", [R, L])
        parts = m.sb("parts", [96, L], BF16)
        state = m.sb("state", [P, C * (NS + 1)])
        r = ScanRing(m)
        mid = r.prod[0:32, 0, :].bitcast(BF16)
        rest = r.h[0:32, :, :].rearrange("p a t -> p (a t)")
        s = SoftPlus(m, r.drive[:, 0, :], r.drive[:, 1, :], r.h[:, 0, :], r.h[:, 1, :], one[:, 0:1])

        loaded, cleared = m.sem("loaded"), m.sem("cleared")
        ea_ready, setup, rs_turned, rs_kept = m.sem("ea_ready"), m.sem("setup"), m.sem("rs_turned"), m.sem("rs_kept")
        batch_done = m.sem("batch_done")
        tap_done, u_ready = m.sem("tap_done"), m.sem("u_ready")
        par_ready, par_kept, split = m.sem("par_ready"), m.sem("par_kept"), m.sem("split")
        dt_ready = m.sem("dt_ready")
        shaped, step_ready = m.sem("shaped"), m.sem("step_ready")
        mask_ready, saved = m.sem("mask_ready"), m.sem("saved")
        rs_ready, y_step, y_ready = m.sem("rs_ready"), m.sem("y_step"), m.sem("y_ready")
        z_ready, gate_ready, gated = m.sem("z_ready"), m.sem("gate_ready"), m.sem("gated")
        out_ready, added = m.sem("out_ready"), m.sem("added")
        SETUP = 9
        block = ctx.enter_context(nc.Block())

        @block.sync
        def _(sp):
            sp.wait_ge(cleared, 1)
            for dst, src in (
                (wz[:], a["W_z"].rearrange("(c p) m -> p c m", p=P)),
                (wout[:], a["W_out"].rearrange("(c p) m -> p c m", p=P)),
                (wpar[:, :, 0:NS], a["W_par"][:, R + NS:R + 2 * NS].rearrange("(c p) m -> p c m", p=P)),
                (wpar[:, :, 64:64 + R], a["W_par"][:, 0:R].rearrange("(c p) m -> p c m", p=P)),
                (wdt[:], a["W_dt"]),
                (taps[:], a["conv_w"].rearrange("(c p) k -> p c k", p=P)),
                (bdt[:], a["b_dt"]),
                (alog[:], a["A_log"].rearrange("(c p) n -> p c n", p=P)),
                (dcol[:], a["D"]),
            ):
                sp.dma_start(dst, src).then_inc(loaded, 16)

        LOADS = 9 * 16

        @block.gpsimd
        def _(pool):
            with pool.Fori(0, B) as b:
                for c in range(C):
                    for hf in range(H2):
                        g = c * H2 + hf
                        with pool.Fori(0, NS // 2) as n2:
                            for j in range(2):
                                un = scan_counts(b, g) + n2 * 2 + j
                                pool.wait_ge(mask_ready, un + 1)
                                pool.tensor_tensor(r.drive[:, j, :], r.drive[:, j, :],
                                                   du[:, c, hf * TC:(hf + 1) * TC],
                                                   ALU.add).then_inc(r.drive_ready, 1)

        @block.scalar
        def _(act):
            act.preload_act_table_set("natural_log_exp_and_others")
            act.wait_ge(loaded, LOADS)
            act.activation(ea[:], alog[:].rearrange("p c n -> p (c n)"), ACT.Exp).then_inc(ea_ready, 1)
            act.wait_ge(rs_turned, 1)
            act.activation(rsum_t[:], r.banks[0:NS, 0, 0:C * P].rearrange("n (c p) -> n c p", c=C),
                           ACT.Copy).then_inc(rs_kept, 1)
            with act.Fori(0, B) as b:
                for c in range(C):
                    act.wait_ge(tap_done, b * 8 + 4 * (c + 1))
                    act.activation(u[:, c, 1:L + 1], u[:, c, 1:L + 1], ACT.Silu).then_inc(u_ready, 1)
                act.preload_act_table_set("natural_log_exp_and_others")
                act.wait_ge(par_ready, b + 1)
                act.activation(rows[:], r.banks[0:32, 0:4, :].rearrange("p a t -> p (a t)"),
                               ACT.Copy).then_inc(par_kept, 1)
                act.activation(dtin[:], r.banks[64:128, 0:4, :].rearrange("p a t -> p (a t)"),
                               ACT.Copy).then_inc(par_kept, 1)
                act.wait_ge(split, b * 5 + 5)
                for c in range(C):
                    for hf in range(H2):
                        i = b * 4 + (c * H2 + hf)
                        act.wait_ge(dt_ready, i + 1)
                        softplus_act(act, s, flat(r.decay[hf]), bdt[:, c:c + 1], i, 1)
                act.wait_ge(step_ready, b + 1)
                for c in range(C):
                    for hf in range(H2):
                        g = c * H2 + hf
                        if g:
                            act.wait_ge(saved, b * 4 + g)
                        with act.Fori(0, NS // 2) as n2:
                            for j in range(2):
                                un = scan_counts(b, g) + n2 * 2 + j
                                at = n2 * 2 + (c * NS + j)
                                act.wait_ge(r.scan_done, CREDIT + un - 1)
                                act.activation(r.drive[:, j, :], dd[:, c, hf * TC:(hf + 1) * TC], ACT.Copy,
                                               scale=mask[:, ds(at, 1)]).then_inc(mask_ready, 1)
                                act.wait_ge(r.sum_done, CREDIT + un - 1)
                                act.activation(diag_r[:, j, :], k.ident[:], ACT.Copy, scale=reff[:, ds(at, 1)])
                                act.activation(flat(r.decay[j]), dt[:, c, hf * TC:(hf + 1) * TC], ACT.Exp,
                                               scale=neg_a[:, ds(at, 1)]).then_inc(r.decay_ready, 1)
                                act.wait_ge(r.scan_done, CREDIT + un)
                                act.activation(state[:, ds(at + c, 1)], r.h[:, 1 - j, TC - 1:TC], ACT.Copy)
                        act.wait_ge(r.scan_done, CREDIT + scan_counts(b, g) + NS)
                        act.activation(state[:, c * (NS + 1) + NS:(c + 1) * (NS + 1)], r.h[:, 1, TC - 1:TC],
                                       ACT.Copy).then_inc(saved, 1)
                for c in range(C):
                    for hf in range(H2):
                        g = c * H2 + hf
                        act.wait_ge(z_ready, b * 4 + g + 1)
                        act.activation(dd[:, c, hf * TC:(hf + 1) * TC], flat(r.decay[hf]),
                                       ACT.Silu).then_inc(gate_ready, 1)

        @block.vector
        def _(dve):
            dve.memset(wpar[:], 0.0).then_inc(cleared, 1)
            dve.memset(one[:], 1.0).then_inc(batch_done, 1)
            dve_credits(dve, r)
            dve.wait_ge(r.scan_done, CREDIT)
            dve.wait_ge(r.prod_ready, CREDIT)
            dve.memset(s.off, 0.0).then_inc(s.soft_done, 1)
            dve.wait_ge(loaded, LOADS)
            for c in range(C):
                dve.tensor_scalar(diag_d[:, c, :], k.ident[:], dcol[:, c:c + 1], None, ALU.mult)
            dve.wait_ge(ea_ready, 1)
            dve.tensor_scalar(neg_a[:], ea[:], -1.0, None, ALU.mult).then_inc(setup, 1)
            dve.tensor_scalar(mask[:], ea[:], 1e-5, None, ALU.is_lt).then_inc(setup, 1)
            dve.wait_ge(setup, 2)
            dve.tensor_scalar(keep[:], mask[:], -1.0, 1.0, ALU.mult, ALU.add).then_inc(setup, 1)
            dve.tensor_scalar(den[:], neg_a[:], 1e-10, None, ALU.add).then_inc(setup, 1)
            dve.wait_ge(setup, 4)
            dve.tensor_tensor(den[:], den[:], mask[:], ALU.subtract).then_inc(setup, 1)
            dve.wait_ge(setup, 5)
            dve.reciprocal(rec[:], den[:]).then_inc(setup, 1)
            dve.wait_ge(setup, 6)
            dve.tensor_tensor(rsum[:], rec[:], keep[:], ALU.mult).then_inc(setup, 1)
            dve.wait_ge(setup, 7)
            dve.tensor_tensor(reff[:], rsum[:], mask[:], ALU.add).then_inc(setup, 1)
            dve.memset(state[:], 0.0).then_inc(setup, 1)
            dve.wait_ge(setup, SETUP)
            with dve.Fori(0, B) as b:
                for c in range(C):
                    uc = u[:, c, 1:L + 1]
                    dve.tensor_scalar(uc, k.xn[:, c, ds(b, 1), 0:L], taps[:, c, 0:1], None,
                                      ALU.mult).then_inc(tap_done, 1)
                    for t in range(1, KC):
                        dve.wait_ge(tap_done, b * 8 + (4 * c + t))
                        dve.scalar_tensor_tensor(out=uc, in0=k.xn[:, c, b, t:t + L], scalar=taps[:, c, t:t + 1],
                                                 in1=uc, op0=ALU.mult, op1=ALU.add).then_inc(tap_done, 1)
                dve.wait_ge(par_kept, b * 2 + 1)
                split_rows(dve, split, b, rows[:], parts, None, mid, rest)
                dve.wait_ge(split, b * 5 + 5)
                for c in range(C):
                    for hf in range(H2):
                        softplus_dve(dve, s, dt[:, c, 1 + hf * TC:1 + (hf + 1) * TC], b * 4 + (c * H2 + hf))
                dve.wait_ge(u_ready, b * 2 + 2)
                dve.wait_ge(s.soft_done, 1 + b * 4 + 4)
                for c in range(C):
                    dve.tensor_copy(u[:, c, 0:1], u[:, c, 1:2])
                    dve.tensor_copy(dt[:, c, 0:1], dt[:, c, 1:2]).then_inc(shaped, 1)
                dve.wait_ge(shaped, b * 6 + 2)
                for c in range(C):
                    dve.tensor_tensor(du[:, c, :], u[:, c, 1:L + 1], u[:, c, 0:L], ALU.subtract)
                    dve.tensor_tensor(dd[:, c, :], u[:, c, 0:L], dt[:, c, 0:L], ALU.mult).then_inc(shaped, 1)
                    dve.tensor_scalar(state[:, 1 + c * (NS + 1):(c + 1) * (NS + 1)], keep[:, c * NS:(c + 1) * NS],
                                      u[:, c, 0:1], None, ALU.mult).then_inc(shaped, 1)
                dve.wait_ge(shaped, b * 6 + 6)
                for c in range(C):
                    ins = dve.tensor_tensor(dd[:, c, :], dd[:, c, :], du[:, c, :], ALU.subtract)
                ins.then_inc(step_ready, 1)
                for c in range(C):
                    for hf in range(H2):
                        g = c * H2 + hf
                        dve_scans(dve, r, b, g, state, 1 + c * (NS + 1))
                        dve.wait_ge(rs_ready, b * 4 + g + 1)
                        dve.wait_ge(r.prod_ready, CREDIT + scan_counts(b, g) + NS)
                        dve.tensor_tensor(r.prod[:, 0, :], flat(r.chat), u[:, c, 1 + hf * TC:1 + (hf + 1) * TC],
                                          ALU.mult).then_inc(y_step, 1)
                        dve.wait_ge(y_step, b * 4 + g + 1)
                        dve.tensor_tensor(du[:, c, hf * TC:(hf + 1) * TC], flat(r.y), r.prod[:, 0, :],
                                          ALU.subtract).then_inc(y_ready, 1)
                for c in range(C):
                    for hf in range(H2):
                        g = c * H2 + hf
                        yc = du[:, c, hf * TC:(hf + 1) * TC]
                        dve.wait_ge(gate_ready, b * 4 + g + 1)
                        dve.wait_ge(y_ready, b * 4 + g + 1)
                        dve.tensor_tensor(yc, yc, dd[:, c, hf * TC:(hf + 1) * TC], ALU.mult).then_inc(gated, 1)
                for c in range(C):
                    for hf in range(H2):
                        g = c * H2 + hf
                        dve.wait_ge(out_ready, b * 4 + g + 1)
                        ac = acc[:, c, ds(b * L + hf * TC, TC)]
                        ins = dve.tensor_tensor(ac, flat(r.decay[hf]), ac, ALU.add).then_inc(added, 1)
                dve.wait_ge(added, b * 4 + 4)
                dve.memset(one[:], 1.0).then_inc(batch_done, 1)

        @block.tensor
        def _(pe):
            pe.sem_inc(r.sum_done, CREDIT)
            pe.wait_ge(loaded, LOADS)
            pe.wait_ge(setup, SETUP)
            for c in range(C):
                mm = pe.transpose(r.banks[0:NS, 0, c * P:(c + 1) * P], rsum[:, c * NS:(c + 1) * NS], k.ident[:])
            mm.then_inc(rs_turned, 1)
            pe.wait_ge(rs_kept, 1)
            with pe.Fori(0, B) as b:
                pe.wait_ge(batch_done, b + 1)
                for q in range(4):
                    for c in range(C):
                        mm = pe.matmul(r.banks[:, q, :], wpar[:, c, :],
                                       k.xn[:, c, b, PAD + q * TT:PAD + (q + 1) * TT],
                                       start=c == 0, stop=c == C - 1)
                mm.then_inc(par_ready, 1)
                pe.wait_ge(par_kept, b * 2 + 2)
                for c in range(C):
                    for hf in range(H2):
                        i = b * 4 + (c * H2 + hf)
                        if c:
                            pe.wait_ge(s.log_done, i - 1)
                        for q in range(2):
                            mm = pe.matmul(r.decay[hf][:, q, :], wdt[:, c * P:(c + 1) * P],
                                           dtin[:, hf * TC + q * TT:hf * TC + (q + 1) * TT],
                                           start=True, stop=True)
                        mm.then_inc(dt_ready, 1)
                for c in range(C):
                    for hf in range(H2):
                        g = c * H2 + hf
                        if g == 0:
                            pe.wait_ge(step_ready, b + 1)
                            pe.wait_ge(split, b * 5 + 5)
                        else:
                            pe.wait_ge(y_ready, b * 4 + g)
                        for q in range(2):
                            o = 1 + hf * TC + q * TT
                            pe.matmul(r.y[:, q, :], diag_d[:, c, :], u[:, c, o:o + TT], start=True, stop=True,
                                      skip_group_check=True)
                        pe_sums(pe, r, b, g, lambda j: diag_r[:, j, :],
                                lambda n: k.sel[:, n, :] if isinstance(n, int) else k.sel[:, ds(n, 1), :],
                                parts[:, hf * TC:(hf + 1) * TC])
                        for q in range(2):
                            o = hf * TC + q * TT
                            mm = pe.matmul(r.chat[:, q, :], rsum_t[:, c, :], rows[0:NS, o:o + TT],
                                           start=True, stop=True)
                        mm.then_inc(rs_ready, 1)
                for c in range(C):
                    for hf in range(H2):
                        g = c * H2 + hf
                        if g == 0:
                            pe.wait_ge(saved, b * 4 + 4)
                        if c:
                            pe.wait_ge(gate_ready, b * 4 + g - 1)
                        for q in range(2):
                            o = PAD + hf * TC + q * TT
                            for kk in range(C):
                                mm = pe.matmul(r.decay[hf][:, q, :], wz[:, kk, c * P:(c + 1) * P],
                                               k.xn[:, kk, b, o:o + TT], start=kk == 0, stop=kk == C - 1)
                        mm.then_inc(z_ready, 1)
                pe.wait_ge(gated, b * 4 + 4)
                for c in range(C):
                    for hf in range(H2):
                        g = c * H2 + hf
                        if c:
                            pe.wait_ge(added, b * 4 + g - 1)
                        for q in range(2):
                            o = hf * TC + q * TT
                            for kk in range(C):
                                mm = pe.matmul(r.decay[hf][:, q, :], wout[:, kk, c * P:(c + 1) * P],
                                               du[:, kk, o:o + TT], start=kk == 0, stop=kk == C - 1)
                        mm.then_inc(out_ready, 1)


def experts0(nc, k, acc):
    GS, SL, F = 16, 64, 64
    NG = L // GS
    QG = TT // GS
    NQ = L // TT
    EG = 8
    NE = SL // EG
    a = k.a
    z = nc.dram_tensor("slot_outputs", (B, NG, SL, E), F32, kind="Internal").ap()
    with ExitStack() as keep:
        perm_t = Mem(nc, keep, "exp").sb("perm_t", [P, T])
        with ExitStack() as ctx:
            m = Mem(nc, ctx, "exa")
            ctrl, bias = m.sb("ctrl", [P, C, P]), m.sb("bias", [F, SL])
            tie, parity = m.sb("tie", [P, QG, GS]), m.sb("parity", [P, QG, GS])
            pair_of = m.sb("pair_of", [P, 4])
            lt, pq = m.sb("lt", [P, TT]), m.sb("pq", [P, TT])
            top = m.sb("top", [P, QG])
            work = m.sb("work", [P, 2, EG * P])
            xs = work[:, 0, :].rearrange("p (c t) -> p c t", c=C)
            xtok = work[:, 1, :].rearrange("p (t e) -> p t e", t=4)
            inner = work[0:F, :, :].rearrange("p j (s g) -> p j s g", s=EG)
            pex = m.sb("pex", [P, 2, 4, P])
            sel_t = m.sb("sel_t", [P, C, SL, NG])
            f1 = m.sb("f1", [P, 2, C, EG, F])
            f2 = m.sb("f2", [F, 2, EG, E])
            inter = m.sb("inter", [P, 2, 4, E])
            banks = m.ps("banks", [P, 8, TT])
            loaded, built = m.sem("loaded"), m.sem("built")
            lg_ready, pstep, perm_ready = m.sem("lg_ready"), m.sem("pstep"), m.sem("perm_ready")
            xs_ready, turned, xtok_ready, pex_ready = m.sem("xs_ready"), m.sem("turned"), m.sem("xtok_ready"), m.sem("pex_ready")
            sel_ready, sel_kept = m.sem("sel_ready"), m.sem("sel_kept")
            w_loaded = [m.sem(f"w_loaded{j}") for j in range(2)]
            stored = [m.sem(f"stored{j}") for j in range(2)]
            slot_free = [m.sem(f"slot_free{j}") for j in range(2)]
            biased = m.sem("biased")
            in_ready, inner_ready = m.sem("in_ready"), m.sem("inner_ready")
            fill_ready, act_kept, dve_kept = m.sem("fill_ready"), m.sem("act_kept"), m.sem("dve_kept")
            block = ctx.enter_context(nc.Block())

            @block.sync
            def _(sp):
                ctl = a["controller"].rearrange("(c p) m -> p c m", p=P)
                for dst, src in ((ctrl[:, :, 0:SL], ctl), (ctrl[:, :, SL:P], ctl), (bias[:], a["bias"]),
                                 (tie[:], a["tie"])):
                    sp.dma_start(dst, src).then_inc(loaded, 16)
                with sp.Fori(0, B) as b, sp.Fori(0, NE // 2) as e2:
                    for j in range(2):
                        e = b * NE + e2 * 2 + j
                        sp.wait_ge(fill_ready, 8 + e * 4 - 4)
                        sp.dma_start(f1[:, j], a["f1"].rearrange("(c p) (e s) f -> p c e s f", p=P, s=EG)[
                            :, :, ds(e2 * 2 + j, 1)].rearrange("p c e s f -> p c (e s f)")).then_inc(w_loaded[j], 16)
                        sp.dma_start(f2[:, j], a["f2"].rearrange("(e s) f d -> f e s d", e=NE)[
                            :, ds(e2 * 2 + j, 1)].rearrange("p e s d -> p (e s) d")).then_inc(w_loaded[j], 16)

            @block.gpsimd
            def _(pool):
                for j in range(2):
                    pool.sem_inc(slot_free[j], 1)
                with pool.Fori(0, B) as b, pool.Fori(0, NE) as e:
                    i = b * NE + e
                    for j in range(2):
                        pool.wait_ge(act_kept, 1 + i * 2 + (j + 1))
                        pool.wait_ge(dve_kept, 1 + i * 2 + (j + 1))
                        pool.dma_start(z[ds(b, 1), :, ds(e * EG + j * 4, 4), :].rearrange("b g s d -> (b g) (s d)"),
                                       inter[:, j].rearrange("p s d -> p (s d)")).then_inc(stored[j], 16)
                    for j in range(2):
                        pool.wait_ge(stored[j], i * 16 + 16)
                        pool.sem_inc(slot_free[j], 1)

            @block.scalar
            def _(act):
                act.wait_ge(loaded, 16 * 4)
                act.sem_inc(act_kept, 1)
                with act.Fori(0, B) as b:
                    with act.Fori(0, NQ) as q:
                        i = b * NQ + q
                        act.wait_ge(sel_ready, 1 + i * 8)
                        act.activation(xs, k.xn[:, :, b, ds(PAD + q * TT, TT)], ACT.Copy).then_inc(xs_ready, 1)
                        act.wait_ge(perm_ready, 1 + (i + 1))
                        act.activation(perm_t[:, ds(b * L + q * TT, TT)], pq[:], ACT.Copy)
                        act.wait_ge(turned, i + 1)
                        act.activation(work[:, 1, :],
                                       banks[:, 1:3, :].rearrange("p a t -> p (a t)"), ACT.Copy).then_inc(xtok_ready, 1)
                        for t in range(4):
                            for c in range(C):
                                n = i * 8 + (t * C + c)
                                act.wait_ge(sel_ready, 1 + (n + 1))
                                act.activation(
                                    sel_t[:, c, :, ds(q * QG + t * 8, 8)].rearrange("p s g -> p g s"),
                                    banks[:, 4 + c, :].rearrange("p (g s) -> p g s", s=SL),
                                    ACT.Copy).then_inc(sel_kept, 1)
                    with act.Fori(0, NE // 2) as e2:
                        for j in range(2):
                            e = b * NE + e2 * 2 + j
                            for h in range(2):
                                act.wait_ge(fill_ready, 8 + e * 4 + (2 * h + 1))
                                act.wait_ge(slot_free[h], e + 1)
                                act.activation(inter[:, h, 0:2, :].rearrange("p s d -> p (s d)"), banks[:, 7, :],
                                               ACT.Copy).then_inc(act_kept, 1)

            @block.vector
            def _(dve):
                dve.memset(parity[0:64, 0:QG:2], 1.0)
                dve.memset(parity[0:64, 1:QG:2], 0.0)
                dve.memset(parity[64:128, 0:QG:2], 0.0)
                dve.memset(parity[64:128, 1:QG:2], 1.0).then_inc(built, 1)
                for i in range(4):
                    for v in range(4):
                        ins = dve.memset(pair_of[32 * v:32 * v + 32, i:i + 1], 1.0 if i == v else 0.0)
                ins.then_inc(built, 1)
                dve.memset(lt[:], 0.0).then_inc(perm_ready, 1)
                dve.memset(pex[:], 0.0).then_inc(dve_kept, 1)
                dve.wait_ge(perm_ready, 1)
                dve.wait_ge(dve_kept, 1)
                dve.wait_ge(loaded, 16 * 4)
                dve.wait_ge(built, 2)
                with dve.Fori(0, B) as b:
                    with dve.Fori(0, NQ) as q:
                        i = b * NQ + q
                        lg = banks[:, 0, :].rearrange("p (g t) -> p g t", t=GS)
                        ltg = lt[:].rearrange("p (g t) -> p g t", t=GS)
                        dve.wait_ge(lg_ready, i + 1)
                        dve.tensor_tensor(ltg, lg, tie[:], ALU.add).then_inc(pstep, 1)
                        dve.wait_ge(pstep, i * 3 + 1)
                        dve.tensor_reduce(top[:], ltg, AX.X, ALU.max).then_inc(pstep, 1)
                        dve.wait_ge(pstep, i * 3 + 2)
                        dve.tensor_tensor(ltg, ltg, top[:].unsqueeze(2).broadcast_to([P, QG, GS]),
                                          ALU.is_equal).then_inc(pstep, 1)
                        dve.wait_ge(pstep, i * 3 + 3)
                        dve.tensor_tensor(pq[:].rearrange("p (g t) -> p g t", t=GS), ltg, parity[:],
                                          ALU.mult).then_inc(perm_ready, 1)
                        dve.wait_ge(turned, i + 1)
                        for t in range(4):
                            dve.wait_ge(sel_ready, 1 + i * 8 + 2 * (t - 1) if t > 1 else 1 + i * 8)
                            dve.tensor_tensor(pex[:, t % 2], banks[:, 3, t * P:(t + 1) * P].unsqueeze(1)
                                              .broadcast_to([P, 4, P]),
                                              pair_of[:].unsqueeze(2).broadcast_to([P, 4, P]),
                                              ALU.mult).then_inc(pex_ready, 1)
                    with dve.Fori(0, NE // 2) as e2:
                        for j in range(2):
                            ex = b * NE + e2 * 2 + j
                            dve.wait_ge(in_ready, ex + 1)
                            dve.wait_ge(fill_ready, 8 + ex * 4 - 4)
                            dve.tensor_tensor(inner[:, j], banks[0:F, 5:7, :].rearrange("p a (s g) -> p (a s) g", g=P),
                                              bias[:, ds((e2 * 2 + j) * EG, EG)].unsqueeze(2).broadcast_to([F, EG, P]),
                                              ALU.add).then_inc(biased, 1)
                            dve.wait_ge(biased, ex + 1)
                            dve.tensor_scalar(inner[:, j], inner[:, j], 0.0, None, ALU.max).then_inc(inner_ready, 1)
                            for h in range(2):
                                dve.wait_ge(fill_ready, 8 + ex * 4 + (2 * h + 2))
                                dve.wait_ge(slot_free[h], ex + 1)
                                dve.tensor_copy(inter[:, h, 2:4, :].rearrange("p s d -> p (s d)"),
                                                banks[:, 0, :]).then_inc(dve_kept, 1)

            @block.tensor
            def _(pe):
                pe.sem_inc(fill_ready, 8)
                pe.sem_inc(sel_ready, 1)
                pe.wait_ge(loaded, 16 * 4)
                with pe.Fori(0, B) as b:
                    with pe.Fori(0, NQ) as q:
                        i = b * NQ + q
                        pe.wait_ge(perm_ready, 1 + i)
                        pe.wait_ge(dve_kept, 1 + b * 2 * NE)
                        for c in range(C):
                            mm = pe.matmul(banks[:, 0, :], ctrl[:, c, :], k.xn[:, c, b, ds(PAD + q * TT, TT)],
                                           start=c == 0, stop=c == C - 1)
                        mm.then_inc(lg_ready, 1)
                        pe.wait_ge(xs_ready, i + 1)
                        for t in range(4):
                            for c in range(C):
                                o = (t * C + c) * P
                                pe.transpose(banks[:, 1 + o // TT, o % TT:o % TT + P], xs[:, c, t * P:(t + 1) * P],
                                             k.ident[:])
                        pe.wait_ge(perm_ready, 1 + (i + 1))
                        for t in range(4):
                            mm = pe.transpose(banks[:, 3, t * P:(t + 1) * P], pq[:, t * P:(t + 1) * P], k.ident[:])
                        mm.then_inc(turned, 1)
                        pe.wait_ge(xtok_ready, i + 1)
                        for t in range(4):
                            pe.wait_ge(pex_ready, i * 4 + (t + 1))
                            for c in range(C):
                                n = i * 8 + (t * C + c)
                                if t:
                                    pe.wait_ge(sel_kept, n - 1)
                                mm = pe.matmul(banks[:, 4 + c, :], xtok[:, t, c * P:(c + 1) * P],
                                               pex[:, t % 2].rearrange("p a n -> p (a n)"), start=True, stop=True)
                                mm.then_inc(sel_ready, 1)
                    with pe.Fori(0, NE // 2) as e2:
                        for j in range(2):
                            e = b * NE + e2 * 2 + j
                            pe.wait_ge(w_loaded[j], (b * (NE // 2) + e2 + 1) * 32)
                            pe.wait_ge(sel_kept, (b + 1) * NQ * 8)
                            for s in range(EG):
                                for c in range(C):
                                    mm = pe.matmul(banks[0:F, 5 + s // 4, s % 4 * P:(s % 4 + 1) * P],
                                                   f1[:, j, c, s, :],
                                                   sel_t[:, c, ds((e2 * 2 + j) * EG + s, 1), :],
                                                   start=c == 0, stop=c == C - 1)
                            mm.then_inc(in_ready, 1)
                            pe.wait_ge(inner_ready, e + 1)
                            for f in range(4):
                                kept = act_kept if f % 2 == 0 else dve_kept
                                bank = 7 if f % 2 == 0 else 0
                                pe.wait_ge(kept, 1 + e * 2 + f // 2)
                                for h in range(2):
                                    mm = pe.matmul(banks[:, bank, h * E:(h + 1) * E], inner[:, j, 2 * f + h, :],
                                                   f2[:, j, 2 * f + h, :], start=True, stop=True)
                                mm.then_inc(fill_ready, 1)

        with ExitStack() as ctx:
            m = Mem(nc, ctx, "exb")
            zp = m.sb("zp", [P, 2, TT // 32, E])
            out = m.ps("out", [P, 2, C, TT])
            z_loaded = [m.sem(f"z_loaded{j}") for j in range(2)]
            out_ready, added = m.sem("out_ready"), m.sem("added")
            block = ctx.enter_context(nc.Block())

            @block.sync
            def _(sp):
                zr = z.rearrange("b (q r h) s d -> (h s) (b q) r d", h=2, r=TT // 32)
                with sp.Fori(0, B * NQ // 2) as i2:
                    for j in range(2):
                        sp.wait_ge(out_ready, i2 * 2 + (j + 1))
                        sp.dma_start(zp[:, j], zr[:, ds(i2 * 2 + j, 1)].rearrange("p q r d -> p (q r) d")
                                     ).then_inc(z_loaded[j], 16)

            @block.tensor
            def _(pe):
                pe.sem_inc(out_ready, 2)
                with pe.Fori(0, B * NQ // 2) as i2:
                    for j in range(2):
                        i = i2 * 2 + j
                        pe.wait_ge(z_loaded[j], i2 * 16 + 16)
                        pe.wait_ge(added, i + 1)
                        for t in range(TT // 32):
                            for c in range(C):
                                mm = pe.matmul(out[:, j, c, t * 32:(t + 1) * 32], zp[:, j, t, c * P:(c + 1) * P],
                                               perm_t[:, ds(i * TT + t * 32, 32)], start=True, stop=True)
                        mm.then_inc(out_ready, 1)

            @block.vector
            def _(dve):
                dve.sem_inc(added, 2)
                with dve.Fori(0, B * NQ // 2) as i2:
                    for j in range(2):
                        i = i2 * 2 + j
                        dve.wait_ge(out_ready, 2 + (i + 1))
                        ac = acc[:, :, ds(i * TT, TT)]
                        dve.tensor_tensor(ac, out[:, j], ac, ALU.add).then_inc(added, 1)


def mixer1(nc, k, way, y_in, y_out_dram):
    D2, R, MB = 512, 16, 4
    a = k.a
    bw = way == "bw"
    NC = L // TC
    NP = B * NC
    assert NC == 2
    with ExitStack() as ctx:
        m = Mem(nc, ctx, way)
        win, wout = m.sb("win", [P, C, 2 * D2]), m.sb("wout", [P, MB, E])
        wx, wdt = m.sb("wx", [P, MB, 64 + R]), m.sb("wdt", [R, D2])
        taps, small = m.sb("taps", [P, MB, KC]), m.sb("small", [P, 3, MB])
        convb, bdt, dcol = small[:, 0, :], small[:, 1, :], small[:, 2, :]
        norm, norm_s = m.sb("norm", [P, 2, C]), m.sb("norm_s", [P, 2, C])
        alog, neg_a = m.sb("alog", [P, MB * NS]), m.sb("neg_a", [P, MB * NS])
        diag_d = m.sb("diag_d", [P, MB, P])
        consts = m.sb("consts", [P, 4])
        one, eps, carry = consts[:, 0:1], consts[:, 1:2], consts[:, 2:4]
        u, dt, dtu = m.sb("u", [P, MB, TC]), m.sb("dt", [P, MB, TC]), m.sb("dtu", [P, MB, TC])
        parts = m.sb("parts", [96, TC], BF16)
        brep = m.sb("brep", [P, NS, TC])
        state = m.sb("state", [P, MB * (NS + 1)])
        decay_sb = m.sb("decay", [P, 2, TC])
        r = ScanRing(m)
        banks = r.banks
        flatb = banks[:].rearrange("p a t -> p (a t)")
        y_banks = [banks[:, 2:4, :], banks[:, 6:8, :]]
        z_banks = flatb[:, 0:2 * TT]
        stat = flatb[:, 0:2 * TT]
        x_bank = [5, 2]
        par_bank = 6
        dt_bank = [2, 0]
        b_bank = [4, 6]
        x_slot = [flat(r.prod)[:, 0:PAD + TC], flat(decay_sb)[:, 0:PAD + TC]]
        lin, ex, lg, off = ([r.drive[:, 0, :], r.prod[:, 0, :]], [r.drive[:, 1, :], r.prod[:, 1, :]],
                            [r.h[:, 0, :], decay_sb[:, 0, :]], [r.h[:, 1, :], decay_sb[:, 1, :]])
        mid, rest, dtin = dtu[0:32, 1, 0:TC // 2].bitcast(BF16), dtu[0:32, 2, :], dtu[0:R, 3, :]
        res, sq, logv, r0, r2, ra, rstd, yf = (brep[:, 14:16], brep[:, 12:14], brep[:, 11], brep[:, 10], brep[:, 9],
                                               brep[:, 8], brep[:, 7], brep[:, 5:7])
        (loaded, cleared, ea_ready, setup, xi_ready, xi_kept, tap0, tap_done, u_ready, par_ready, dtin_kept, split,
         dt_ready, abs_done, exp_done, log_done, soft_step, log_sum, soft_done, dtu_ready, b_spread, b_act, b_dve,
         b_free, started, saved, z_ready, gate_ready, gated, out_ready, summed, mean_ready, centred, squared,
         var_ready, logged, root, root_ready, newton, scaled, y_out, stored, yf_loaded) = (m.sem(n) for n in (
             "loaded cleared ea_ready setup xi_ready xi_kept tap0 tap_done u_ready par_ready dtin_kept split "
             "dt_ready abs_done exp_done log_done soft_step log_sum soft_done dtu_ready b_spread b_act b_dve "
             "b_free started saved z_ready gate_ready gated out_ready summed mean_ready centred squared "
             "var_ready logged root root_ready newton scaled y_out stored yf_loaded").split())
        LOADS = 11 * 16
        block = ctx.enter_context(nc.Block())

        def passes(eng):
            both = ExitStack()
            b = both.enter_context(eng.Fori(0, B))
            tc = both.enter_context(eng.Fori(0, NC))
            return both, b, b * NC + tc, tc, ((tc * -TC) + (L - TC)) if bw else tc * TC

        def before(b, tc):
            return b * L + tc * (L + TC) if bw else b * L + tc * TC + TC

        @block.sync
        def _(sp):
            sp.wait_ge(cleared, 1)
            wxa = a[way + "_Wx"].rearrange("(c p) m -> p c m", p=P)
            for dst, src in ((win[:], a[way + "_Win"].rearrange("(c p) m -> p c m", p=P)),
                             (taps[:], a[way + "_convw"].rearrange("(c p) k -> p c k", p=P)),
                             (convb, a[way + "_convb"]), (bdt, a[way + "_bdt"]), (dcol, a[way + "_D"]),
                             (wx[:, :, 0:2 * NS], wxa[:, :, R:R + 2 * NS]),
                             (wx[:, :, 64:64 + R], wxa[:, :, 0:R]),
                             (wdt[:], a[way + "_Wdt"]),
                             (alog[:].rearrange("p (c n) -> p c n", n=NS), a[way + "_Alog"].rearrange("(c p) n -> p c n", p=P)),
                             (norm[:], a["fwn"]),
                             (wout[:], a[way + "_Wout"].rearrange("(c p) m -> p c m", p=P))):
                sp.dma_start(dst, src).then_inc(loaded, 16)
            to = y_out_dram.rearrange("(c p) t -> p c t", p=P)
            if bw:
                sp.dma_start(yf, k.x1.rearrange("(c p) t -> p c t", p=P)[:, :, 0:TC]).then_inc(yf_loaded, 16)
            both, b, it, tc, t0 = passes(sp)
            with both:
                sp.wait_ge(y_out, it + 1)
                sp.dma_start(to[:, :, ds(before(b, tc), TC)], res).then_inc(stored, 16)
                sp.wait_ge(stored, it * 16 + 16)
                sp.sem_inc(b_free, 1)
                if bw:
                    sp.wait_ge(gated, it * MB + MB)
                    sp.dma_start(yf, y_in.rearrange("(c p) t -> p c t", p=P)[:, :, ds(b * L + (t0 + L), TC)]
                                 ).then_inc(yf_loaded, 16)
            sp.wait_ge(y_out, NP + 1)
            sp.dma_start(to[:, :, before(B, 0):before(B, 0) + TC], res).then_inc(stored, 16)
            sp.wait_ge(stored, NP * 16 + 16)

        @block.gpsimd
        def _(pool):
            both, b, it, tc, t0 = passes(pool)
            with both:
                pool.wait_ge(split, it * 5 + 5)

                def log_add(g):
                    pool.wait_ge(log_done, it * MB + (g + 1))
                    pool.wait_ge(soft_step, it * 2 * MB + 2 * (g + 1))
                    pool.tensor_tensor(lg[g % 2], lg[g % 2], off[g % 2], ALU.add).then_inc(log_sum, 1)

                def times_u(g):
                    pool.wait_ge(soft_done, it * MB + (g + 1))
                    pool.wait_ge(u_ready, it * MB + (g + 1))
                    pool.tensor_tensor(dtu[:, g, :], dt[:, g, :], u[:, g, :], ALU.mult).then_inc(dtu_ready, 1)

                log_add(0)
                for g in range(1, MB):
                    log_add(g)
                    times_u(g - 1)
                times_u(MB - 1)
                for g in range(MB):
                    with pool.Fori(0, NS // 2) as n2:
                        for j in range(2):
                            un = scan_counts(it, g) + n2 * 2 + j
                            if g == 0:
                                pool.wait_ge(b_act, it * 8 + n2 + 1)
                                pool.wait_ge(b_dve, it * 8 + n2 + 1)
                                pool.wait_ge(dtu_ready, it * MB + MB)
                            pool.wait_ge(r.scan_done, CREDIT + un - 1)
                            pool.tensor_tensor(r.drive[:, j, :], brep[:, ds(n2 * 2 + j, 1), :].rearrange("p n t -> p (n t)"),
                                               dtu[:, g, :], ALU.mult).then_inc(r.drive_ready, 1)

        @block.scalar
        def _(act):
            def post_square(i):
                act.wait_ge(centred, i + 1)
                act.activation(sq, res, ACT.Square).then_inc(squared, 1)

            def post_root(i):
                act.wait_ge(var_ready, i + 1)
                act.activation(logv, stat, ACT.Ln, bias=eps).then_inc(logged, 1)
                act.wait_ge(logged, i + 1)
                act.activation(r0, logv, ACT.Exp, scale=-0.5).then_inc(root, 1)
                act.wait_ge(root, i + 1)
                act.activation(r2, r0, ACT.Square).then_inc(root_ready, 1)

            act.preload_act_table_set("natural_log_exp_and_others")
            act.wait_ge(loaded, LOADS)
            act.activation(alog[:], alog[:], ACT.Exp).then_inc(ea_ready, 1)
            act.wait_ge(setup, 1)
            both, b, it, tc, t0 = passes(act)
            with both:
                act.wait_ge(r.scan_done, CREDIT + it * UNITS)
                act.wait_ge(r.sum_done, CREDIT + it * UNITS)
                for g in range(MB):
                    x0 = PAD if bw else 0
                    act.wait_ge(xi_ready, it * MB + (g + 1))
                    if g > 1:
                        act.wait_ge(tap_done, it * 12 + 3 * (g - 1))
                    act.activation(x_slot[g % 2], flatb[:, x_bank[g % 2] * TT:x_bank[g % 2] * TT + PAD + TC],
                                   ACT.Copy).then_inc(xi_kept, 1)
                    act.wait_ge(xi_kept, it * MB + (g + 1))
                    act.activation(u[:, g, :], x_slot[g % 2][:, x0:x0 + TC], ACT.Identity, bias=convb[:, g:g + 1],
                                   scale=taps[:, g, 0:1]).then_inc(tap0, 1)
                    if g == 1:
                        post_square(it)
                post_root(it)
                for g in range(MB):
                    act.wait_ge(tap_done, it * 12 + 3 * (g + 1))
                    act.activation(u[:, g, :], u[:, g, :], ACT.Silu).then_inc(u_ready, 1)
                act.preload_act_table_set("natural_log_exp_and_others")
                act.wait_ge(par_ready, it + 1)
                act.activation(dtin, flatb[64:64 + R, par_bank * TT:par_bank * TT + TC], ACT.Copy).then_inc(dtin_kept, 1)

                def softplus_parts(g):
                    s = g % 2
                    x = flatb[:, dt_bank[s] * TT:dt_bank[s] * TT + TC]
                    act.wait_ge(dt_ready, it * MB + (g + 1))
                    if g > 1:
                        act.wait_ge(soft_done, it * MB + (g - 1))
                    act.activation(lin[s], x, ACT.Identity, bias=bdt[:, g:g + 1])
                    act.activation(ex[s], x, ACT.Abs, bias=bdt[:, g:g + 1]).then_inc(abs_done, 1)
                    act.wait_ge(abs_done, it * MB + (g + 1))
                    act.activation(ex[s], ex[s], ACT.Exp, scale=-1.0).then_inc(exp_done, 1)
                    act.wait_ge(exp_done, it * MB + (g + 1))
                    act.activation(lg[s], ex[s], ACT.Ln, bias=one).then_inc(log_done, 1)

                def keep_b(n):
                    if n == 2:
                        act.wait_ge(y_out, it + 1)
                    if n == 14:
                        act.wait_ge(b_free, it + 1)
                    act.wait_ge(b_spread, it * NS + n + 1)
                    act.activation(brep[:, n, :], flatb[:, b_bank[0] * TT:b_bank[0] * TT + TC], ACT.Copy).then_inc(b_act, 1)

                for g in range(MB):
                    softplus_parts(g)
                    keep_b(2 * g)
                for n in range(2 * MB, NS, 2):
                    keep_b(n)
                act.wait_ge(soft_done, it * MB + MB)
                act.wait_ge(started, it + 1)

                def pair(g, n2):
                    for j in range(2):
                        un = scan_counts(it, g) + n2 * 2 + j
                        at = n2 * 2 + (g * NS + j)
                        act.wait_ge(r.scan_done, CREDIT + un - 1)
                        act.activation(decay_sb[:, j, :], dt[:, g, :], ACT.Exp,
                                       scale=neg_a[:, ds(at, 1)] if not isinstance(at, int)
                                       else neg_a[:, at:at + 1]).then_inc(r.decay_ready, 1)
                        act.wait_ge(r.scan_done, CREDIT + un)
                        if isinstance(at, int) and n2 * 2 + j == 0:
                            continue
                        act.activation(state[:, ds(at + g, 1)] if not isinstance(at, int)
                                       else state[:, at + g:at + g + 1],
                                       r.h[:, 1 - j, 0:1] if bw else r.h[:, 1 - j, TC - 1:TC], ACT.Copy)

                def gate(g):
                    act.wait_ge(z_ready, it * MB + (g + 1))
                    act.wait_ge(r.drive_ready, scan_counts(it, g) + NS)
                    act.activation(dtu[:, g, :], z_banks, ACT.Silu).then_inc(gate_ready, 1)
                    act.preload_act_table_set("natural_log_exp_and_others")

                for g in range(MB):
                    pair(g, 0)
                    if g:
                        gate(g - 1)
                    with act.Fori(1, NS // 2) as n2:
                        pair(g, n2)
                    act.wait_ge(r.scan_done, CREDIT + scan_counts(it, g) + NS)
                    last = g * (NS + 1) + NS
                    act.activation(state[:, last:last + 1], r.h[:, 1, 0:1] if bw else r.h[:, 1, TC - 1:TC],
                                   ACT.Copy).then_inc(saved, 1)
                gate(MB - 1)
            post_square(NP)
            post_root(NP)

        @block.vector
        def _(dve):
            def post_centre(i):
                dve.wait_ge(summed, i + 1)
                dve.wait_ge(mean_ready, i + 1)
                for c in range(C):
                    ins = dve.tensor_tensor(res[:, c, :], res[:, c, :], stat, ALU.subtract)
                ins.then_inc(centred, 1)

            def post_norm(i):
                dve.wait_ge(root_ready, i + 1)
                dve.scalar_tensor_tensor(out=ra, in0=stat, scalar=EPS,
                                         in1=r2, op0=ALU.add,
                                         op1=ALU.mult).then_inc(newton, 1)
                dve.wait_ge(newton, i * 2 + 1)
                dve.scalar_tensor_tensor(out=rstd, in0=ra, scalar=-3.0, in1=r0, op0=ALU.add,
                                         op1=ALU.mult).then_inc(newton, 1)
                dve.wait_ge(newton, i * 2 + 2)
                dve.wait_ge(centred, i + 1)
                for c in range(C):
                    ins = dve.scalar_tensor_tensor(out=res[:, c, :], in0=res[:, c, :], scalar=norm_s[:, 0, c:c + 1],
                                                   in1=rstd, op0=ALU.mult, op1=ALU.mult)
                ins.then_inc(scaled if bw else y_out, 1)
                if bw:
                    dve.wait_ge(scaled, i + 1)
                    dve.wait_ge(yf_loaded, i * 16 + 16)
                    for c in range(C):
                        ins = dve.scalar_tensor_tensor(out=res[:, c, :], in0=res[:, c, :], scalar=norm_s[:, 1, c:c + 1],
                                                       in1=yf[:, c, :], op0=ALU.add, op1=ALU.add)
                    ins.then_inc(y_out, 1)

            dve.memset(wx[:], 0.0).then_inc(cleared, 1)
            dve.memset(one, 1.0)
            dve.memset(eps, EPS)
            dve.memset(carry[:, 0:1], 0.0)
            dve.memset(carry[:, 1:2], 1.0)
            dve.memset(res, 0.0).then_inc(summed, 1)
            dve.memset(state[:], 0.0)
            dve_credits(dve, r)
            dve.wait_ge(summed, 1)
            dve.wait_ge(r.scan_done, CREDIT)
            dve.wait_ge(r.prod_ready, CREDIT)
            dve.wait_ge(loaded, LOADS)
            dve.wait_ge(ea_ready, 1)
            for g in range(MB):
                dve.tensor_scalar(diag_d[:, g, :], k.ident[:], dcol[:, g:g + 1], None, ALU.mult)
            dve.tensor_scalar(norm_s[:, 0, :], norm[:, 0, :], -0.5, None, ALU.mult)
            dve.tensor_scalar(norm_s[:, 1, :], norm[:, 1, :], 2.0, None, ALU.mult)
            dve.tensor_scalar(neg_a[:], alog[:], -1.0, None, ALU.mult).then_inc(setup, 1)
            dve.wait_ge(setup, 1)
            both, b, it, tc, t0 = passes(dve)
            with both:
                for g in range(MB):
                    for t in range(1, KC):
                        if t == 1:
                            dve.wait_ge(tap0, it * MB + (g + 1))
                        else:
                            dve.wait_ge(tap_done, it * 12 + (3 * g + t - 1))
                        x0 = PAD - t if bw else t
                        dve.scalar_tensor_tensor(out=u[:, g, :], in0=x_slot[g % 2][:, x0:x0 + TC],
                                                 scalar=taps[:, g, t:t + 1], in1=u[:, g, :], op0=ALU.mult,
                                                 op1=ALU.add).then_inc(tap_done, 1)
                    if g == 0:
                        post_centre(it)
                post_norm(it)
                dve.wait_ge(par_ready, it + 1)
                split_rows(dve, split, it, flatb[0:32, par_bank * TT:par_bank * TT + TC], parts, None, mid, rest)

                def rounded_off(g):
                    s = g % 2
                    dve.wait_ge(exp_done, it * MB + (g + 1))
                    if g > 1:
                        dve.wait_ge(log_sum, it * MB + (g - 1))
                    dve.tensor_scalar(off[s], ex[s], 1.0, -1.0, ALU.add, ALU.add).then_inc(soft_step, 1)
                    dve.wait_ge(soft_step, it * 2 * MB + (2 * g + 1))
                    dve.scalar_tensor_tensor(out=off[s], in0=off[s], scalar=-1.0, in1=ex[s], op0=ALU.mult,
                                             op1=ALU.add).then_inc(soft_step, 1)

                def step_size(g):
                    dve.wait_ge(log_sum, it * MB + (g + 1))
                    dve.scalar_tensor_tensor(out=dt[:, g, :], in0=lin[g % 2], scalar=0.0, in1=lg[g % 2], op0=ALU.max,
                                             op1=ALU.add).then_inc(soft_done, 1)

                def keep_b(n):
                    if n == 15:
                        dve.wait_ge(b_free, it + 1)
                    dve.wait_ge(b_spread, it * NS + n + 1)
                    dve.tensor_copy(brep[:, n, :], flatb[:, b_bank[1] * TT:b_bank[1] * TT + TC]).then_inc(b_dve, 1)

                dve.wait_ge(y_out, it + 1)
                rounded_off(0)
                for g in range(MB):
                    keep_b(2 * g + 1)
                    if g + 1 < MB:
                        rounded_off(g + 1)
                    step_size(g)
                for n in range(2 * MB + 1, NS, 2):
                    keep_b(n)
                dve.tensor_scalar(state[:], state[:], carry[:, ds(tc, 1)], None, ALU.mult).then_inc(started, 1)
                dve.wait_ge(started, it + 1)
                step = slice(None, None, -1) if bw else slice(None)

                def pair(g, n2):
                    for j in range(2):
                        un = scan_counts(it, g) + n2 * 2 + j
                        at = n2 * 2 + (1 + g * (NS + 1) + j)
                        dve.wait_ge(r.decay_ready, un + 1)
                        dve.wait_ge(r.drive_ready, un + 1)
                        dve.wait_ge(r.prod_ready, CREDIT + un - 1)
                        dve.tensor_tensor_scan(r.h[:, j, step], decay_sb[:, j, step], r.drive[:, j, step],
                                               state[:, at:at + 1] if isinstance(at, int) else state[:, ds(at, 1)],
                                               ALU.mult, ALU.add).then_inc(r.scan_done, 1)
                        dve.wait_ge(r.scan_done, CREDIT + un + 1)
                        dve.wait_ge(r.chat_ready, un + 1)
                        dve.wait_ge(r.sum_done, CREDIT + un - 1)
                        dve.tensor_tensor(r.prod[:, j, :], flat(r.chat), r.h[:, j, :],
                                          ALU.mult).then_inc(r.prod_ready, 1)

                def gate_y(g):
                    dve.wait_ge(r.sum_done, CREDIT + scan_counts(it, g) + NS)
                    dve.wait_ge(gate_ready, it * MB + (g + 1))
                    dve.tensor_tensor(u[:, g, :], flat(y_banks[g % 2]), dtu[:, g, :], ALU.mult).then_inc(gated, 1)

                for g in range(MB):
                    pair(g, 0)
                    if g:
                        gate_y(g - 1)
                    with dve.Fori(1, NS // 2) as n2:
                        pair(g, n2)
                gate_y(MB - 1)
                dve.wait_ge(out_ready, it + 1)
                dve.tensor_tensor(res, banks[:, 0:4, :].rearrange("p (c q) t -> p c (q t)", c=C),
                                  k.xn[:, :, b, ds(t0 + PAD, TC)], ALU.add).then_inc(summed, 1)
            post_centre(NP)
            post_norm(NP)

        @block.tensor
        def _(pe):
            def post_mean(i):
                pe.wait_ge(summed, i + 1)
                for q in range(2):
                    for c in range(C):
                        mm = pe.matmul(banks[:, q, :], k.mean[:], res[:, c, q * TT:(q + 1) * TT],
                                       start=c == 0, stop=c == C - 1)
                mm.then_inc(mean_ready, 1)

            def post_var(i):
                pe.wait_ge(squared, i + 1)
                for q in range(2):
                    for c in range(C):
                        mm = pe.matmul(banks[:, q, :], k.mean[:], sq[:, c, q * TT:(q + 1) * TT],
                                       start=c == 0, stop=c == C - 1)
                mm.then_inc(var_ready, 1)

            pe.sem_inc(r.sum_done, CREDIT)
            pe.wait_ge(loaded, LOADS)
            pe.wait_ge(setup, 1)
            both, b, it, tc, t0 = passes(pe)
            with both:
                for g in range(MB):
                    if g > 1:
                        pe.wait_ge(xi_kept, it * MB + (g - 1))
                    for q, n in ((0, TT), (1, TT), (2, PAD)):
                        for c in range(C):
                            mm = pe.matmul(banks[:, x_bank[g % 2] + q, 0:n], win[:, c, g * P:(g + 1) * P],
                                           k.xn[:, c, b, ds(t0 + ((PAD if bw else 0) + q * TT), n)],
                                           start=c == 0, stop=c == C - 1)
                    mm.then_inc(xi_ready, 1)
                    if g == 0:
                        post_mean(it)
                    if g == 2:
                        post_var(it)
                pe.wait_ge(xi_kept, it * MB + 3)
                for g in range(MB):
                    pe.wait_ge(u_ready, it * MB + (g + 1))
                    for q in range(2):
                        mm = pe.matmul(banks[0:64 + R, par_bank + q, :], wx[:, g, :], u[:, g, q * TT:(q + 1) * TT],
                                       start=g == 0, stop=g == MB - 1)
                mm.then_inc(par_ready, 1)

                def step_rows(g):
                    if g > 1:
                        pe.wait_ge(abs_done, it * MB + (g - 1))
                    for q in range(2):
                        mm = pe.matmul(banks[:, dt_bank[g % 2] + q, :], wdt[:, g * P:(g + 1) * P],
                                       dtin[:, q * TT:(q + 1) * TT], start=True, stop=True)
                    mm.then_inc(dt_ready, 1)

                def spread_b(n):
                    if n > 1:
                        pe.wait_ge(b_act if n % 2 == 0 else b_dve, it * 8 + n // 2)
                    for q in range(2):
                        mm = pe.matmul(banks[:, b_bank[n % 2] + q, :], k.sel[:, n, :],
                                       parts[:, q * TT:(q + 1) * TT], start=True, stop=True)
                    mm.then_inc(b_spread, 1)

                pe.wait_ge(dtin_kept, it + 1)
                pe.wait_ge(xi_kept, it * MB + MB)
                step_rows(0)
                pe.wait_ge(newton, it * 2 + 1)
                step_rows(1)
                pe.wait_ge(split, it * 5 + 5)
                for n in range(NS):
                    if n in (2, 4):
                        step_rows(1 + n // 2)
                    spread_b(n)
                pe.wait_ge(b_act, it * 8 + 8)
                pe.wait_ge(b_dve, it * 8 + 8)
                pe.wait_ge(abs_done, it * MB + MB)

                def spread_c(un, n):
                    for q in range(2):
                        mm = pe.matmul(r.chat[:, q, :], k.sel[:, NS + n, :] if isinstance(n, int)
                                       else k.sel[:, ds(n + NS, 1), :], parts[:, q * TT:(q + 1) * TT],
                                       start=True, stop=True)
                    mm.then_inc(r.chat_ready, 1)

                def add(g, j):
                    for q in range(2):
                        mm = pe.matmul(y_banks[g % 2][:, q, :], k.ident[:], r.prod[:, j, q * TT:(q + 1) * TT],
                                       start=False, stop=True, skip_group_check=True)
                    mm.then_inc(r.sum_done, 1)

                SLICE = 2 * TC // NS

                def z_slice(g, n2):
                    for c in range(C):
                        mm = pe.matmul(z_banks[:, n2 * SLICE:(n2 + 1) * SLICE] if isinstance(n2, int)
                                       else z_banks[:, ds(n2 * SLICE, SLICE)],
                                       win[:, c, D2 + g * P:D2 + (g + 1) * P],
                                       k.xn[:, c, b, ds(t0 + n2 * SLICE + PAD, SLICE)],
                                       start=c == 0, stop=c == C - 1)
                    return mm

                for g in range(MB):
                    base = scan_counts(it, g)
                    if g == 0:
                        spread_c(base, 0)
                    if g > 1:
                        pe.wait_ge(gated, it * MB + (g - 1))
                    for q in range(2):
                        pe.matmul(y_banks[g % 2][:, q, :], diag_d[:, g, :], u[:, g, q * TT:(q + 1) * TT], start=True,
                                  stop=True, skip_group_check=True)
                    with pe.Fori(0, NS // 2 - 1) as n2:
                        for j in range(2):
                            un = base + n2 * 2 + j
                            pe.wait_ge(r.prod_ready, CREDIT + un + 1)
                            spread_c(un + 1, n2 * 2 + (j + 1))
                            add(g, j)
                        if g:
                            pe.wait_ge(gate_ready, it * MB + g)
                        z_slice(g, n2)
                    pe.wait_ge(r.prod_ready, CREDIT + base + NS - 1)
                    spread_c(base + NS - 1, NS - 1)
                    add(g, 0)
                    z_slice(g, NS // 2 - 1).then_inc(z_ready, 1)
                    pe.wait_ge(r.prod_ready, CREDIT + base + NS)
                    if g + 1 < MB:
                        spread_c(base + NS, 0)
                    add(g, 1)

                def project(c, g):
                    for q in range(2):
                        mm = pe.matmul(banks[:, 2 * c + q, :], wout[:, g, c * P:(c + 1) * P],
                                       u[:, g, q * TT:(q + 1) * TT], start=g == 0, stop=g == MB - 1)
                    return mm

                for c in (1, 0):
                    if c == 1:
                        pe.wait_ge(gated, it * MB + 3)
                    else:
                        pe.wait_ge(gate_ready, it * MB + MB)
                    for g in range(MB - 1):
                        project(c, g)
                pe.wait_ge(gated, it * MB + MB)
                project(1, MB - 1)
                project(0, MB - 1).then_inc(out_ready, 1)
            post_mean(NP)
            post_var(NP)


H = 1024
HB = H // P
LANE = 7
ACROSS = 3


def butterfly(nc, k, tag, x, spare, width, own, cross, upward):
    with ExitStack() as ctx:
        m = Mem(nc, ctx, tag)
        swap, mat = m.sb("swap", [P, LANE, P]), m.sb("mat", [P, 2, P])
        banks = m.ps("banks", [P, 2, TT])
        swapped, half, mat_ready = m.sem("swapped"), m.sem("half"), m.sem("mat_ready")
        turned, kept, scaled, crossed, ready = m.sem("turned"), m.sem("kept"), m.sem("scaled"), m.sem("crossed"), m.sem("ready")
        first = 0 if upward else ACROSS
        start_across = LANE if upward else 0
        block = ctx.enter_context(nc.Block())

        def across(dve):
            a, b = x, spare
            for n in range(ACROSS):
                st = start_across + n
                stride = 1 << (n if upward else ACROSS - 1 - n)
                if n:
                    dve.wait_ge(crossed, n * HB)
                for j in range(HB):
                    dve.tensor_scalar(b[:, j, 0:width], a[:, j, 0:width], own[:, st, j:j + 1], None, ALU.mult).then_inc(scaled, 1)
                for j in range(HB):
                    dve.wait_ge(scaled, n * HB + j + 1)
                    dve.scalar_tensor_tensor(out=b[:, j, 0:width], in0=a[:, j ^ stride, 0:width], scalar=cross[:, st, j:j + 1],
                                             in1=b[:, j, 0:width], op0=ALU.mult, op1=ALU.add).then_inc(crossed, 1)
                a, b = b, a
            dve.wait_ge(crossed, ACROSS * HB)
            dve.tensor_copy(x[:], spare[:]).then_inc(ready, 1)

        @block.vector
        def _(dve):
            for n in range(LANE):
                s = 1 << (n if upward else LANE - 1 - n)
                for side in range(2):
                    ins = dve.tensor_copy(swap[:, n, :].rearrange("p (a two s) -> p a two s", two=2, s=s)[:, :, side, :],
                                          k.ident[:].rearrange("p (a two s) -> p a two s", two=2, s=s)[:, :, 1 - side, :])
            ins.then_inc(swapped, 1)
            if not upward:
                across(dve)
            dve.wait_ge(swapped, 1)
            with dve.Fori(0, LANE) as n:
                for j in range(HB):
                    i = n * HB + j
                    dve.wait_ge(turned, i + 1)
                    dve.tensor_scalar(mat[:, j % 2, :], k.ident[:], own[:, ds(n + first, 1), j], None,
                                      ALU.mult).then_inc(half, 1)
                    dve.wait_ge(half, i + 1)
                    dve.scalar_tensor_tensor(out=mat[:, j % 2, :], in0=swap[:, ds(n, 1), :].rearrange("p n q -> p (n q)"),
                                             scalar=cross[:, ds(n + first, 1), j], in1=mat[:, j % 2, :], op0=ALU.mult,
                                             op1=ALU.add).then_inc(mat_ready, 1)
            if upward:
                dve.wait_ge(kept, 2 + LANE * HB)
                across(dve)

        @block.tensor
        def _(pe):
            pe.sem_inc(turned, 2)
            if not upward:
                pe.wait_ge(ready, 1)
            with pe.Fori(0, LANE) as n:
                for j in range(HB):
                    i = n * HB + j
                    pe.wait_ge(mat_ready, i + 1)
                    pe.wait_ge(kept, i + 1)
                    pe.matmul(banks[:, j % 2, 0:width], mat[:, j % 2, :], x[:, j, 0:width], start=True,
                              stop=True).then_inc(turned, 1)

        @block.scalar
        def _(act):
            act.sem_inc(kept, 2)
            with act.Fori(0, LANE) as n:
                for j in range(HB):
                    i = n * HB + j
                    act.wait_ge(turned, 2 + (i + 1))
                    act.activation(x[:, j, 0:width], banks[:, j % 2, 0:width], ACT.Copy).then_inc(kept, 1)


def last(nc, k, out):
    FF = 512
    FB = FF // P
    a = k.a
    W = E + 1
    with ExitStack() as keep:
        mk = Mem(nc, keep, "fin")
        up, down = mk.sb("up", [P, HB, W]), mk.sb("down", [P, HB, W])
        up_b, w_up = mk.sb("up_b", [P, HB]), mk.sb("w_up", [P, C, H])
        w1, w2, b1 = mk.sb("w1", [P, C, FF]), mk.sb("w2", [P, FB, E]), mk.sb("b1", [P, FB])
        vec = mk.sb("vec", [P, 5, C])
        add_b = mk.sb("add_b", [P, C])
        with ExitStack() as ctx:
            m = Mem(nc, ctx, "fina")
            spare = m.sb("spare", [P, HB, W])
            fac = m.sb("fac", [P, 4, LANE + ACROSS, HB])
            with ExitStack() as ctx2:
                loaded = Mem(nc, ctx2, "finl").sem("loaded")
                filled = Mem(nc, ctx2, "finl").sem("filled")
                block = ctx2.enter_context(nc.Block())

                @block.sync
                def _(sp):
                    sp.wait_ge(filled, 1)
                    n = 0
                    for dst, src in ((up[:], a["exp"].rearrange("(j p) e -> p j e", p=P)), (down[:, :, 0:E], a["W_con"].rearrange("(j p) e -> p j e", p=P)),
                                     (fac[:], a["factors"]), (up_b[:], a["up_bias"]),
                                     (w1[:], a["W1"].rearrange("(c p) m -> p c m", p=P)),
                                     (w2[:], a["W2"].rearrange("(c p) m -> p c m", p=P)), (b1[:], a["b1"]),
                                     (vec[:], a["vec"])):
                        sp.dma_start(dst, src).then_inc(loaded, 16)
                        n += 16
                    sp.wait_ge(loaded, n)

                @block.vector
                def _(dve):
                    dve.memset(down[:, :, E:W], 0.0)
                    dve.memset(spare[:, :, E:W], 0.0).then_inc(filled, 1)
            butterfly(nc, k, "bup", up, spare, W, fac[:, 0], fac[:, 1], True)
            butterfly(nc, k, "bdn", down, spare, E, fac[:, 2], fac[:, 3], False)

        with ExitStack() as ctx:
            m = Mem(nc, ctx, "finb")
            y, x1 = m.sb("y", [P, 2, C, TT]), m.sb("x1", [P, 2, C, TT])
            f, g = m.sb("f", [P, FB, TT]), m.sb("g", [P, HB, TT])
            res, sq, o = m.sb("res", [P, C, TT]), m.sb("sq", [P, C, TT]), m.sb("o", [P, 2, C, TT])
            logv, r0, ra, rb, rstd = (m.sb(n, [P, TT]) for n in ("logv", "r0", "ra", "rb", "rstd"))
            eps = m.sb("eps", [P, 1])
            banks = m.ps("banks", [P, 8, TT])
            (turned, w_ready, f_ready, f_kept, ff_ready, summed, up_ready, g_ready, mean_ready, centred, squared, var_ready,
             logged, root_ready, newton, step, down_ready, o_ready) = (m.sem(n) for n in (
                 "turned w_ready f_ready f_kept ff_ready summed up_ready g_ready mean_ready centred squared var_ready "
                 "logged root_ready newton step down_ready o_ready").split())
            loaded = [m.sem(f"loaded{j}") for j in range(2)]
            stored = [m.sem(f"stored{j}") for j in range(2)]
            slot_free = m.sem("slot_free")
            NT = T // TT
            STEPS = 8
            block = ctx.enter_context(nc.Block())

            @block.sync
            def _(sp):
                yd, xd, od = (v.rearrange("(c p) t -> p c t", p=P) for v in (k.y, k.x1, out))
                with sp.Fori(0, NT // 2) as i2:
                    for j in range(2):
                        i = i2 * 2 + j
                        sp.wait_ge(o_ready, i + 1)
                        sp.dma_start(y[:, j], yd[:, :, ds(i * TT + L, TT)]).then_inc(loaded[j], 16)
                        sp.dma_start(x1[:, j], xd[:, :, ds(i * TT, TT)]).then_inc(loaded[j], 16)

            @block.gpsimd
            def _(pool):
                od = out.rearrange("(c p) t -> p c t", p=P)
                pool.sem_inc(slot_free, 1)
                with pool.Fori(0, NT // 2) as i2:
                    for j in range(2):
                        i = i2 * 2 + j
                        pool.wait_ge(o_ready, 2 + (i + 1))
                        pool.dma_start(od[:, :, ds(i * TT, TT)], o[:, j]).then_inc(stored[j], 16)
                        pool.wait_ge(stored[j], i2 * 16 + 16)
                        pool.sem_inc(slot_free, 1)

            @block.tensor
            def _(pe):
                for j in range(HB):
                    for c in range(C):
                        n = j * C + c
                        if n >= 4:
                            pe.wait_ge(w_ready, n - 3)
                        pe.transpose(banks[:, n % 4, 0:P], up[:, j, c * P:(c + 1) * P], k.ident[:]).then_inc(turned, 1)
                pe.wait_ge(w_ready, HB * C)
                with pe.Fori(0, NT // 2) as i2:
                    for j in range(2):
                        i = i2 * 2 + j
                        pe.wait_ge(loaded[j], i2 * 32 + 32)
                        pe.wait_ge(o_ready, 2 + i)
                        for h in range(FB):
                            for c in range(C):
                                mm = pe.matmul(banks[:, h, :], w1[:, c, h * P:(h + 1) * P], y[:, j, c, :],
                                               start=c == 0, stop=c == C - 1)
                            mm.then_inc(f_ready, 1)
                        for h in range(FB):
                            pe.wait_ge(f_kept, i * FB + (h + 1))
                        for c in range(C):
                            for h in range(FB):
                                mm = pe.matmul(banks[:, 6 + c, :], w2[:, h, c * P:(c + 1) * P], f[:, h, :],
                                               start=h == 0, stop=h == FB - 1)
                        mm.then_inc(ff_ready, 1)

                        def up_block(h):
                            if h >= 4:
                                pe.wait_ge(g_ready, i * HB + (h - 3))
                            for c in range(C):
                                mm = pe.matmul(banks[:, h % 4, :], w_up[:, c, h * P:(h + 1) * P],
                                               xnow(c, i2, j), start=c == 0, stop=c == C - 1)
                            mm.then_inc(up_ready, 1)

                        def xnow(c, i2, j):
                            return k.xn[:, c, :, :].rearrange("p b t -> p (b t)")[
                                :, ds(i2 * (2 * TT) + (i2 // 2) * (2 * PAD) + (j * TT + PAD), TT)]

                        for h in range(4):
                            up_block(h)
                        pe.wait_ge(summed, i + 1)
                        for c in range(C):
                            mm = pe.matmul(banks[:, 6, :], k.mean[:], res[:, c, :], start=c == 0, stop=c == C - 1)
                        mm.then_inc(mean_ready, 1)
                        for h in range(4, HB):
                            up_block(h)
                        pe.wait_ge(squared, i + 1)
                        for c in range(C):
                            mm = pe.matmul(banks[:, 7, :], k.mean[:], sq[:, c, :], start=c == 0, stop=c == C - 1)
                        mm.then_inc(var_ready, 1)
                        for h in range(HB):
                            pe.wait_ge(g_ready, i * HB + (h + 1))
                            for c in range(C):
                                mm = pe.matmul(banks[:, 4 + c, :], down[:, h, c * P:(c + 1) * P], g[:, h, :],
                                               start=h == 0, stop=h == HB - 1)
                        mm.then_inc(down_ready, 1)

            @block.scalar
            def _(act):
                act.wait_ge(w_ready, HB * C)
                with act.Fori(0, NT) as i:
                    for h in range(FB):
                        act.wait_ge(f_ready, i * FB + (h + 1))
                        act.activation(f[:, h, :], banks[:, h, :], ACT.Relu, bias=b1[:, h:h + 1]).then_inc(f_kept, 1)

                    def gelu(h):
                        act.wait_ge(up_ready, i * HB + (h + 1))
                        act.activation(g[:, h, :], banks[:, h % 4, :], ACT.Gelu, bias=up_b[:, h:h + 1]).then_inc(g_ready, 1)

                    for h in range(4):
                        gelu(h)
                    act.wait_ge(centred, i + 1)
                    act.activation(sq[:], res[:], ACT.Square).then_inc(squared, 1)
                    for h in range(4, HB):
                        gelu(h)
                    act.preload_act_table_set("natural_log_exp_and_others")
                    act.wait_ge(var_ready, i + 1)
                    act.activation(logv[:], banks[:, 7, :], ACT.Ln, bias=eps[:, 0:1]).then_inc(logged, 1)
                    act.wait_ge(logged, i + 1)
                    act.activation(r0[:], logv[:], ACT.Exp, scale=-0.5).then_inc(root_ready, 1)

            @block.vector
            def _(dve):
                dve.memset(eps[:], EPS)
                for j in range(HB):
                    for c in range(C):
                        n = j * C + c
                        dve.wait_ge(turned, n + 1)
                        dve.tensor_copy(w_up[:, c, j * P:(j + 1) * P], banks[:, n % 4, 0:P]).then_inc(w_ready, 1)
                dve.tensor_tensor(up_b[:], up_b[:], up[:, :, E:W].rearrange("p j o -> p (j o)"), ALU.add)
                dve.tensor_tensor(add_b[:], vec[:, 3, :], vec[:, 4, :], ALU.add).then_inc(o_ready, 2)
                dve.wait_ge(o_ready, 2)
                with dve.Fori(0, NT // 2) as i2:
                    for j in range(2):
                        i = i2 * 2 + j
                        dve.wait_ge(ff_ready, i + 1)
                        dve.wait_ge(loaded[j], i2 * 32 + 32)
                        for c in range(C):
                            ins = dve.scalar_tensor_tensor(out=res[:, c, :], in0=banks[:, 6 + c, :], scalar=vec[:, 0, c:c + 1],
                                                           in1=y[:, j, c, :], op0=ALU.add, op1=ALU.add)
                        ins.then_inc(summed, 1)
                        dve.wait_ge(summed, i + 1)
                        dve.wait_ge(mean_ready, i + 1)
                        for c in range(C):
                            ins = dve.tensor_tensor(res[:, c, :], res[:, c, :], banks[:, 6, :], ALU.subtract)
                        ins.then_inc(centred, 1)
                        dve.wait_ge(root_ready, i + 1)
                        dve.scalar_tensor_tensor(out=ra[:], in0=banks[:, 7, :], scalar=EPS, in1=r0[:], op0=ALU.add,
                                                 op1=ALU.mult).then_inc(newton, 1)
                        dve.wait_ge(newton, i * 3 + 1)
                        dve.scalar_tensor_tensor(out=rb[:], in0=ra[:], scalar=-0.5, in1=r0[:], op0=ALU.mult,
                                                 op1=ALU.mult).then_inc(newton, 1)
                        dve.wait_ge(newton, i * 3 + 2)
                        dve.scalar_tensor_tensor(out=rstd[:], in0=rb[:], scalar=1.5, in1=r0[:], op0=ALU.add,
                                                 op1=ALU.mult).then_inc(newton, 1)
                        dve.wait_ge(newton, i * 3 + 3)
                        for c in range(C):
                            dve.tensor_tensor(res[:, c, :], res[:, c, :], rstd[:], ALU.mult).then_inc(step, 1)
                        for c in range(C):
                            dve.wait_ge(step, i * STEPS + (c + 1))
                            dve.tensor_scalar(res[:, c, :], res[:, c, :], vec[:, 1, c:c + 1], vec[:, 2, c:c + 1],
                                              ALU.mult, ALU.add).then_inc(step, 1)
                        for c in range(C):
                            dve.wait_ge(step, i * STEPS + (3 + c))
                            dve.tensor_tensor(res[:, c, :], res[:, c, :], x1[:, j, c, :], ALU.add).then_inc(step, 1)
                        dve.wait_ge(down_ready, i + 1)
                        dve.wait_ge(slot_free, i + 1)
                        for c in range(C):
                            dve.wait_ge(step, i * STEPS + (5 + c))
                            ins = dve.scalar_tensor_tensor(out=o[:, j, c, :], in0=banks[:, 4 + c, :], scalar=add_b[:, c:c + 1],
                                                           in1=res[:, c, :], op0=ALU.add, op1=ALU.add)
                            ins.then_inc(step, 1)
                        dve.wait_ge(step, i * STEPS + 8)
                        dve.memset(eps[:], EPS).then_inc(o_ready, 1)


class Kept:
    pass


def program(nc, a, out):
    Mem.used = []
    with ExitStack() as ctx:
        m = Mem(nc, ctx, "kept")
        k = Kept()
        k.ident = m.sb("ident", [P, P])
        k.mean = m.sb("mean", [P, P])
        k.sel = m.sb("sel", [96, 32, P], BF16)
        k.xn = m.sb("xn", [P, C, B, LP])
        k.a = a
        k.x1 = nc.dram_tensor("x1_scratch", (E, T), F32, kind="Internal").ap()
        k.yf, k.y = (nc.dram_tensor(n, (E, L + T), F32, kind="Internal").ap() for n in ("fw_scratch", "both_scratch"))
        constants(nc, k)
        with ExitStack() as first:
            acc = Mem(nc, first, "first").sb("acc", [P, C, T])
            layernorm(nc, k, acc, a["xT"])
            mixer0(nc, k, acc)
            experts0(nc, k, acc)
            layernorm(nc, k, acc, save=k.x1)
        clear_semaphores(nc)
        mixer1(nc, k, "fw", None, k.yf)
        mixer1(nc, k, "bw", k.yf, k.y)
        last(nc, k, out)


def _factors(w, upward):
    import numpy as np

    i = np.arange(H)
    own, cross = [], []
    for stage in range(LANE + ACROSS):
        s = 1 << stage
        bit, pair = i // s % 2, i // (2 * s) * s + i % s
        own.append(w[stage, pair, bit, bit])
        leaves = w[stage, pair, 1 - bit, bit]
        arrives = w[stage, pair, bit, 1 - bit]
        cross.append(leaves if (stage < LANE) == upward else arrives)
    order = list(range(LANE + ACROSS)) if upward else list(range(LANE + ACROSS))[::-1]
    return [np.stack([v[n].reshape(HB, P).T for n in order], axis=1) for v in (own, cross)]


def _laid_out(i):
    import numpy as np

    def arr(name):
        return np.asarray(i[name])

    def cols(name):
        return arr(name).reshape(-1, P).T

    a = {"xT": arr("L0_attn_x").transpose(2, 0, 1).reshape(E, T),
         "W_z": arr("L0_attn_W_z").T, "W_out": arr("L0_attn_W_out").T, "W_par": arr("L0_attn_W_params").T,
         "W_dt": arr("L0_attn_W_dt").T, "conv_w": arr("L0_attn_conv_w")[:, 0], "b_dt": cols("L0_attn_b_dt"),
         "A_log": arr("L0_attn_A_log"), "D": cols("L0_attn_D"),
         "controller": arr("L0_ffn_controller").reshape(E, -1), "f1": arr("L0_ffn_f1").reshape(E, 64, 64),
         "f2": arr("L0_ffn_f2").reshape(64, 64, E), "bias": arr("L0_ffn_bias").reshape(64, 64).T,
         "tie": np.broadcast_to(np.linspace(0.0, 1e-6, 16, dtype=np.float32), (P, 32, 16))}
    for way in ("fw", "bw"):
        for w in ("Win", "Wout", "Wx", "Wdt", "convw", "Alog"):
            a[f"{way}_{w}"] = arr(f"L1_attn_{way}_{w}")
        for w in ("convb", "bdt", "D"):
            a[f"{way}_{w}"] = cols(f"L1_attn_{way}_{w}")
    for w in ("fwn", "fin"):
        a[w] = np.stack([cols(f"L1_attn_{w}_w"), cols(f"L1_attn_{w}_b")], axis=1)
    a["W1"], a["W2"] = arr("L1_attn_ff_W1"), arr("L1_attn_ff_W2")
    a["b1"] = cols("L1_attn_ff_b1")
    a["vec"] = np.stack([cols(n) for n in ("L1_attn_ff_b2", "L1_attn_fin_w", "L1_attn_fin_b", "L1_ffn_b_con",
                                           "L1_ffn_down_bias")], axis=1)
    a["exp"] = np.concatenate([arr("L1_ffn_W_exp").T, arr("L1_ffn_b_exp")[:, None]], axis=1)
    a["W_con"], a["up_bias"] = arr("L1_ffn_W_con"), cols("L1_ffn_up_bias")
    a["factors"] = np.stack(_factors(arr("L1_ffn_up_weights"), True) + _factors(arr("L1_ffn_down_weights"), False),
                            axis=1)
    return {n: np.ascontiguousarray(v) for n, v in a.items()}


def kernel(**inputs):
    import concourse.bacc as _bacc
    from concourse.bass_utils import run_bass_kernel_spmd as _run

    nc = _bacc.Bacc("TRN2", target_bir_lowering=False, num_devices=1)
    arrays = _laid_out(inputs)
    args = {n: nc.dram_tensor(n, v.shape, mybir.dt.from_np(v.dtype), kind="ExternalInput").ap()
            for n, v in arrays.items()}
    out = nc.dram_tensor("out", (E, T), F32, kind="ExternalOutput").ap()
    program(nc, args, out)
    r = _run(nc, [arrays], core_ids=[0])
    return r.results[0]["out"].reshape(E, B, L).transpose(1, 2, 0)
```

```python
from contextlib import ExitStack

import concourse.bass as bass
from concourse import mybir

ALU = mybir.AluOpType
ACT = mybir.ActivationFunctionType
F32 = mybir.dt.float32
BF16 = mybir.dt.bfloat16
AX = mybir.AxisListType

P = 128
E = 256
C = E // P
B = 2
L = 2048
T = B * L
TT = 512
TC = 1024
NS = 16
KC = 4
PAD = KC - 1
LP = L + 2 * PAD
GROUPS = 4
UNITS = GROUPS * NS
CREDIT = 2
EPS = 1e-5
ds = bass.ds


class Mem:

    used = []

    def __init__(self, nc, ctx, tag):
        self.nc, self.ctx, self.tag = nc, ctx, tag

    def sb(self, name, shape, dt=F32):
        return self.ctx.enter_context(self.nc.sbuf_tensor(f"{self.tag}_{name}", shape, dt))

    def ps(self, name, shape, dt=F32):
        return self.ctx.enter_context(self.nc.psum_tensor(f"{self.tag}_{name}", shape, dt))

    def sem(self, name):
        Mem.used.append(self.nc.alloc_semaphore(name=f"{self.tag}_{name}"))
        return Mem.used[-1]


def clear_semaphores(nc):
    nc.clear_and_free_semaphores(Mem.used)
    nc.all_engine_barrier()
    Mem.used = []


def constants(nc, k):
    with ExitStack() as ctx:
        m = Mem(nc, ctx, "const")
        zeroed, step = m.sem("zeroed"), m.sem("step")
        block = ctx.enter_context(nc.Block())

        @block.vector
        def _(dve):
            dve.memset(k.mean[:], 1.0 / E)
            dve.memset(k.xn[:, :, :, 0:PAD], 0.0)
            dve.memset(k.xn[:, :, :, PAD + L:LP], 0.0).then_inc(zeroed, 1)

        @block.gpsimd
        def _(pool):
            pool.memset(k.ident[:], 0.0).then_inc(step, 1)
            pool.wait_ge(step, 1)
            pool.affine_select(out=k.ident[:], in_=k.ident[:], compare_op=ALU.not_equal, fill=1.0,
                               base=0, pattern=[[-1, P]], channel_multiplier=1).then_inc(step, 1)


def selectors(pool, k, built):
    pool.memset(k.sel[:], 0.0).then_inc(built, 1)
    for part in range(3):
        pool.wait_ge(built, 1 + part)
        pool.affine_select(out=k.sel[:], in_=k.sel[:], compare_op=ALU.not_equal, fill=1.0, base=-32 * part,
                           pattern=[[-1, 32], [0, P]], channel_multiplier=1).then_inc(built, 1)


def layernorm(nc, k, src, load=None, save=None, before=None):
    with ExitStack() as ctx:
        m = Mem(nc, ctx, "ln" if load is not None else "ln1")
        stat, var = m.ps("mean", [P, 2, TT]), m.ps("var", [P, 2, TT])
        sq = m.sb("sq", [P, 2, C, TT])
        logv, r0, r2, ra, rstd = (m.sb(n, [P, 2, TT]) for n in ("logv", "r0", "r2", "ra", "rstd"))
        half_mean = m.sb("half_mean", [P, P])
        epst = m.sb("eps", [P, 1])
        PB = L // TT
        set_up, mean_ready, centred = m.sem("set_up"), m.sem("mean_ready"), m.sem("centred")
        squared, var_ready, root, root_ready = m.sem("squared"), m.sem("var_ready"), m.sem("root"), m.sem("root_ready")
        logged, newton, normed, saved = m.sem("logged"), m.sem("newton"), m.sem("normed"), m.sem("saved")
        loaded = [m.sem(f"loaded{q}") for q in range(PB)] if load is not None else None
        if before is not None:
            before.place(m)
        block = ctx.enter_context(nc.Block())

        def staggered(first_half, second_half, ahead=None):
            if ahead is not None:
                ahead(0)
            for q in range(PB):
                if ahead is not None and q + 1 < PB:
                    ahead(q + 1)
                first_half(q)
                if q:
                    second_half(q - 1)
            second_half(PB - 1)

        @block.sync
        def _(sp):
            if load is not None:
                with sp.Fori(0, B) as b:
                    for q in range(PB):
                        sp.wait_ge(centred, b * (q + 2) + 1)
                        sp.dma_start(src[:, :, ds(b * L + q * TT, TT)],
                                     load.rearrange("(c p) t -> p c t", p=P)[:, :, ds(b * L + q * TT, TT)]
                                     ).then_inc(loaded[q], 16)
            if before is not None:
                with sp.Fori(0, B) as b:
                    for q in range(PB):
                        before.load(sp, b * PB + q, b * (PB // 2) + q // 2, q % 2)

        @block.gpsimd
        def _(pool):
            pool.sem_inc(normed, 2)
            with pool.Fori(0, B) as b:
                for q in range(PB):
                    i = b * PB + q
                    if save is not None:
                        pool.wait_ge(before.added, 2 + (i + 1))
                        pool.dma_start(save.rearrange("(c p) t -> p c t", p=P)[:, :, ds(b * L + q * TT, TT)],
                                       src[:, :, ds(b * L + q * TT, TT)]).then_inc(saved, 16)
                    pool.wait_ge(newton, 4 + 2 * i + 2)
                    for c in range(C):
                        xs = k.xn[:, c, b, ds(PAD + q * TT, TT)]
                        ins = pool.tensor_tensor(xs, xs, rstd[:, q % 2, :], ALU.mult)
                    ins.then_inc(normed, 1)
            if save is not None:
                pool.wait_ge(saved, 16 * B * PB)

        @block.tensor
        def _(pe):
            if before is not None:
                pe.sem_inc(before.out_ready, 2)
            pe.sem_inc(var_ready, 2)
            pe.wait_ge(set_up, 1)
            with pe.Fori(0, B) as b:
                def means(q):
                    i = b * PB + q
                    if load is not None:
                        pe.wait_ge(loaded[q], b * 16 + 16)
                    if before is not None:
                        pe.wait_ge(before.added, 2 + (i + 1))
                    pe.wait_ge(centred, i + 1)
                    for c in range(C):
                        mm = pe.matmul(stat[:, q % 2, :], half_mean[:], src[:, c, ds(b * L + q * TT, TT)],
                                       start=c == 0, stop=c == C - 1)
                    mm.then_inc(mean_ready, 1)

                def variances(q):
                    i = b * PB + q
                    pe.wait_ge(squared, i + 1)
                    pe.wait_ge(newton, 4 + 2 * i - 2)
                    for c in range(C):
                        mm = pe.matmul(var[:, q % 2, :], k.mean[:], sq[:, q % 2, c, :], start=c == 0, stop=c == C - 1)
                    mm.then_inc(var_ready, 1)

                staggered(means, variances, before and (lambda q: before.products(pe, b * PB + q, b * (PB // 2) + q // 2, q % 2)))

        @block.scalar
        def _(act):
            act.preload_act_table_set("natural_log_exp_and_others")
            act.wait_ge(set_up, 1)
            with act.Fori(0, B) as b:
                def squares(q):
                    i = b * PB + q
                    act.wait_ge(centred, 2 + (i + 1))
                    act.wait_ge(var_ready, 1 + i)
                    act.activation(sq[:, q % 2], k.xn[:, :, b, ds(PAD + q * TT, TT)], ACT.Square,
                                   scale=2.0).then_inc(squared, 1)

                def roots(q):
                    i = b * PB + q
                    act.wait_ge(var_ready, 2 + (i + 1))
                    act.wait_ge(newton, 4 + 2 * i - 2)
                    act.activation(logv[:, q % 2, :], var[:, q % 2, :], ACT.Ln, bias=epst[:, 0:1]).then_inc(logged, 1)
                    act.wait_ge(logged, i + 1)
                    act.activation(r0[:, q % 2, :], logv[:, q % 2, :], ACT.Exp, scale=-0.5).then_inc(root, 1)
                    act.wait_ge(root, i + 1)
                    act.activation(r2[:, q % 2, :], r0[:, q % 2, :], ACT.Square).then_inc(root_ready, 1)

                staggered(squares, roots)

        @block.vector
        def _(dve):
            dve.memset(epst[:], EPS)
            dve.memset(half_mean[:], 0.5 / E).then_inc(set_up, 1)
            if before is not None:
                dve.sem_inc(before.added, 2)
            dve.sem_inc(centred, 2)
            dve.sem_inc(newton, 4)
            with dve.Fori(0, B) as b:
                def centre(q):
                    i = b * PB + q
                    dve.wait_ge(mean_ready, i + 1)
                    for c in range(C):
                        ins = dve.scalar_tensor_tensor(
                            out=k.xn[:, c, b, ds(PAD + q * TT, TT)], in0=src[:, c, ds(b * L + q * TT, TT)], scalar=-0.5,
                            in1=stat[:, q % 2, :], op0=ALU.mult, op1=ALU.add)
                    ins.then_inc(centred, 1)

                def correct(q):
                    i = b * PB + q
                    j = q % 2
                    dve.wait_ge(root_ready, i + 1)
                    dve.scalar_tensor_tensor(out=ra[:, j, :], in0=var[:, j, :], scalar=EPS, in1=r2[:, j, :], op0=ALU.add,
                                             op1=ALU.mult).then_inc(newton, 1)
                    dve.wait_ge(newton, 4 + 2 * i + 1)
                    dve.wait_ge(normed, 1 + i)
                    dve.scalar_tensor_tensor(out=rstd[:, j, :], in0=ra[:, j, :], scalar=-3.0, in1=r0[:, j, :],
                                             op0=ALU.add, op1=ALU.mult).then_inc(newton, 1)

                staggered(centre, correct, before and (lambda q: before.add(dve, b * PB + q, q % 2)))


def scan_counts(it, g):
    return it * UNITS + g * NS


class ScanRing:

    def __init__(self, m):
        banks = m.ps("banks", [P, 8, TT])
        self.banks = banks
        self.decay = [banks[:, 2 * j:2 * j + 2, :] for j in range(2)]
        self.chat = banks[:, 4:6, :]
        self.y = banks[:, 6:8, :]
        self.drive = m.sb("drive", [P, 2, TC])
        self.h = m.sb("h", [P, 2, TC])
        self.prod = m.sb("prod", [P, 2, TC])
        self.decay_ready = m.sem("decay_ready")
        self.drive_ready = m.sem("drive_ready")
        self.scan_done = m.sem("scan_done")
        self.prod_ready = m.sem("prod_ready")
        self.chat_ready = m.sem("chat_ready")
        self.sum_done = m.sem("sum_done")


def flat(ap):
    return ap.rearrange("p a t -> p (a t)")


def dve_credits(dve, r):
    dve.sem_inc(r.scan_done, CREDIT)
    dve.sem_inc(r.prod_ready, CREDIT)


def split_rows(dve, step, i, rows, parts, mid, rest):
    dve.tensor_copy(parts[0:32, :], rows).then_inc(step, 1)
    dve.wait_ge(step, i * 5 + 1)
    dve.tensor_tensor(rest, rows, parts[0:32, :], ALU.subtract).then_inc(step, 1)
    dve.wait_ge(step, i * 5 + 2)
    dve.tensor_copy(mid, rest).then_inc(step, 1)
    dve.wait_ge(step, i * 5 + 3)
    dve.tensor_copy(parts[32:64, :], mid)
    dve.tensor_tensor(rest, rest, mid, ALU.subtract).then_inc(step, 1)
    dve.wait_ge(step, i * 5 + 4)
    dve.tensor_copy(parts[64:96, :], rest).then_inc(step, 1)


def mixer0(nc, k, acc):
    R = 64
    G = GROUPS
    a = k.a
    H2 = L // TC
    blocks = [(c, hf) for c in range(C) for hf in range(H2)]
    with ExitStack() as ctx:
        m = Mem(nc, ctx, "mix0")
        wz, wout = m.sb("wz", [P, C, E]), m.sb("wout", [P, C, E])
        wpar = m.sb("wpar", [P, C, P])
        wdt = m.sb("wdt", [R, E])
        taps, bdt, alog, dcol = m.sb("taps", [P, C, KC]), m.sb("bdt", [P, C]), m.sb("alog", [P, C, NS]), m.sb("dcol", [P, C])
        ea, neg_a, mask, keep = (m.sb(n, [P, C * NS]) for n in ("ea", "neg_a", "mask", "keep"))
        den, rec, reff, rsum = (m.sb(n, [P, C * NS]) for n in ("den", "rec", "reff", "rsum"))
        rsum_t = m.sb("rsum_t", [NS, C, P])
        diag_r = m.sb("diag_r", [P, 2, P])
        one = m.sb("one", [P, 1])
        u = m.sb("u", [P, C, L + 1])
        dt = m.sb("dt", [P, C, L + 1])
        du = m.sb("du", [P, C, L])
        dd = m.sb("dd", [P, C, L])
        rows, dtin = m.sb("rows", [32, L]), m.sb("dtin", [R, L])
        parts = m.sb("parts", [96, L], BF16)
        state = m.sb("state", [P, C * (NS + 1)])
        decay_sb = m.sb("decay", [P, 2, TC])
        r = ScanRing(m)
        banks = r.banks
        flatb = banks[:].rearrange("p a t -> p (a t)")
        y_banks = [banks[:, 2:4, :], banks[:, 6:8, :]]
        z_banks = flatb[:, 0:2 * TT]
        dt_bank = [4, 6]
        rs_bank = [0, 2]
        lin, ex, lg, off = ([r.drive[:, 0, :], r.prod[:, 0, :]], [r.drive[:, 1, :], r.prod[:, 1, :]],
                            [r.h[:, 0, :], decay_sb[:, 0, :]], [r.h[:, 1, :], decay_sb[:, 1, :]])
        mid, rest = dd[0:32, 0, 0:L // 2].bitcast(BF16), dd[0:32, 1, :]

        (loaded, cleared, ea_ready, setup, rs_turned, rs_kept, tap0, tap_done, u_ready, par_ready, par_kept, split,
         dt_ready, abs_done, exp_done, log_done, soft_step, log_sum, soft_done, u_first, du_ready, shaped, step_ready,
         rs_ready, mask_ready, saved, z_ready, gate_ready, y_step, gated, out_ready, added, sel_built) = (m.sem(n) for n in (
             "loaded cleared ea_ready setup rs_turned rs_kept tap0 tap_done u_ready par_ready par_kept split "
             "dt_ready abs_done exp_done log_done soft_step log_sum soft_done u_first du_ready shaped step_ready "
             "rs_ready mask_ready saved z_ready gate_ready y_step gated out_ready added sel_built").split())
        SETUP = 9
        LOADS = 9 * 16
        block = ctx.enter_context(nc.Block())

        def part(x, g, first=0):
            c, hf = blocks[g]
            return x[:, c, first + hf * TC:first + (hf + 1) * TC]

        @block.sync
        def _(sp):
            sp.wait_ge(cleared, 1)
            for dst, src in (
                (wz[:], a["W_z"].rearrange("(c p) m -> p c m", p=P)),
                (wout[:], a["W_out"].rearrange("(c p) m -> p c m", p=P)),
                (wpar[:, :, 0:NS], a["W_par"][:, R + NS:R + 2 * NS].rearrange("(c p) m -> p c m", p=P)),
                (wpar[:, :, 64:64 + R], a["W_par"][:, 0:R].rearrange("(c p) m -> p c m", p=P)),
                (wdt[:], a["W_dt"]),
                (taps[:], a["conv_w"].rearrange("(c p) k -> p c k", p=P)),
                (bdt[:], a["b_dt"]),
                (alog[:], a["A_log"].rearrange("(c p) n -> p c n", p=P)),
                (dcol[:], a["D"]),
            ):
                sp.dma_start(dst, src).then_inc(loaded, 16)

        @block.gpsimd
        def _(pool):
            selectors(pool, k, sel_built)
            with pool.Fori(0, B) as b:
                def log_add(g):
                    pool.wait_ge(log_done, b * G + (g + 1))
                    pool.wait_ge(soft_step, b * 2 * G + 2 * (g + 1))
                    pool.tensor_tensor(lg[g % 2], lg[g % 2], off[g % 2], ALU.add).then_inc(log_sum, 1)

                for c in range(C):
                    log_add(H2 * c)
                    log_add(H2 * c + 1)
                    pool.wait_ge(u_first, b * C + (c + 1))
                    pool.tensor_tensor(du[:, c, :], u[:, c, 1:L + 1], u[:, c, 0:L], ALU.subtract).then_inc(du_ready, 1)
                for g in range(G):
                    with pool.Fori(0, NS // 2) as n2:
                        for j in range(2):
                            un = scan_counts(b, g) + n2 * 2 + j
                            pool.wait_ge(mask_ready, un + 1)
                            pool.tensor_tensor(r.drive[:, j, :], r.drive[:, j, :], part(du, g),
                                               ALU.add).then_inc(r.drive_ready, 1)

        @block.scalar
        def _(act):
            act.preload_act_table_set("natural_log_exp_and_others")
            act.wait_ge(loaded, LOADS)
            act.activation(ea[:], alog[:].rearrange("p c n -> p (c n)"), ACT.Exp).then_inc(ea_ready, 1)
            act.wait_ge(rs_turned, 1)
            act.activation(rsum_t[:], banks[0:NS, 0, 0:C * P].rearrange("n (c p) -> n c p", c=C),
                           ACT.Copy).then_inc(rs_kept, 1)
            with act.Fori(0, B) as b:
                act.wait_ge(r.scan_done, CREDIT + b * UNITS)
                act.wait_ge(r.sum_done, CREDIT + b * UNITS)
                act.wait_ge(out_ready, 1 + b * G)
                for c in range(C):
                    act.activation(u[:, c, 1:L + 1], k.xn[:, c, b, 0:L], ACT.Copy, scale=taps[:, c, 0:1]).then_inc(tap0, 1)
                act.wait_ge(par_ready, b + 1)
                act.activation(dtin[:], flatb[64:128, 0:L], ACT.Copy).then_inc(par_kept, 1)
                act.activation(rows[:], flatb[0:32, 0:L], ACT.Copy).then_inc(par_kept, 1)
                for c in range(C):
                    act.wait_ge(tap_done, b * 6 + 3 * (c + 1))
                    act.activation(u[:, c, 1:L + 1], u[:, c, 1:L + 1], ACT.Silu).then_inc(u_ready, 1)
                act.preload_act_table_set("natural_log_exp_and_others")
                for g in range(G):
                    s = g % 2
                    x = flatb[:, dt_bank[s] * TT:dt_bank[s] * TT + TC]
                    c = blocks[g][0]
                    act.wait_ge(dt_ready, b * G + (g + 1))
                    if g > 1:
                        act.wait_ge(soft_done, b * G + (g - 1))
                    act.activation(lin[s], x, ACT.Identity, bias=bdt[:, c:c + 1])
                    act.activation(ex[s], x, ACT.Abs, bias=bdt[:, c:c + 1]).then_inc(abs_done, 1)
                    act.wait_ge(abs_done, b * G + (g + 1))
                    act.activation(ex[s], ex[s], ACT.Exp, scale=-1.0).then_inc(exp_done, 1)
                    act.wait_ge(exp_done, b * G + (g + 1))
                    act.activation(lg[s], ex[s], ACT.Ln, bias=one[:, 0:1]).then_inc(log_done, 1)
                act.wait_ge(step_ready, b + 1)

                def pair(g, n2):
                    c = blocks[g][0]
                    for j in range(2):
                        un = scan_counts(b, g) + n2 * 2 + j
                        at = n2 * 2 + (c * NS + j)
                        col = slice(at, at + 1) if isinstance(at, int) else ds(at, 1)
                        act.wait_ge(r.scan_done, CREDIT + un - 1)
                        act.activation(r.drive[:, j, :], part(dd, g), ACT.Copy, scale=mask[:, col]).then_inc(mask_ready, 1)
                        act.activation(decay_sb[:, j, :], part(dt, g), ACT.Exp, scale=neg_a[:, col]).then_inc(r.decay_ready, 1)
                        act.wait_ge(r.scan_done, CREDIT + un)
                        if isinstance(at, int) and n2 * 2 + j == 0:
                            continue
                        act.activation(state[:, at + c:at + c + 1] if isinstance(at, int) else state[:, ds(at + c, 1)],
                                       r.h[:, 1 - j, TC - 1:TC], ACT.Copy)

                def gate(g):
                    act.wait_ge(z_ready, b * G + (g + 1))
                    act.wait_ge(mask_ready, scan_counts(b, g) + NS)
                    act.activation(part(dd, g), z_banks, ACT.Silu).then_inc(gate_ready, 1)
                    act.preload_act_table_set("natural_log_exp_and_others")

                for g in range(G):
                    c = blocks[g][0]
                    if g:
                        act.wait_ge(saved, b * G + g)
                    pair(g, 0)
                    if g:
                        gate(g - 1)
                    with act.Fori(1, NS // 2) as n2:
                        pair(g, n2)
                    act.wait_ge(r.scan_done, CREDIT + scan_counts(b, g) + NS)
                    act.activation(state[:, c * (NS + 1) + NS:(c + 1) * (NS + 1)], r.h[:, 1, TC - 1:TC],
                                   ACT.Copy).then_inc(saved, 1)
                gate(G - 1)

        @block.vector
        def _(dve):
            dve.memset(wpar[:], 0.0).then_inc(cleared, 1)
            dve.memset(one[:], 1.0)
            dve.sem_inc(added, 3)
            dve_credits(dve, r)
            dve.wait_ge(loaded, LOADS)
            dve.wait_ge(ea_ready, 1)
            dve.tensor_scalar(neg_a[:], ea[:], -1.0, None, ALU.mult).then_inc(setup, 1)
            dve.tensor_scalar(mask[:], ea[:], 1e-5, None, ALU.is_lt).then_inc(setup, 1)
            dve.wait_ge(setup, 2)
            dve.tensor_scalar(keep[:], mask[:], -1.0, 1.0, ALU.mult, ALU.add).then_inc(setup, 1)
            dve.tensor_scalar(den[:], neg_a[:], 1e-10, None, ALU.add).then_inc(setup, 1)
            dve.wait_ge(setup, 4)
            dve.tensor_tensor(den[:], den[:], mask[:], ALU.subtract).then_inc(setup, 1)
            dve.wait_ge(setup, 5)
            dve.reciprocal(rec[:], den[:]).then_inc(setup, 1)
            dve.wait_ge(setup, 6)
            dve.tensor_tensor(rsum[:], rec[:], keep[:], ALU.mult).then_inc(setup, 1)
            dve.wait_ge(setup, 7)
            dve.tensor_tensor(reff[:], rsum[:], mask[:], ALU.add).then_inc(setup, 1)
            dve.memset(state[:], 0.0).then_inc(setup, 1)
            dve.wait_ge(setup, SETUP)
            with dve.Fori(0, B) as b:
                for c in range(C):
                    uc = u[:, c, 1:L + 1]
                    for t in range(1, KC):
                        if t == 1:
                            dve.wait_ge(tap0, b * C + (c + 1))
                        else:
                            dve.wait_ge(tap_done, b * 6 + (3 * c + t - 1))
                        dve.scalar_tensor_tensor(out=uc, in0=k.xn[:, c, b, t:t + L], scalar=taps[:, c, t:t + 1],
                                                 in1=uc, op0=ALU.mult, op1=ALU.add).then_inc(tap_done, 1)
                dve.wait_ge(par_kept, b * 2 + 2)
                split_rows(dve, split, b, rows[:], parts, mid, rest)
                for c in range(C):
                    dve.wait_ge(u_ready, b * C + (c + 1))
                    dve.tensor_copy(u[:, c, 0:1], u[:, c, 1:2]).then_inc(u_first, 1)
                for c in range(C):
                    dve.wait_ge(u_first, b * C + (c + 1))
                    dve.tensor_scalar(state[:, 1 + c * (NS + 1):(c + 1) * (NS + 1)], keep[:, c * NS:(c + 1) * NS],
                                      u[:, c, 0:1], None, ALU.mult)
                dve.wait_ge(split, b * 5 + 5)

                def rounded_off(g):
                    s = g % 2
                    dve.wait_ge(exp_done, b * G + (g + 1))
                    if g > 1:
                        dve.wait_ge(log_sum, b * G + (g - 1))
                    dve.tensor_scalar(off[s], ex[s], 1.0, -1.0, ALU.add, ALU.add).then_inc(soft_step, 1)
                    dve.wait_ge(soft_step, b * 2 * G + (2 * g + 1))
                    dve.scalar_tensor_tensor(out=off[s], in0=off[s], scalar=-1.0, in1=ex[s], op0=ALU.mult,
                                             op1=ALU.add).then_inc(soft_step, 1)

                def step_size(g):
                    dve.wait_ge(log_sum, b * G + (g + 1))
                    dve.scalar_tensor_tensor(out=part(dt, g, 1), in0=lin[g % 2], scalar=0.0, in1=lg[g % 2], op0=ALU.max,
                                             op1=ALU.add).then_inc(soft_done, 1)

                def shape(c):
                    dve.wait_ge(soft_done, b * G + 2 * (c + 1))
                    dve.tensor_copy(dt[:, c, 0:1], dt[:, c, 1:2]).then_inc(shaped, 1)
                    dve.wait_ge(shaped, b * 2 * C + (2 * c + 1))
                    dve.tensor_tensor(dd[:, c, :], u[:, c, 0:L], dt[:, c, 0:L], ALU.mult).then_inc(shaped, 1)
                    dve.wait_ge(shaped, b * 2 * C + (2 * c + 2))
                    dve.wait_ge(du_ready, b * C + (c + 1))
                    dve.tensor_tensor(dd[:, c, :], dd[:, c, :], du[:, c, :], ALU.subtract)
                    for hf in range(H2):
                        g = c * H2 + hf
                        dve.wait_ge(rs_ready, b * G + (g + 1))
                        rs = flatb[:, rs_bank[g % 2] * TT:rs_bank[g % 2] * TT + TC]
                        ins = dve.scalar_tensor_tensor(out=part(u, g, 1), in0=rs, scalar=dcol[:, c:c + 1],
                                                       in1=part(u, g, 1), op0=ALU.subtract, op1=ALU.mult)
                    return ins

                for c in range(C):
                    rounded_off(H2 * c)
                    rounded_off(H2 * c + 1)
                    step_size(H2 * c)
                    step_size(H2 * c + 1)
                    ins = shape(c)
                ins.then_inc(step_ready, 1)
                dve.wait_ge(step_ready, b + 1)

                def pair(g, n2):
                    c = blocks[g][0]
                    for j in range(2):
                        un = scan_counts(b, g) + n2 * 2 + j
                        at = n2 * 2 + (c * NS + j)
                        fixed = isinstance(at, int)
                        dve.wait_ge(r.decay_ready, un + 1)
                        dve.wait_ge(r.drive_ready, un + 1)
                        dve.wait_ge(r.prod_ready, CREDIT + un - 1)
                        dve.tensor_tensor_scan(r.h[:, j, :], decay_sb[:, j, :], r.drive[:, j, :],
                                               state[:, at + c + 1:at + c + 2] if fixed else state[:, ds(at + c + 1, 1)],
                                               ALU.mult, ALU.add).then_inc(r.scan_done, 1)
                        dve.wait_ge(r.sum_done, CREDIT + un - 1)
                        dve.tensor_scalar(diag_r[:, j, :], k.ident[:], reff[:, at:at + 1] if fixed else reff[:, ds(at, 1)],
                                          None, ALU.mult)
                        dve.wait_ge(r.scan_done, CREDIT + un + 1)
                        dve.wait_ge(r.chat_ready, un + 1)
                        dve.tensor_tensor(r.prod[:, j, :], flat(r.chat), r.h[:, j, :],
                                          ALU.mult).then_inc(r.prod_ready, 1)

                def gate_y(g):
                    yg = part(u, g, 1)
                    dve.wait_ge(r.sum_done, CREDIT + scan_counts(b, g) + NS)
                    dve.tensor_tensor(yg, flat(y_banks[g % 2]), yg, ALU.subtract).then_inc(y_step, 1)
                    dve.wait_ge(y_step, b * G + (g + 1))
                    dve.wait_ge(gate_ready, b * G + (g + 1))
                    dve.tensor_tensor(yg, yg, part(dd, g), ALU.mult).then_inc(gated, 1)

                for g in range(G):
                    pair(g, 0)
                    if g:
                        gate_y(g - 1)
                    with dve.Fori(1, NS // 2) as n2:
                        pair(g, n2)
                gate_y(G - 1)
                for n in range(G):
                    hf, c = n // C, n % C
                    dve.wait_ge(out_ready, 1 + b * G + (n + 1))
                    ac = acc[:, c, ds(b * L + hf * TC, TC)]
                    dve.tensor_tensor(ac, flat(banks[:, 2 * n:2 * n + 2, :]), ac, ALU.add).then_inc(added, 1)

        @block.tensor
        def _(pe):
            pe.sem_inc(r.sum_done, CREDIT)
            pe.sem_inc(out_ready, 1)
            pe.wait_ge(loaded, LOADS)
            pe.wait_ge(setup, SETUP)
            for c in range(C):
                mm = pe.transpose(banks[0:NS, 0, c * P:(c + 1) * P], rsum[:, c * NS:(c + 1) * NS], k.ident[:])
            mm.then_inc(rs_turned, 1)
            pe.wait_ge(rs_kept, 1)
            with pe.Fori(0, B) as b:
                pe.wait_ge(added, 3 + b * G - 2)
                for q in range(4):
                    for c in range(C):
                        mm = pe.matmul(banks[:, q, :], wpar[:, c, :], k.xn[:, c, b, PAD + q * TT:PAD + (q + 1) * TT],
                                       start=c == 0, stop=c == C - 1)
                mm.then_inc(par_ready, 1)
                pe.wait_ge(par_kept, b * 2 + 2)
                pe.wait_ge(added, 3 + b * G)
                for g in range(G):
                    c, hf = blocks[g]
                    if g > 1:
                        pe.wait_ge(abs_done, b * G + (g - 1))
                    for q in range(2):
                        mm = pe.matmul(banks[:, dt_bank[g % 2] + q, :], wdt[:, c * P:(c + 1) * P],
                                       dtin[:, hf * TC + q * TT:hf * TC + (q + 1) * TT], start=True, stop=True)
                    mm.then_inc(dt_ready, 1)

                def row_sums(g):
                    c, hf = blocks[g]
                    for q in range(2):
                        o = hf * TC + q * TT
                        mm = pe.matmul(banks[:, rs_bank[g % 2] + q, :], rsum_t[:, c, :], rows[0:NS, o:o + TT],
                                       start=True, stop=True)
                    mm.then_inc(rs_ready, 1)

                row_sums(0)
                row_sums(1)
                pe.wait_ge(soft_step, b * 2 * G + 2 * H2 + 1)
                row_sums(2)
                row_sums(3)
                pe.wait_ge(sel_built, 4)
                pe.wait_ge(split, b * 5 + 5)
                pe.wait_ge(abs_done, b * G + G)
                pe.wait_ge(step_ready, b + 1)

                def spread_c(un, n, hf):
                    for q in range(2):
                        o = hf * TC + q * TT
                        mm = pe.matmul(r.chat[:, q, :], k.sel[:, n, :] if isinstance(n, int) else k.sel[:, ds(n, 1), :],
                                       parts[:, o:o + TT], start=True, stop=True)
                    mm.then_inc(r.chat_ready, 1)

                def add(g, j, first=False):
                    for q in range(2):
                        mm = pe.matmul(y_banks[g % 2][:, q, :], diag_r[:, j, :], r.prod[:, j, q * TT:(q + 1) * TT],
                                       start=first, stop=True, skip_group_check=True)
                    mm.then_inc(r.sum_done, 1)

                SLICE = 2 * TC // NS

                def z_slice(g, s):
                    c, hf = blocks[g]
                    for kk in range(C):
                        mm = pe.matmul(z_banks[:, s * SLICE:(s + 1) * SLICE] if isinstance(s, int)
                                       else z_banks[:, ds(s * SLICE, SLICE)], wz[:, kk, c * P:(c + 1) * P],
                                       k.xn[:, kk, b, ds(s * SLICE + (hf * TC + PAD), SLICE)],
                                       start=kk == 0, stop=kk == C - 1)
                    return mm

                for g in range(G):
                    hf = blocks[g][1]
                    base = scan_counts(b, g)
                    if g == 0:
                        spread_c(base, 0, hf)
                    if g > 1:
                        pe.wait_ge(gated, b * G + (g - 1))
                    for j in range(2):
                        pe.wait_ge(r.prod_ready, CREDIT + base + j + 1)
                        spread_c(base + j + 1, j + 1, hf)
                        add(g, j, first=j == 0)
                    with pe.Fori(1, NS // 2 - 1) as n2:
                        for j in range(2):
                            un = base + n2 * 2 + j
                            pe.wait_ge(r.prod_ready, CREDIT + un + 1)
                            spread_c(un + 1, n2 * 2 + (j + 1), hf)
                            add(g, j)
                        if g:
                            pe.wait_ge(gate_ready, b * G + g)
                        z_slice(g, n2 + -1)
                    pe.wait_ge(r.prod_ready, CREDIT + base + NS - 1)
                    spread_c(base + NS - 1, NS - 1, hf)
                    add(g, 0)
                    z_slice(g, NS // 2 - 2)
                    z_slice(g, NS // 2 - 1).then_inc(z_ready, 1)
                    pe.wait_ge(r.prod_ready, CREDIT + base + NS)
                    if g + 1 < G:
                        spread_c(base + NS, 0, blocks[g + 1][1])
                    add(g, 1)
                pe.wait_ge(gate_ready, b * G + G)
                pe.wait_ge(gated, b * G + 3)
                for n in range(G):
                    hf, c = n // C, n % C
                    if n == 2:
                        pe.wait_ge(gated, b * G + G)
                    for q in range(2):
                        o = 1 + hf * TC + q * TT
                        for kk in range(C):
                            mm = pe.matmul(banks[:, 2 * n + q, :], wout[:, kk, c * P:(c + 1) * P], u[:, kk, o:o + TT],
                                           start=kk == 0, stop=kk == C - 1)
                    mm.then_inc(out_ready, 1)


def experts0(nc, k, acc):
    GS, SL, F = 16, 64, 64
    NG = L // GS
    QG = TT // GS
    NQ = L // TT
    EG = 8
    NE = SL // EG
    a = k.a
    z = nc.dram_tensor("slot_outputs", (B, NG, SL, E), F32, kind="Internal").ap()
    with ExitStack() as keep:
        perm_t = Mem(nc, keep, "exp").sb("perm_t", [P, T])
        with ExitStack() as ctx:
            m = Mem(nc, ctx, "exa")
            ctrl, bias = m.sb("ctrl", [P, C, P]), m.sb("bias", [F, SL])
            tie, parity = m.sb("tie", [P, QG, GS]), m.sb("parity", [P, QG, GS])
            pair_of = m.sb("pair_of", [P, 4])
            lt, pq = m.sb("lt", [P, TT]), m.sb("pq", [P, TT])
            top = m.sb("top", [P, QG])
            work = m.sb("work", [P, 2, EG * P])
            xs = work[:, 0, :].rearrange("p (c t) -> p c t", c=C)
            xtok = work[:, 1, :].rearrange("p (t e) -> p t e", t=4)
            inner = work[0:F, :, :].rearrange("p j (s g) -> p j s g", s=EG)
            pex = m.sb("pex", [P, 2, 4, P])
            sel_t = m.sb("sel_t", [P, C, SL, NG])
            f1 = m.sb("f1", [P, 2, C, EG, F])
            f2 = m.sb("f2", [F, 2, EG, E])
            inter = m.sb("inter", [P, 2, 4, E])
            banks = m.ps("banks", [P, 8, TT])
            loaded, built = m.sem("loaded"), m.sem("built")
            lg_ready, pstep, perm_ready = m.sem("lg_ready"), m.sem("pstep"), m.sem("perm_ready")
            xs_ready, turned, xtok_ready, pex_ready = m.sem("xs_ready"), m.sem("turned"), m.sem("xtok_ready"), m.sem("pex_ready")
            sel_ready, sel_kept = m.sem("sel_ready"), m.sem("sel_kept")
            w_loaded = [m.sem(f"w_loaded{j}") for j in range(2)]
            stored = [m.sem(f"stored{j}") for j in range(2)]
            slot_free = [m.sem(f"slot_free{j}") for j in range(2)]
            biased = m.sem("biased")
            in_ready, inner_ready = m.sem("in_ready"), m.sem("inner_ready")
            fill_ready, act_kept, dve_kept = m.sem("fill_ready"), m.sem("act_kept"), m.sem("dve_kept")
            block = ctx.enter_context(nc.Block())

            @block.sync
            def _(sp):
                ctl = a["controller"].rearrange("(c p) m -> p c m", p=P)
                for dst, src in ((ctrl[:, :, 0:SL], ctl), (ctrl[:, :, SL:P], ctl), (bias[:], a["bias"]),
                                 (tie[:], a["tie"])):
                    sp.dma_start(dst, src).then_inc(loaded, 16)
                with sp.Fori(0, B) as b, sp.Fori(0, NE // 2) as e2:
                    for j in range(2):
                        e = b * NE + e2 * 2 + j
                        sp.wait_ge(fill_ready, 8 + e * 4 - 4)
                        sp.dma_start(f1[:, j], a["f1"].rearrange("(c p) (e s) f -> p c e s f", p=P, s=EG)[
                            :, :, ds(e2 * 2 + j, 1)].rearrange("p c e s f -> p c (e s f)")).then_inc(w_loaded[j], 16)
                        sp.dma_start(f2[:, j], a["f2"].rearrange("(e s) f d -> f e s d", e=NE)[
                            :, ds(e2 * 2 + j, 1)].rearrange("p e s d -> p (e s) d")).then_inc(w_loaded[j], 16)

            @block.gpsimd
            def _(pool):
                for j in range(2):
                    pool.sem_inc(slot_free[j], 1)
                with pool.Fori(0, B) as b, pool.Fori(0, NE) as e:
                    i = b * NE + e
                    for j in range(2):
                        pool.wait_ge(act_kept, 1 + i * 2 + (j + 1))
                        pool.wait_ge(dve_kept, 1 + i * 2 + (j + 1))
                        pool.dma_start(z[ds(b, 1), :, ds(e * EG + j * 4, 4), :].rearrange("b g s d -> (b g) (s d)"),
                                       inter[:, j].rearrange("p s d -> p (s d)")).then_inc(stored[j], 16)
                    for j in range(2):
                        pool.wait_ge(stored[j], i * 16 + 16)
                        pool.sem_inc(slot_free[j], 1)

            @block.scalar
            def _(act):
                act.wait_ge(loaded, 16 * 4)
                act.sem_inc(act_kept, 1)
                with act.Fori(0, B) as b:
                    with act.Fori(0, NQ) as q:
                        i = b * NQ + q
                        act.wait_ge(sel_ready, 1 + i * 8)
                        act.activation(xs, k.xn[:, :, b, ds(PAD + q * TT, TT)], ACT.Copy).then_inc(xs_ready, 1)
                        act.wait_ge(perm_ready, 1 + (i + 1))
                        act.activation(perm_t[:, ds(b * L + q * TT, TT)], pq[:], ACT.Copy)
                        act.wait_ge(turned, i + 1)
                        act.activation(work[:, 1, :],
                                       banks[:, 1:3, :].rearrange("p a t -> p (a t)"), ACT.Copy).then_inc(xtok_ready, 1)
                        for t in range(4):
                            for c in range(C):
                                n = i * 8 + (t * C + c)
                                act.wait_ge(sel_ready, 1 + (n + 1))
                                act.activation(
                                    sel_t[:, c, :, ds(q * QG + t * 8, 8)].rearrange("p s g -> p g s"),
                                    banks[:, 4 + c, :].rearrange("p (g s) -> p g s", s=SL),
                                    ACT.Copy).then_inc(sel_kept, 1)
                    with act.Fori(0, NE // 2) as e2:
                        for j in range(2):
                            e = b * NE + e2 * 2 + j
                            for h in range(2):
                                act.wait_ge(fill_ready, 8 + e * 4 + (2 * h + 1))
                                act.wait_ge(slot_free[h], e + 1)
                                act.activation(inter[:, h, 0:2, :].rearrange("p s d -> p (s d)"), banks[:, 7, :],
                                               ACT.Copy).then_inc(act_kept, 1)

            @block.vector
            def _(dve):
                dve.memset(parity[0:64, 0:QG:2], 1.0)
                dve.memset(parity[0:64, 1:QG:2], 0.0)
                dve.memset(parity[64:128, 0:QG:2], 0.0)
                dve.memset(parity[64:128, 1:QG:2], 1.0).then_inc(built, 1)
                for i in range(4):
                    for v in range(4):
                        ins = dve.memset(pair_of[32 * v:32 * v + 32, i:i + 1], 1.0 if i == v else 0.0)
                ins.then_inc(built, 1)
                dve.memset(lt[:], 0.0).then_inc(perm_ready, 1)
                dve.memset(pex[:], 0.0).then_inc(dve_kept, 1)
                dve.wait_ge(perm_ready, 1)
                dve.wait_ge(dve_kept, 1)
                dve.wait_ge(loaded, 16 * 4)
                dve.wait_ge(built, 2)
                with dve.Fori(0, B) as b:
                    with dve.Fori(0, NQ) as q:
                        i = b * NQ + q
                        lg = banks[:, 0, :].rearrange("p (g t) -> p g t", t=GS)
                        ltg = lt[:].rearrange("p (g t) -> p g t", t=GS)
                        dve.wait_ge(lg_ready, i + 1)
                        dve.tensor_tensor(ltg, lg, tie[:], ALU.add).then_inc(pstep, 1)
                        dve.wait_ge(pstep, i * 3 + 1)
                        dve.tensor_reduce(top[:], ltg, AX.X, ALU.max).then_inc(pstep, 1)
                        dve.wait_ge(pstep, i * 3 + 2)
                        dve.tensor_tensor(ltg, ltg, top[:].unsqueeze(2).broadcast_to([P, QG, GS]),
                                          ALU.is_equal).then_inc(pstep, 1)
                        dve.wait_ge(pstep, i * 3 + 3)
                        dve.tensor_tensor(pq[:].rearrange("p (g t) -> p g t", t=GS), ltg, parity[:],
                                          ALU.mult).then_inc(perm_ready, 1)
                        dve.wait_ge(turned, i + 1)
                        for t in range(4):
                            dve.wait_ge(sel_ready, 1 + i * 8 + 2 * (t - 1) if t > 1 else 1 + i * 8)
                            dve.tensor_tensor(pex[:, t % 2], banks[:, 3, t * P:(t + 1) * P].unsqueeze(1)
                                              .broadcast_to([P, 4, P]),
                                              pair_of[:].unsqueeze(2).broadcast_to([P, 4, P]),
                                              ALU.mult).then_inc(pex_ready, 1)
                    with dve.Fori(0, NE // 2) as e2:
                        for j in range(2):
                            ex = b * NE + e2 * 2 + j
                            dve.wait_ge(in_ready, ex + 1)
                            dve.wait_ge(fill_ready, 8 + ex * 4 - 4)
                            dve.tensor_tensor(inner[:, j], banks[0:F, 5:7, :].rearrange("p a (s g) -> p (a s) g", g=P),
                                              bias[:, ds((e2 * 2 + j) * EG, EG)].unsqueeze(2).broadcast_to([F, EG, P]),
                                              ALU.add).then_inc(biased, 1)
                            dve.wait_ge(biased, ex + 1)
                            dve.tensor_scalar(inner[:, j], inner[:, j], 0.0, None, ALU.max).then_inc(inner_ready, 1)
                            for h in range(2):
                                dve.wait_ge(fill_ready, 8 + ex * 4 + (2 * h + 2))
                                dve.wait_ge(slot_free[h], ex + 1)
                                dve.tensor_copy(inter[:, h, 2:4, :].rearrange("p s d -> p (s d)"),
                                                banks[:, 0, :]).then_inc(dve_kept, 1)

            @block.tensor
            def _(pe):
                pe.sem_inc(fill_ready, 8)
                pe.sem_inc(sel_ready, 1)
                pe.wait_ge(loaded, 16 * 4)
                with pe.Fori(0, B) as b:
                    with pe.Fori(0, NQ) as q:
                        i = b * NQ + q
                        pe.wait_ge(perm_ready, 1 + i)
                        pe.wait_ge(dve_kept, 1 + b * 2 * NE)
                        for c in range(C):
                            mm = pe.matmul(banks[:, 0, :], ctrl[:, c, :], k.xn[:, c, b, ds(PAD + q * TT, TT)],
                                           start=c == 0, stop=c == C - 1)
                        mm.then_inc(lg_ready, 1)
                        pe.wait_ge(xs_ready, i + 1)
                        for t in range(4):
                            for c in range(C):
                                o = (t * C + c) * P
                                pe.transpose(banks[:, 1 + o // TT, o % TT:o % TT + P], xs[:, c, t * P:(t + 1) * P],
                                             k.ident[:])
                        pe.wait_ge(perm_ready, 1 + (i + 1))
                        for t in range(4):
                            mm = pe.transpose(banks[:, 3, t * P:(t + 1) * P], pq[:, t * P:(t + 1) * P], k.ident[:])
                        mm.then_inc(turned, 1)
                        pe.wait_ge(xtok_ready, i + 1)
                        for t in range(4):
                            pe.wait_ge(pex_ready, i * 4 + (t + 1))
                            for c in range(C):
                                n = i * 8 + (t * C + c)
                                if t:
                                    pe.wait_ge(sel_kept, n - 1)
                                mm = pe.matmul(banks[:, 4 + c, :], xtok[:, t, c * P:(c + 1) * P],
                                               pex[:, t % 2].rearrange("p a n -> p (a n)"), start=True, stop=True)
                                mm.then_inc(sel_ready, 1)
                    with pe.Fori(0, NE // 2) as e2:
                        for j in range(2):
                            e = b * NE + e2 * 2 + j
                            pe.wait_ge(w_loaded[j], (b * (NE // 2) + e2 + 1) * 32)
                            pe.wait_ge(sel_kept, (b + 1) * NQ * 8)
                            for s in range(EG):
                                for c in range(C):
                                    mm = pe.matmul(banks[0:F, 5 + s // 4, s % 4 * P:(s % 4 + 1) * P],
                                                   f1[:, j, c, s, :],
                                                   sel_t[:, c, ds((e2 * 2 + j) * EG + s, 1), :],
                                                   start=c == 0, stop=c == C - 1)
                            mm.then_inc(in_ready, 1)
                            pe.wait_ge(inner_ready, e + 1)
                            for f in range(4):
                                kept = act_kept if f % 2 == 0 else dve_kept
                                bank = 7 if f % 2 == 0 else 0
                                pe.wait_ge(kept, 1 + e * 2 + f // 2)
                                for h in range(2):
                                    mm = pe.matmul(banks[:, bank, h * E:(h + 1) * E], inner[:, j, 2 * f + h, :],
                                                   f2[:, j, 2 * f + h, :], start=True, stop=True)
                                mm.then_inc(fill_ready, 1)

        layernorm(nc, k, acc, save=k.x1, before=Combine(acc, perm_t, z))


class Combine:

    def __init__(self, acc, perm_t, z):
        self.acc, self.perm_t, self.z = acc, perm_t, z

    def place(self, m):
        self.zp = m.sb("zp", [P, 2, TT // 32, E])
        self.out = m.ps("out", [P, 2, C, TT])
        self.z_loaded = [m.sem(f"z_loaded{j}") for j in range(2)]
        self.out_ready = m.sem("out_ready")
        self.added = m.sem("added")

    def load(self, sp, i, i2, j):
        zr = self.z.rearrange("b (q r h) s d -> (h s) (b q) r d", h=2, r=TT // 32)
        sp.wait_ge(self.out_ready, i + 1)
        sp.dma_start(self.zp[:, j], zr[:, ds(i, 1)].rearrange("p q r d -> p (q r) d")).then_inc(self.z_loaded[j], 16)

    def products(self, pe, i, i2, j):
        pe.wait_ge(self.z_loaded[j], i2 * 16 + 16)
        pe.wait_ge(self.added, i + 1)
        for t in range(TT // 32):
            for c in range(C):
                mm = pe.matmul(self.out[:, j, c, t * 32:(t + 1) * 32], self.zp[:, j, t, c * P:(c + 1) * P],
                               self.perm_t[:, ds(i * TT + t * 32, 32)], start=True, stop=True)
        mm.then_inc(self.out_ready, 1)

    def add(self, dve, i, j):
        dve.wait_ge(self.out_ready, 2 + (i + 1))
        ac = self.acc[:, :, ds(i * TT, TT)]
        dve.tensor_tensor(ac, self.out[:, j], ac, ALU.add).then_inc(self.added, 1)


class Mixer1Weights:

    D2, R, MB = 512, 16, 4
    LOADS = 10 * 16

    def __init__(self, m):
        self.win, self.wout = m.sb("win", [P, C, 2 * self.D2]), m.sb("wout", [P, self.MB, E])
        self.wx, self.wdt = m.sb("wx", [P, self.MB, 64 + self.R]), m.sb("wdt", [self.R, self.D2])
        self.taps, self.small = m.sb("taps", [P, self.MB, KC]), m.sb("small", [P, 3, self.MB])
        self.alog = m.sb("alog", [P, self.MB * NS])

    def load(self, sp, a, way, loaded):
        R = self.R
        wxa = a[way + "_Wx"].rearrange("(c p) m -> p c m", p=P)
        for dst, src in ((self.win[:], a[way + "_Win"].rearrange("(c p) m -> p c m", p=P)),
                         (self.taps[:], a[way + "_convw"].rearrange("(c p) k -> p c k", p=P)),
                         (self.small[:, 0, :], a[way + "_convb"]), (self.small[:, 1, :], a[way + "_bdt"]),
                         (self.small[:, 2, :], a[way + "_D"]),
                         (self.wx[:, :, 0:2 * NS], wxa[:, :, R:R + 2 * NS]),
                         (self.wx[:, :, 64:64 + R], wxa[:, :, 0:R]),
                         (self.wdt[:], a[way + "_Wdt"]),
                         (self.alog[:].rearrange("p (c n) -> p c n", n=NS),
                          a[way + "_Alog"].rearrange("(c p) n -> p c n", p=P)),
                         (self.wout[:], a[way + "_Wout"].rearrange("(c p) m -> p c m", p=P))):
            sp.dma_start(dst, src).then_inc(loaded, 16)


def mixer1(nc, k, w, way, y_in, y_out_dram):
    D2, R, MB = w.D2, w.R, w.MB
    a = k.a
    bw = way == "bw"
    NC = L // TC
    NP = B * NC
    assert NC == 2
    with ExitStack() as ctx:
        m = Mem(nc, ctx, way)
        win, wout, wx, wdt, taps, alog = w.win, w.wout, w.wx, w.wdt, w.taps, w.alog
        convb, bdt, dcol = w.small[:, 0, :], w.small[:, 1, :], w.small[:, 2, :]
        norm, norm_s = m.sb("norm", [P, 2, C]), m.sb("norm_s", [P, 2, C])
        neg_a = m.sb("neg_a", [P, MB * NS])
        diag_d = m.sb("diag_d", [P, MB, P])
        consts = m.sb("consts", [P, 4])
        one, eps, carry = consts[:, 0:1], consts[:, 1:2], consts[:, 2:4]
        u, dt, dtu = m.sb("u", [P, MB, TC]), m.sb("dt", [P, MB, TC]), m.sb("dtu", [P, MB, TC])
        parts = m.sb("parts", [96, TC], BF16)
        brep = m.sb("brep", [P, NS, TC])
        state = m.sb("state", [P, MB * (NS + 1)])
        decay_sb = m.sb("decay", [P, 2, TC])
        r = ScanRing(m)
        banks = r.banks
        flatb = banks[:].rearrange("p a t -> p (a t)")
        y_banks = [banks[:, 2:4, :], banks[:, 6:8, :]]
        z_banks = flatb[:, 0:2 * TT]
        stat = flatb[:, 0:2 * TT]
        x_bank = [5, 2]
        par_bank = 6
        dt_bank = [2, 0]
        b_bank = [4 + n % 2 * 2 for n in range(10)] + [2, 0, 4, 6, 2, 0]
        x_slot = [flat(r.prod)[:, 0:PAD + TC], flat(decay_sb)[:, 0:PAD + TC]]
        lin, ex, lg, off = ([r.drive[:, 0, :], r.prod[:, 0, :]], [r.drive[:, 1, :], r.prod[:, 1, :]],
                            [r.h[:, 0, :], decay_sb[:, 0, :]], [r.h[:, 1, :], decay_sb[:, 1, :]])
        mid, rest, dtin = dtu[0:32, 1, 0:TC // 2].bitcast(BF16), dtu[0:32, 2, :], dtu[0:R, 3, :]
        res, sq, logv, r0, r2, ra, rstd, yf = (brep[:, 14:16], brep[:, 12:14], brep[:, 11], brep[:, 10], brep[:, 9],
                                               brep[:, 8], brep[:, 7], brep[:, 5:7])
        (loaded, cleared, ea_ready, setup, xi_ready, xi_kept, tap0, tap_done, u_ready, par_ready, dtin_kept, split,
         dt_ready, abs_done, exp_done, log_done, soft_step, log_sum, soft_done, dtu_ready, b_spread, b_act, b_dve,
         b_free, started, saved, z_ready, gate_ready, gated, out_ready, summed, mean_ready, centred, squared,
         var_ready, logged, root, root_ready, newton, scaled, y_out, stored, yf_loaded, next_loaded) = (m.sem(n) for n in (
             "loaded cleared ea_ready setup xi_ready xi_kept tap0 tap_done u_ready par_ready dtin_kept split "
             "dt_ready abs_done exp_done log_done soft_step log_sum soft_done dtu_ready b_spread b_act b_dve "
             "b_free started saved z_ready gate_ready gated out_ready summed mean_ready centred squared "
             "var_ready logged root root_ready newton scaled y_out stored yf_loaded next_loaded").split())
        LOADS = 16 + (0 if bw else w.LOADS)
        block = ctx.enter_context(nc.Block())

        def passes(eng):
            both = ExitStack()
            b = both.enter_context(eng.Fori(0, B))
            tc = both.enter_context(eng.Fori(0, NC))
            return both, b, b * NC + tc, tc, ((tc * -TC) + (L - TC)) if bw else tc * TC

        def before(b, tc):
            return b * L + tc * (L + TC) if bw else b * L + tc * TC + TC

        @block.sync
        def _(sp):
            sp.dma_start(norm[:], a["fwn"]).then_inc(loaded, 16)
            if not bw:
                sp.wait_ge(cleared, 1)
                w.load(sp, a, "fw", loaded)
            to = y_out_dram.rearrange("(c p) t -> p c t", p=P)
            if bw:
                sp.dma_start(yf, k.x1.rearrange("(c p) t -> p c t", p=P)[:, :, 0:TC]).then_inc(yf_loaded, 16)
            both, b, it, tc, t0 = passes(sp)
            with both:
                sp.wait_ge(y_out, it + 1)
                sp.dma_start(to[:, :, ds(before(b, tc), TC)], res).then_inc(stored, 16)
                sp.wait_ge(stored, it * 16 + 16)
                sp.sem_inc(b_free, 1)
                if bw:
                    sp.wait_ge(gated, it * MB + MB)
                    sp.dma_start(yf, y_in.rearrange("(c p) t -> p c t", p=P)[:, :, ds(b * L + (t0 + L), TC)]
                                 ).then_inc(yf_loaded, 16)
            if not bw:
                sp.wait_ge(out_ready, NP)
                w.load(sp, a, "bw", next_loaded)
                sp.wait_ge(next_loaded, w.LOADS)
            sp.wait_ge(y_out, NP + 1)
            sp.dma_start(to[:, :, before(B, 0):before(B, 0) + TC], res).then_inc(stored, 16)
            sp.wait_ge(stored, NP * 16 + 16)

        @block.gpsimd
        def _(pool):
            both, b, it, tc, t0 = passes(pool)
            with both:
                pool.wait_ge(split, it * 5 + 5)

                def log_add(g):
                    pool.wait_ge(log_done, it * MB + (g + 1))
                    pool.wait_ge(soft_step, it * 2 * MB + 2 * (g + 1))
                    pool.tensor_tensor(lg[g % 2], lg[g % 2], off[g % 2], ALU.add).then_inc(log_sum, 1)

                def times_u(g):
                    pool.wait_ge(soft_done, it * MB + (g + 1))
                    pool.wait_ge(u_ready, it * MB + (g + 1))
                    pool.tensor_tensor(dtu[:, g, :], dt[:, g, :], u[:, g, :], ALU.mult).then_inc(dtu_ready, 1)

                log_add(0)
                for g in range(1, MB):
                    log_add(g)
                    times_u(g - 1)
                times_u(MB - 1)
                for g in range(MB):
                    with pool.Fori(0, NS // 2) as n2:
                        for j in range(2):
                            un = scan_counts(it, g) + n2 * 2 + j
                            if g == 0:
                                pool.wait_ge(b_act, it * 8 + n2 + 1)
                                pool.wait_ge(b_dve, it * 8 + n2 + 1)
                                pool.wait_ge(dtu_ready, it * MB + MB)
                            pool.wait_ge(r.scan_done, CREDIT + un - 1)
                            pool.tensor_tensor(r.drive[:, j, :], brep[:, ds(n2 * 2 + j, 1), :].rearrange("p n t -> p (n t)"),
                                               dtu[:, g, :], ALU.mult).then_inc(r.drive_ready, 1)

        @block.scalar
        def _(act):
            def post_square(i):
                act.wait_ge(centred, i + 1)
                act.activation(sq, res, ACT.Square).then_inc(squared, 1)

            def post_root(i):
                act.wait_ge(var_ready, i + 1)
                act.activation(logv, stat, ACT.Ln, bias=eps).then_inc(logged, 1)
                act.wait_ge(logged, i + 1)
                act.activation(r0, logv, ACT.Exp, scale=-0.5).then_inc(root, 1)
                act.wait_ge(root, i + 1)
                act.activation(r2, r0, ACT.Square).then_inc(root_ready, 1)

            act.preload_act_table_set("natural_log_exp_and_others")
            act.wait_ge(loaded, LOADS)
            act.activation(alog[:], alog[:], ACT.Exp).then_inc(ea_ready, 1)
            act.wait_ge(setup, 1)
            both, b, it, tc, t0 = passes(act)
            with both:
                act.wait_ge(r.scan_done, CREDIT + it * UNITS)
                act.wait_ge(r.sum_done, CREDIT + it * UNITS)

                def silu(g):
                    act.wait_ge(tap_done, it * 12 + 3 * (g + 1))
                    act.activation(u[:, g, :], u[:, g, :], ACT.Silu).then_inc(u_ready, 1)

                for g in range(MB):
                    if g == MB - 1:
                        silu(0)
                        silu(1)
                    x0 = PAD if bw else 0
                    act.wait_ge(xi_ready, it * MB + (g + 1))
                    if g > 1:
                        act.wait_ge(tap_done, it * 12 + 3 * (g - 1))
                    act.activation(x_slot[g % 2], flatb[:, x_bank[g % 2] * TT:x_bank[g % 2] * TT + PAD + TC],
                                   ACT.Copy).then_inc(xi_kept, 1)
                    act.wait_ge(xi_kept, it * MB + (g + 1))
                    act.activation(u[:, g, :], x_slot[g % 2][:, x0:x0 + TC], ACT.Identity, bias=convb[:, g:g + 1],
                                   scale=taps[:, g, 0:1]).then_inc(tap0, 1)
                    if g == 1:
                        post_square(it)
                silu(2)
                silu(3)
                act.preload_act_table_set("natural_log_exp_and_others")
                post_root(it)
                act.wait_ge(par_ready, it + 1)
                act.activation(dtin, flatb[64:64 + R, par_bank * TT:par_bank * TT + TC], ACT.Copy).then_inc(dtin_kept, 1)

                def softplus_parts(g):
                    s = g % 2
                    x = flatb[:, dt_bank[s] * TT:dt_bank[s] * TT + TC]
                    act.wait_ge(dt_ready, it * MB + (g + 1))
                    if g > 1:
                        act.wait_ge(soft_done, it * MB + (g - 1))
                    act.activation(lin[s], x, ACT.Identity, bias=bdt[:, g:g + 1])
                    act.activation(ex[s], x, ACT.Abs, bias=bdt[:, g:g + 1]).then_inc(abs_done, 1)
                    act.wait_ge(abs_done, it * MB + (g + 1))
                    act.activation(ex[s], ex[s], ACT.Exp, scale=-1.0).then_inc(exp_done, 1)
                    act.wait_ge(exp_done, it * MB + (g + 1))
                    act.activation(lg[s], ex[s], ACT.Ln, bias=one).then_inc(log_done, 1)

                def keep_b(n):
                    if n == 2:
                        act.wait_ge(y_out, it + 1)
                    if n == 14:
                        act.wait_ge(b_free, it + 1)
                    act.wait_ge(b_spread, it * NS + n + 1)
                    act.activation(brep[:, n, :], flatb[:, b_bank[n] * TT:b_bank[n] * TT + TC], ACT.Copy).then_inc(b_act, 1)

                for g in range(MB):
                    softplus_parts(g)
                    keep_b(2 * g)
                for n in range(2 * MB, NS, 2):
                    keep_b(n)
                act.wait_ge(soft_done, it * MB + MB)
                act.wait_ge(started, it + 1)

                def pair(g, n2):
                    for j in range(2):
                        un = scan_counts(it, g) + n2 * 2 + j
                        at = n2 * 2 + (g * NS + j)
                        act.wait_ge(r.scan_done, CREDIT + un - 1)
                        act.activation(decay_sb[:, j, :], dt[:, g, :], ACT.Exp,
                                       scale=neg_a[:, ds(at, 1)] if not isinstance(at, int)
                                       else neg_a[:, at:at + 1]).then_inc(r.decay_ready, 1)
                        act.wait_ge(r.scan_done, CREDIT + un)
                        if isinstance(at, int) and n2 * 2 + j == 0:
                            continue
                        act.activation(state[:, ds(at + g, 1)] if not isinstance(at, int)
                                       else state[:, at + g:at + g + 1],
                                       r.h[:, 1 - j, 0:1] if bw else r.h[:, 1 - j, TC - 1:TC], ACT.Copy)

                def gate(g):
                    act.wait_ge(z_ready, it * MB + (g + 1))
                    act.wait_ge(r.drive_ready, scan_counts(it, g) + NS)
                    act.activation(dtu[:, g, :], z_banks, ACT.Silu).then_inc(gate_ready, 1)
                    act.preload_act_table_set("natural_log_exp_and_others")

                for g in range(MB):
                    pair(g, 0)
                    if g:
                        gate(g - 1)
                    with act.Fori(1, NS // 2) as n2:
                        pair(g, n2)
                    act.wait_ge(r.scan_done, CREDIT + scan_counts(it, g) + NS)
                    last = g * (NS + 1) + NS
                    act.activation(state[:, last:last + 1], r.h[:, 1, 0:1] if bw else r.h[:, 1, TC - 1:TC],
                                   ACT.Copy).then_inc(saved, 1)
                gate(MB - 1)
            post_square(NP)
            post_root(NP)

        @block.vector
        def _(dve):
            def post_centre(i):
                dve.wait_ge(summed, i + 1)
                dve.wait_ge(mean_ready, i + 1)
                for c in range(C):
                    ins = dve.tensor_tensor(res[:, c, :], res[:, c, :], stat, ALU.subtract)
                ins.then_inc(centred, 1)

            def post_norm(i):
                dve.wait_ge(root_ready, i + 1)
                dve.scalar_tensor_tensor(out=ra, in0=stat, scalar=EPS,
                                         in1=r2, op0=ALU.add,
                                         op1=ALU.mult).then_inc(newton, 1)
                dve.wait_ge(newton, i * 2 + 1)
                dve.scalar_tensor_tensor(out=rstd, in0=ra, scalar=-3.0, in1=r0, op0=ALU.add,
                                         op1=ALU.mult).then_inc(newton, 1)
                dve.wait_ge(newton, i * 2 + 2)
                dve.wait_ge(centred, i + 1)
                for c in range(C):
                    ins = dve.scalar_tensor_tensor(out=res[:, c, :], in0=res[:, c, :], scalar=norm_s[:, 0, c:c + 1],
                                                   in1=rstd, op0=ALU.mult, op1=ALU.mult)
                ins.then_inc(scaled if bw else y_out, 1)
                if bw:
                    dve.wait_ge(scaled, i + 1)
                    dve.wait_ge(yf_loaded, i * 16 + 16)
                    for c in range(C):
                        ins = dve.scalar_tensor_tensor(out=res[:, c, :], in0=res[:, c, :], scalar=norm_s[:, 1, c:c + 1],
                                                       in1=yf[:, c, :], op0=ALU.add, op1=ALU.add)
                    ins.then_inc(y_out, 1)

            if not bw:
                dve.memset(wx[:], 0.0).then_inc(cleared, 1)
            dve.memset(one, 1.0)
            dve.memset(eps, EPS)
            dve.memset(carry[:, 0:1], 0.0)
            dve.memset(carry[:, 1:2], 1.0)
            dve.memset(res, 0.0).then_inc(summed, 1)
            dve.memset(state[:], 0.0)
            dve_credits(dve, r)
            dve.wait_ge(summed, 1)
            dve.wait_ge(loaded, LOADS)
            dve.wait_ge(ea_ready, 1)
            for g in range(MB):
                dve.tensor_scalar(diag_d[:, g, :], k.ident[:], dcol[:, g:g + 1], None, ALU.mult)
            dve.tensor_scalar(norm_s[:, 0, :], norm[:, 0, :], -0.5, None, ALU.mult)
            dve.tensor_scalar(norm_s[:, 1, :], norm[:, 1, :], 2.0, None, ALU.mult)
            dve.tensor_scalar(neg_a[:], alog[:], -1.0, None, ALU.mult).then_inc(setup, 1)
            dve.wait_ge(setup, 1)
            both, b, it, tc, t0 = passes(dve)
            with both:
                for g in range(MB):
                    for t in range(1, KC):
                        if t == 1:
                            dve.wait_ge(tap0, it * MB + (g + 1))
                        else:
                            dve.wait_ge(tap_done, it * 12 + (3 * g + t - 1))
                        x0 = PAD - t if bw else t
                        dve.scalar_tensor_tensor(out=u[:, g, :], in0=x_slot[g % 2][:, x0:x0 + TC],
                                                 scalar=taps[:, g, t:t + 1], in1=u[:, g, :], op0=ALU.mult,
                                                 op1=ALU.add).then_inc(tap_done, 1)
                    if g == 0:
                        post_centre(it)
                dve.wait_ge(par_ready, it + 1)
                split_rows(dve, split, it, flatb[0:32, par_bank * TT:par_bank * TT + TC], parts, mid, rest)

                def rounded_off(g):
                    s = g % 2
                    dve.wait_ge(exp_done, it * MB + (g + 1))
                    if g > 1:
                        dve.wait_ge(log_sum, it * MB + (g - 1))
                    dve.tensor_scalar(off[s], ex[s], 1.0, -1.0, ALU.add, ALU.add).then_inc(soft_step, 1)
                    dve.wait_ge(soft_step, it * 2 * MB + (2 * g + 1))
                    dve.scalar_tensor_tensor(out=off[s], in0=off[s], scalar=-1.0, in1=ex[s], op0=ALU.mult,
                                             op1=ALU.add).then_inc(soft_step, 1)

                def step_size(g):
                    dve.wait_ge(log_sum, it * MB + (g + 1))
                    dve.scalar_tensor_tensor(out=dt[:, g, :], in0=lin[g % 2], scalar=0.0, in1=lg[g % 2], op0=ALU.max,
                                             op1=ALU.add).then_inc(soft_done, 1)

                def keep_b(n):
                    if n == 15:
                        dve.wait_ge(b_free, it + 1)
                    dve.wait_ge(b_spread, it * NS + n + 1)
                    dve.tensor_copy(brep[:, n, :], flatb[:, b_bank[n] * TT:b_bank[n] * TT + TC]).then_inc(b_dve, 1)

                post_norm(it)
                dve.wait_ge(y_out, it + 1)
                rounded_off(0)
                for g in range(MB):
                    keep_b(2 * g + 1)
                    step_size(g)
                    if g + 1 < MB:
                        rounded_off(g + 1)
                for n in range(2 * MB + 1, NS, 2):
                    keep_b(n)
                dve.tensor_scalar(state[:], state[:], carry[:, ds(tc, 1)], None, ALU.mult).then_inc(started, 1)
                dve.wait_ge(started, it + 1)
                step = slice(None, None, -1) if bw else slice(None)

                def pair(g, n2):
                    for j in range(2):
                        un = scan_counts(it, g) + n2 * 2 + j
                        at = n2 * 2 + (1 + g * (NS + 1) + j)
                        dve.wait_ge(r.decay_ready, un + 1)
                        dve.wait_ge(r.drive_ready, un + 1)
                        dve.wait_ge(r.prod_ready, CREDIT + un - 1)
                        dve.tensor_tensor_scan(r.h[:, j, step], decay_sb[:, j, step], r.drive[:, j, step],
                                               state[:, at:at + 1] if isinstance(at, int) else state[:, ds(at, 1)],
                                               ALU.mult, ALU.add).then_inc(r.scan_done, 1)
                        dve.wait_ge(r.scan_done, CREDIT + un + 1)
                        dve.wait_ge(r.chat_ready, un + 1)
                        dve.wait_ge(r.sum_done, CREDIT + un - 1)
                        dve.tensor_tensor(r.prod[:, j, :], flat(r.chat), r.h[:, j, :],
                                          ALU.mult).then_inc(r.prod_ready, 1)

                def gate_y(g):
                    dve.wait_ge(r.sum_done, CREDIT + scan_counts(it, g) + NS)
                    dve.wait_ge(gate_ready, it * MB + (g + 1))
                    dve.tensor_tensor(u[:, g, :], flat(y_banks[g % 2]), dtu[:, g, :], ALU.mult).then_inc(gated, 1)

                for g in range(MB):
                    pair(g, 0)
                    if g:
                        gate_y(g - 1)
                    with dve.Fori(1, NS // 2) as n2:
                        pair(g, n2)
                gate_y(MB - 1)
                dve.wait_ge(out_ready, it + 1)
                dve.tensor_tensor(res, banks[:, 0:4, :].rearrange("p (c q) t -> p c (q t)", c=C),
                                  k.xn[:, :, b, ds(t0 + PAD, TC)], ALU.add).then_inc(summed, 1)
            post_centre(NP)
            post_norm(NP)

        @block.tensor
        def _(pe):
            def post_mean(i):
                pe.wait_ge(summed, i + 1)
                for q in range(2):
                    for c in range(C):
                        mm = pe.matmul(banks[:, q, :], k.mean[:], res[:, c, q * TT:(q + 1) * TT],
                                       start=c == 0, stop=c == C - 1)
                mm.then_inc(mean_ready, 1)

            def post_var(i):
                pe.wait_ge(squared, i + 1)
                for q in range(2):
                    for c in range(C):
                        mm = pe.matmul(banks[:, q, :], k.mean[:], sq[:, c, q * TT:(q + 1) * TT],
                                       start=c == 0, stop=c == C - 1)
                mm.then_inc(var_ready, 1)

            pe.sem_inc(r.sum_done, CREDIT)
            pe.wait_ge(loaded, LOADS)
            pe.wait_ge(setup, 1)
            both, b, it, tc, t0 = passes(pe)
            with both:
                for g in range(MB):
                    if g > 1:
                        pe.wait_ge(xi_kept, it * MB + (g - 1))
                    for q, n in ((0, TT), (1, TT), (2, PAD)):
                        for c in range(C):
                            mm = pe.matmul(banks[:, x_bank[g % 2] + q, 0:n], win[:, c, g * P:(g + 1) * P],
                                           k.xn[:, c, b, ds(t0 + ((PAD if bw else 0) + q * TT), n)],
                                           start=c == 0, stop=c == C - 1)
                    mm.then_inc(xi_ready, 1)
                    if g == 0:
                        post_mean(it)
                post_var(it)
                pe.wait_ge(xi_kept, it * MB + 3)
                for g in range(MB):
                    pe.wait_ge(u_ready, it * MB + (g + 1))
                    for q in range(2):
                        mm = pe.matmul(banks[0:64 + R, par_bank + q, :], wx[:, g, :], u[:, g, q * TT:(q + 1) * TT],
                                       start=g == 0, stop=g == MB - 1)
                mm.then_inc(par_ready, 1)

                def step_rows(g):
                    if g > 1:
                        pe.wait_ge(abs_done, it * MB + (g - 1))
                    for q in range(2):
                        mm = pe.matmul(banks[:, dt_bank[g % 2] + q, :], wdt[:, g * P:(g + 1) * P],
                                       dtin[:, q * TT:(q + 1) * TT], start=True, stop=True)
                    mm.then_inc(dt_ready, 1)

                def spread_b(n):
                    if n in (10, 11):
                        pe.wait_ge(abs_done, it * MB + MB)
                    elif n > 1:
                        pe.wait_ge(b_act if n % 2 == 0 else b_dve, it * 8 + (n // 2 if n < 10 else n // 2 - 1))
                    for q in range(2):
                        mm = pe.matmul(banks[:, b_bank[n] + q, :], k.sel[:, n, :],
                                       parts[:, q * TT:(q + 1) * TT], start=True, stop=True)
                    mm.then_inc(b_spread, 1)

                pe.wait_ge(dtin_kept, it + 1)
                pe.wait_ge(xi_kept, it * MB + MB)
                step_rows(0)
                pe.wait_ge(newton, it * 2 + 1)
                step_rows(1)
                pe.wait_ge(split, it * 5 + 5)
                for n in range(NS):
                    if n in (2, 4):
                        step_rows(1 + n // 2)
                    spread_b(n)
                pe.wait_ge(b_act, it * 8 + 8)
                pe.wait_ge(b_dve, it * 8 + 8)
                pe.wait_ge(abs_done, it * MB + MB)

                def spread_c(un, n):
                    for q in range(2):
                        mm = pe.matmul(r.chat[:, q, :], k.sel[:, NS + n, :] if isinstance(n, int)
                                       else k.sel[:, ds(n + NS, 1), :], parts[:, q * TT:(q + 1) * TT],
                                       start=True, stop=True)
                    mm.then_inc(r.chat_ready, 1)

                def add(g, j):
                    for q in range(2):
                        mm = pe.matmul(y_banks[g % 2][:, q, :], k.ident[:], r.prod[:, j, q * TT:(q + 1) * TT],
                                       start=False, stop=True, skip_group_check=True)
                    mm.then_inc(r.sum_done, 1)

                SLICE = 2 * TC // NS

                def z_slice(g, n2):
                    for c in range(C):
                        mm = pe.matmul(z_banks[:, n2 * SLICE:(n2 + 1) * SLICE] if isinstance(n2, int)
                                       else z_banks[:, ds(n2 * SLICE, SLICE)],
                                       win[:, c, D2 + g * P:D2 + (g + 1) * P],
                                       k.xn[:, c, b, ds(t0 + n2 * SLICE + PAD, SLICE)],
                                       start=c == 0, stop=c == C - 1)
                    return mm

                for g in range(MB):
                    base = scan_counts(it, g)
                    if g == 0:
                        spread_c(base, 0)
                    if g > 1:
                        pe.wait_ge(gated, it * MB + (g - 1))
                    for q in range(2):
                        pe.matmul(y_banks[g % 2][:, q, :], diag_d[:, g, :], u[:, g, q * TT:(q + 1) * TT], start=True,
                                  stop=True, skip_group_check=True)
                    with pe.Fori(0, NS // 2 - 1) as n2:
                        for j in range(2):
                            un = base + n2 * 2 + j
                            pe.wait_ge(r.prod_ready, CREDIT + un + 1)
                            spread_c(un + 1, n2 * 2 + (j + 1))
                            add(g, j)
                        if g:
                            pe.wait_ge(gate_ready, it * MB + g)
                        z_slice(g, n2)
                    pe.wait_ge(r.prod_ready, CREDIT + base + NS - 1)
                    spread_c(base + NS - 1, NS - 1)
                    add(g, 0)
                    z_slice(g, NS // 2 - 1).then_inc(z_ready, 1)
                    pe.wait_ge(r.prod_ready, CREDIT + base + NS)
                    if g + 1 < MB:
                        spread_c(base + NS, 0)
                    add(g, 1)

                def project(c, g):
                    for q in range(2):
                        mm = pe.matmul(banks[:, 2 * c + q, :], wout[:, g, c * P:(c + 1) * P],
                                       u[:, g, q * TT:(q + 1) * TT], start=g == 0, stop=g == MB - 1)
                    return mm

                for c in (1, 0):
                    if c == 1:
                        pe.wait_ge(gated, it * MB + 3)
                    else:
                        pe.wait_ge(gate_ready, it * MB + MB)
                    for g in range(MB - 1):
                        project(c, g)
                pe.wait_ge(gated, it * MB + MB)
                project(1, MB - 1)
                project(0, MB - 1).then_inc(out_ready, 1)
            post_mean(NP)
            post_var(NP)


H = 1024
HB = H // P
LANE = 7
ACROSS = 3


def butterflies(nc, k, up, down, spare, fac, loads):
    with ExitStack() as ctx:
        m = Mem(nc, ctx, "fly")
        swap, mat = m.sb("swap", [P, LANE, P]), m.sb("mat", [P, 4, P])
        banks = m.ps("banks", [P, 4, TT])
        swapped, half, mat_ready = m.sem("swapped"), m.sem("half"), m.sem("mat_ready")
        turned, kept = m.sem("turned"), m.sem("kept")
        scaled, crossed, ready = ([m.sem(f"{n}{w}") for w in range(2)] for n in ("scaled", "crossed", "ready"))
        width = up.shape[2]
        filled = m.sem("filled")
        loaded = [m.sem(f"loaded{n}") for n in range(3)]
        block = ctx.enter_context(nc.Block())
        way = [(up, 0, LANE, 0), (down, ACROSS, 0, 2)]

        def buffers(w, n):
            return (way[w][0], spare) if n % 2 == 0 else (spare, way[w][0])

        def across_act(act, w):
            for n in range(ACROSS):
                a, b = buffers(w, n)
                if n:
                    act.wait_ge(crossed[w], n * HB)
                for j in range(HB):
                    act.activation(b[:, j, :], a[:, j, :], ACT.Copy,
                                   scale=fac[:, way[w][3], way[w][2] + n, j:j + 1]).then_inc(scaled[w], 1)

        def across_dve(dve, w):
            for n in range(ACROSS):
                a, b = buffers(w, n)
                stride = 1 << (n if w == 0 else ACROSS - 1 - n)
                if n:
                    dve.wait_ge(crossed[w], n * HB)
                for j in range(HB):
                    dve.wait_ge(scaled[w], n * HB + j + 1)
                    dve.scalar_tensor_tensor(out=b[:, j, :], in0=a[:, j ^ stride, :],
                                             scalar=fac[:, way[w][3] + 1, way[w][2] + n, j:j + 1], in1=b[:, j, :],
                                             op0=ALU.mult, op1=ALU.add).then_inc(crossed[w], 1)
            dve.wait_ge(crossed[w], ACROSS * HB)
            dve.tensor_copy(way[w][0][:], spare[:]).then_inc(ready[w], 1)

        @block.sync
        def _(sp):
            sp.wait_ge(filled, 1)
            for group, signal in zip(loads, loaded):
                for dst, src in group:
                    sp.dma_start(dst, src).then_inc(signal, 16)
            for group, signal in zip(loads, loaded):
                sp.wait_ge(signal, 16 * len(group))

        @block.vector
        def _(dve):
            dve.memset(down[:, :, E:width], 0.0).then_inc(filled, 1)
            for n in range(LANE):
                s = 1 << n
                for side in range(2):
                    ins = dve.tensor_copy(swap[:, n, :].rearrange("p (a two s) -> p a two s", two=2, s=s)[:, :, side, :],
                                          k.ident[:].rearrange("p (a two s) -> p a two s", two=2, s=s)[:, :, 1 - side, :])
            ins.then_inc(swapped, 1)
            dve.wait_ge(filled, 1)
            dve.wait_ge(loaded[0], 16 * len(loads[0]))
            across_dve(dve, 1)
            dve.wait_ge(swapped, 1)
            with dve.Fori(0, LANE) as n:
                for j in range(HB):
                    i = n * (2 * HB) + 2 * j
                    for w in range(2):
                        dve.wait_ge(turned, i + w + 1)
                        dve.tensor_scalar(mat[:, (2 * j + w) % 4, :], k.ident[:], fac[:, way[w][3], ds(n + way[w][1], 1), j],
                                          None, ALU.mult).then_inc(half, 1)
                    for w in range(2):
                        one = mat[:, (2 * j + w) % 4, :]
                        sw = n if w == 0 else n * -1 + (LANE - 1)
                        dve.wait_ge(half, i + w + 1)
                        dve.scalar_tensor_tensor(out=one, in0=swap[:, ds(sw, 1), :].rearrange("p n q -> p (n q)"),
                                                 scalar=fac[:, way[w][3] + 1, ds(n + way[w][1], 1), j], in1=one,
                                                 op0=ALU.mult, op1=ALU.add).then_inc(mat_ready, 1)
            across_dve(dve, 0)

        @block.tensor
        def _(pe):
            pe.sem_inc(turned, 4)
            pe.wait_ge(ready[1], 1)
            pe.wait_ge(loaded[1], 16 * len(loads[1]))
            with pe.Fori(0, LANE) as n:
                for j in range(HB):
                    for w in range(2):
                        i = n * (2 * HB) + (2 * j + w)
                        slot = (2 * j + w) % 4
                        pe.wait_ge(mat_ready, i + 1)
                        pe.wait_ge(kept, i + 1)
                        pe.matmul(banks[:, slot, 0:width], mat[:, slot, :], way[w][0][:, j, :], start=True,
                                  stop=True).then_inc(turned, 1)

        @block.scalar
        def _(act):
            act.sem_inc(kept, 4)
            act.wait_ge(filled, 1)
            act.wait_ge(loaded[0], 16 * len(loads[0]))
            across_act(act, 1)
            with act.Fori(0, LANE) as n:
                for j in range(HB):
                    for w in range(2):
                        i = n * (2 * HB) + (2 * j + w)
                        act.wait_ge(turned, 4 + (i + 1))
                        act.activation(way[w][0][:, j, :], banks[:, (2 * j + w) % 4, 0:width], ACT.Copy).then_inc(kept, 1)
            act.wait_ge(kept, 4 + 2 * LANE * HB)
            act.wait_ge(ready[1], 1)
            across_act(act, 0)


def last(nc, k, out):
    FF = 512
    FB = FF // P
    a = k.a
    W = E + 1
    with ExitStack() as keep:
        mk = Mem(nc, keep, "fin")
        up, down = mk.sb("up", [P, HB, W]), mk.sb("down", [P, HB, W])
        up_b, w_up = mk.sb("up_b", [P, HB]), mk.sb("w_up", [P, C, H])
        w1, w2, b1 = mk.sb("w1", [P, C, FF]), mk.sb("w2", [P, FB, E]), mk.sb("b1", [P, FB])
        vec = mk.sb("vec", [P, 5, C])
        add_b = mk.sb("add_b", [P, C])
        with ExitStack() as ctx:
            m = Mem(nc, ctx, "fina")
            spare = m.sb("spare", [P, HB, W])
            fac = m.sb("fac", [P, 4, LANE + ACROSS, HB])
            butterflies(nc, k, up, down, spare, fac, [
                [(fac[:], a["factors"]), (down[:, :, 0:E], a["W_con"].rearrange("(j p) e -> p j e", p=P))],
                [(up[:], a["exp"].rearrange("(j p) e -> p j e", p=P))],
                [(up_b[:], a["up_bias"]), (w1[:], a["W1"].rearrange("(c p) m -> p c m", p=P)),
                 (w2[:], a["W2"].rearrange("(c p) m -> p c m", p=P)), (b1[:], a["b1"]), (vec[:], a["vec"])]])

        with ExitStack() as ctx:
            m = Mem(nc, ctx, "finb")
            y, x1 = m.sb("y", [P, 2, C, TT]), m.sb("x1", [P, 2, C, TT])
            f, g = m.sb("f", [P, FB, TT]), m.sb("g", [P, HB, TT])
            res, sq, o = m.sb("res", [P, C, TT]), m.sb("sq", [P, C, TT]), m.sb("o", [P, 2, C, TT])
            logv, r0, ra, rb, rstd = (m.sb(n, [P, TT]) for n in ("logv", "r0", "ra", "rb", "rstd"))
            eps = m.sb("eps", [P, 1])
            banks = m.ps("banks", [P, 8, TT])
            (turned, w_ready, f_ready, f_kept, ff_ready, summed, up_ready, g_ready, mean_ready, centred, squared, var_ready,
             logged, root_ready, newton, step, down_ready, o_ready) = (m.sem(n) for n in (
                 "turned w_ready f_ready f_kept ff_ready summed up_ready g_ready mean_ready centred squared var_ready "
                 "logged root_ready newton step down_ready o_ready").split())
            loaded = [m.sem(f"loaded{j}") for j in range(2)]
            stored = [m.sem(f"stored{j}") for j in range(2)]
            slot_free = m.sem("slot_free")
            NT = T // TT
            STEPS = 8
            block = ctx.enter_context(nc.Block())

            @block.sync
            def _(sp):
                yd, xd, od = (v.rearrange("(c p) t -> p c t", p=P) for v in (k.y, k.x1, out))
                with sp.Fori(0, NT // 2) as i2:
                    for j in range(2):
                        i = i2 * 2 + j
                        sp.wait_ge(o_ready, i + 1)
                        sp.dma_start(y[:, j], yd[:, :, ds(i * TT + L, TT)]).then_inc(loaded[j], 16)
                        sp.dma_start(x1[:, j], xd[:, :, ds(i * TT, TT)]).then_inc(loaded[j], 16)

            @block.gpsimd
            def _(pool):
                od = out.rearrange("(c p) t -> p c t", p=P)
                pool.sem_inc(slot_free, 1)
                with pool.Fori(0, NT // 2) as i2:
                    for j in range(2):
                        i = i2 * 2 + j
                        pool.wait_ge(o_ready, 2 + (i + 1))
                        pool.dma_start(od[:, :, ds(i * TT, TT)], o[:, j]).then_inc(stored[j], 16)
                        pool.wait_ge(stored[j], i2 * 16 + 16)
                        pool.sem_inc(slot_free, 1)

            @block.tensor
            def _(pe):
                for j in range(HB):
                    for c in range(C):
                        n = j * C + c
                        if n >= 4:
                            pe.wait_ge(w_ready, n - 3)
                        pe.transpose(banks[:, n % 4, 0:P], up[:, j, c * P:(c + 1) * P], k.ident[:]).then_inc(turned, 1)
                pe.wait_ge(w_ready, HB * C)
                with pe.Fori(0, NT // 2) as i2:
                    for j in range(2):
                        i = i2 * 2 + j
                        pe.wait_ge(loaded[j], i2 * 32 + 32)
                        pe.wait_ge(o_ready, 2 + i)
                        for h in range(FB):
                            for c in range(C):
                                mm = pe.matmul(banks[:, h, :], w1[:, c, h * P:(h + 1) * P], y[:, j, c, :],
                                               start=c == 0, stop=c == C - 1)
                            mm.then_inc(f_ready, 1)
                        for h in range(FB):
                            pe.wait_ge(f_kept, i * FB + (h + 1))
                        for c in range(C):
                            for h in range(FB):
                                mm = pe.matmul(banks[:, 6 + c, :], w2[:, h, c * P:(c + 1) * P], f[:, h, :],
                                               start=h == 0, stop=h == FB - 1)
                        mm.then_inc(ff_ready, 1)

                        def up_block(h):
                            if h >= 4:
                                pe.wait_ge(g_ready, i * HB + (h - 3))
                            for c in range(C):
                                mm = pe.matmul(banks[:, h % 4, :], w_up[:, c, h * P:(h + 1) * P],
                                               xnow(c, i2, j), start=c == 0, stop=c == C - 1)
                            mm.then_inc(up_ready, 1)

                        def xnow(c, i2, j):
                            return k.xn[:, c, :, :].rearrange("p b t -> p (b t)")[
                                :, ds(i2 * (2 * TT) + (i2 // 2) * (2 * PAD) + (j * TT + PAD), TT)]

                        for h in range(4):
                            up_block(h)
                        pe.wait_ge(summed, i + 1)
                        for c in range(C):
                            mm = pe.matmul(banks[:, 6, :], k.mean[:], res[:, c, :], start=c == 0, stop=c == C - 1)
                        mm.then_inc(mean_ready, 1)
                        for h in range(4, HB):
                            up_block(h)
                        pe.wait_ge(squared, i + 1)
                        for c in range(C):
                            mm = pe.matmul(banks[:, 7, :], k.mean[:], sq[:, c, :], start=c == 0, stop=c == C - 1)
                        mm.then_inc(var_ready, 1)
                        for h in range(HB):
                            pe.wait_ge(g_ready, i * HB + (h + 1))
                            for c in range(C):
                                mm = pe.matmul(banks[:, 4 + c, :], down[:, h, c * P:(c + 1) * P], g[:, h, :],
                                               start=h == 0, stop=h == HB - 1)
                        mm.then_inc(down_ready, 1)

            @block.scalar
            def _(act):
                act.wait_ge(w_ready, HB * C)
                with act.Fori(0, NT) as i:
                    for h in range(FB):
                        act.wait_ge(f_ready, i * FB + (h + 1))
                        act.activation(f[:, h, :], banks[:, h, :], ACT.Relu, bias=b1[:, h:h + 1]).then_inc(f_kept, 1)

                    def gelu(h):
                        act.wait_ge(up_ready, i * HB + (h + 1))
                        act.activation(g[:, h, :], banks[:, h % 4, :], ACT.Gelu, bias=up_b[:, h:h + 1]).then_inc(g_ready, 1)

                    for h in range(4):
                        gelu(h)
                    act.wait_ge(centred, i + 1)
                    act.activation(sq[:], res[:], ACT.Square).then_inc(squared, 1)
                    for h in range(4, HB):
                        gelu(h)
                    act.preload_act_table_set("natural_log_exp_and_others")
                    act.wait_ge(var_ready, i + 1)
                    act.activation(logv[:], banks[:, 7, :], ACT.Ln, bias=eps[:, 0:1]).then_inc(logged, 1)
                    act.wait_ge(logged, i + 1)
                    act.activation(r0[:], logv[:], ACT.Exp, scale=-0.5).then_inc(root_ready, 1)

            @block.vector
            def _(dve):
                dve.memset(eps[:], EPS)
                for j in range(HB):
                    for c in range(C):
                        n = j * C + c
                        dve.wait_ge(turned, n + 1)
                        dve.tensor_copy(w_up[:, c, j * P:(j + 1) * P], banks[:, n % 4, 0:P]).then_inc(w_ready, 1)
                dve.tensor_tensor(up_b[:], up_b[:], up[:, :, E:W].rearrange("p j o -> p (j o)"), ALU.add)
                dve.tensor_tensor(add_b[:], vec[:, 3, :], vec[:, 4, :], ALU.add).then_inc(o_ready, 2)
                dve.wait_ge(o_ready, 2)
                with dve.Fori(0, NT // 2) as i2:
                    for j in range(2):
                        i = i2 * 2 + j
                        dve.wait_ge(ff_ready, i + 1)
                        dve.wait_ge(loaded[j], i2 * 32 + 32)
                        for c in range(C):
                            ins = dve.scalar_tensor_tensor(out=res[:, c, :], in0=banks[:, 6 + c, :], scalar=vec[:, 0, c:c + 1],
                                                           in1=y[:, j, c, :], op0=ALU.add, op1=ALU.add)
                        ins.then_inc(summed, 1)
                        dve.wait_ge(summed, i + 1)
                        dve.wait_ge(mean_ready, i + 1)
                        for c in range(C):
                            ins = dve.tensor_tensor(res[:, c, :], res[:, c, :], banks[:, 6, :], ALU.subtract)
                        ins.then_inc(centred, 1)
                        dve.wait_ge(root_ready, i + 1)
                        dve.scalar_tensor_tensor(out=ra[:], in0=banks[:, 7, :], scalar=EPS, in1=r0[:], op0=ALU.add,
                                                 op1=ALU.mult).then_inc(newton, 1)
                        dve.wait_ge(newton, i * 3 + 1)
                        dve.scalar_tensor_tensor(out=rb[:], in0=ra[:], scalar=-0.5, in1=r0[:], op0=ALU.mult,
                                                 op1=ALU.mult).then_inc(newton, 1)
                        dve.wait_ge(newton, i * 3 + 2)
                        dve.scalar_tensor_tensor(out=rstd[:], in0=rb[:], scalar=1.5, in1=r0[:], op0=ALU.add,
                                                 op1=ALU.mult).then_inc(newton, 1)
                        dve.wait_ge(newton, i * 3 + 3)
                        for c in range(C):
                            dve.tensor_tensor(res[:, c, :], res[:, c, :], rstd[:], ALU.mult).then_inc(step, 1)
                        for c in range(C):
                            dve.wait_ge(step, i * STEPS + (c + 1))
                            dve.tensor_scalar(res[:, c, :], res[:, c, :], vec[:, 1, c:c + 1], vec[:, 2, c:c + 1],
                                              ALU.mult, ALU.add).then_inc(step, 1)
                        for c in range(C):
                            dve.wait_ge(step, i * STEPS + (3 + c))
                            dve.tensor_tensor(res[:, c, :], res[:, c, :], x1[:, j, c, :], ALU.add).then_inc(step, 1)
                        dve.wait_ge(down_ready, i + 1)
                        dve.wait_ge(slot_free, i + 1)
                        for c in range(C):
                            dve.wait_ge(step, i * STEPS + (5 + c))
                            ins = dve.scalar_tensor_tensor(out=o[:, j, c, :], in0=banks[:, 4 + c, :], scalar=add_b[:, c:c + 1],
                                                           in1=res[:, c, :], op0=ALU.add, op1=ALU.add)
                            ins.then_inc(step, 1)
                        dve.wait_ge(step, i * STEPS + 8)
                        dve.memset(eps[:], EPS).then_inc(o_ready, 1)


class Kept:
    pass


def program(nc, a, out):
    Mem.used = []
    with ExitStack() as ctx:
        m = Mem(nc, ctx, "kept")
        k = Kept()
        k.ident = m.sb("ident", [P, P])
        k.mean = m.sb("mean", [P, P])
        k.sel = m.sb("sel", [96, 32, P], BF16)
        k.xn = m.sb("xn", [P, C, B, LP])
        k.a = a
        k.x1 = nc.dram_tensor("x1_scratch", (E, T), F32, kind="Internal").ap()
        k.yf, k.y = (nc.dram_tensor(n, (E, L + T), F32, kind="Internal").ap() for n in ("fw_scratch", "both_scratch"))
        constants(nc, k)
        with ExitStack() as first:
            acc = Mem(nc, first, "first").sb("acc", [P, C, T])
            layernorm(nc, k, acc, a["xT"])
            mixer0(nc, k, acc)
            experts0(nc, k, acc)
        clear_semaphores(nc)
        with ExitStack() as second:
            weights = Mixer1Weights(Mem(nc, second, "mix1"))
            mixer1(nc, k, weights, "fw", None, k.yf)
            mixer1(nc, k, weights, "bw", k.yf, k.y)
        last(nc, k, out)


def _factors(w, upward):
    import numpy as np

    i = np.arange(H)
    own, cross = [], []
    for stage in range(LANE + ACROSS):
        s = 1 << stage
        bit, pair = i // s % 2, i // (2 * s) * s + i % s
        own.append(w[stage, pair, bit, bit])
        leaves = w[stage, pair, 1 - bit, bit]
        arrives = w[stage, pair, bit, 1 - bit]
        cross.append(leaves if (stage < LANE) == upward else arrives)
    order = list(range(LANE + ACROSS)) if upward else list(range(LANE + ACROSS))[::-1]
    return [np.stack([v[n].reshape(HB, P).T for n in order], axis=1) for v in (own, cross)]


def _laid_out(i):
    import numpy as np

    def arr(name):
        return np.asarray(i[name])

    def cols(name):
        return arr(name).reshape(-1, P).T

    a = {"xT": arr("L0_attn_x").transpose(2, 0, 1).reshape(E, T),
         "W_z": arr("L0_attn_W_z").T, "W_out": arr("L0_attn_W_out").T, "W_par": arr("L0_attn_W_params").T,
         "W_dt": arr("L0_attn_W_dt").T, "conv_w": arr("L0_attn_conv_w")[:, 0], "b_dt": cols("L0_attn_b_dt"),
         "A_log": arr("L0_attn_A_log"), "D": cols("L0_attn_D"),
         "controller": arr("L0_ffn_controller").reshape(E, -1), "f1": arr("L0_ffn_f1").reshape(E, 64, 64),
         "f2": arr("L0_ffn_f2").reshape(64, 64, E), "bias": arr("L0_ffn_bias").reshape(64, 64).T,
         "tie": np.broadcast_to(np.linspace(0.0, 1e-6, 16, dtype=np.float32), (P, 32, 16))}
    for way in ("fw", "bw"):
        for w in ("Win", "Wout", "Wx", "Wdt", "convw", "Alog"):
            a[f"{way}_{w}"] = arr(f"L1_attn_{way}_{w}")
        for w in ("convb", "bdt", "D"):
            a[f"{way}_{w}"] = cols(f"L1_attn_{way}_{w}")
    for w in ("fwn", "fin"):
        a[w] = np.stack([cols(f"L1_attn_{w}_w"), cols(f"L1_attn_{w}_b")], axis=1)
    a["W1"], a["W2"] = arr("L1_attn_ff_W1"), arr("L1_attn_ff_W2")
    a["b1"] = cols("L1_attn_ff_b1")
    a["vec"] = np.stack([cols(n) for n in ("L1_attn_ff_b2", "L1_attn_fin_w", "L1_attn_fin_b", "L1_ffn_b_con",
                                           "L1_ffn_down_bias")], axis=1)
    a["exp"] = np.concatenate([arr("L1_ffn_W_exp").T, arr("L1_ffn_b_exp")[:, None]], axis=1)
    a["W_con"], a["up_bias"] = arr("L1_ffn_W_con"), cols("L1_ffn_up_bias")
    a["factors"] = np.stack(_factors(arr("L1_ffn_up_weights"), True) + _factors(arr("L1_ffn_down_weights"), False),
                            axis=1)
    return {n: np.ascontiguousarray(v) for n, v in a.items()}


def kernel(**inputs):
    import concourse.bacc as _bacc
    from concourse.bass_utils import run_bass_kernel_spmd as _run

    nc = _bacc.Bacc("TRN2", target_bir_lowering=False, num_devices=1)
    arrays = _laid_out(inputs)
    args = {n: nc.dram_tensor(n, v.shape, mybir.dt.from_np(v.dtype), kind="ExternalInput").ap()
            for n, v in arrays.items()}
    out = nc.dram_tensor("out", (E, T), F32, kind="ExternalOutput").ap()
    program(nc, args, out)
    r = _run(nc, [arrays], core_ids=[0])
    return r.results[0]["out"].reshape(E, B, L).transpose(1, 2, 0)
```
